# Optimizing a Trainium2 kernel written in Bass

```python
import numpy as np
import jax
import jax.numpy as jnp

def _softmax(x, axis=-1):
    return jax.nn.softmax(x, axis=axis)

def _gelu(x):
    return jax.nn.gelu(x, approximate=True)

def _silu(x):
    return jax.nn.silu(x)

def _sigmoid(x):
    return jax.nn.sigmoid(x)

def _layernorm(x, axis=-1, eps=1e-05):
    m = jnp.mean(x, axis=axis, keepdims=True)
    v = jnp.var(x, axis=axis, keepdims=True)
    return (x - m) / jnp.sqrt(v + eps)

def _scatter_add(tgt, idx, src, axis=0):
    return tgt.at[idx].add(src)

def _segment_sum(src, seg, n):
    return jax.ops.segment_sum(src, seg, n)
kernel_name = 'mk_vit_tower_d2_tok_img512_r4_a4a0cb'

def setup_inputs(seed: int=0):
    np.random.seed(seed)
    _w = jnp.asarray

    def _rec_inputs():
        import jax
        import jax.numpy as jnp
        _rk = jax.random.key(seed)
        x = 7.57192e-06 + 1.00007 * jax.random.normal(jax.random.fold_in(_rk, 1), (64, 3, 224, 224), jnp.float32)
        return x
    x = _rec_inputs()

    def _L0_tok_setup():
        import jax, jax.numpy as jnp
        import numpy as np
        D_MODEL = 128
        N_HEADS = 8
        D_HEAD = D_MODEL // N_HEADS
        D_FF = 344
        PATCH = 16
        IMG = 224
        N_PATCHES = (IMG // PATCH) ** 2
        T = N_PATCHES + 1
        B = 64
        EPS = 1e-06

        def rmsnorm(x, w):
            xf = x.astype(jnp.float32)
            norm = jax.lax.rsqrt(jnp.mean(xf * xf, axis=-1, keepdims=True) + EPS)
            return (xf * norm).astype(x.dtype) * w

        def _patch_embed(images, conv_w, conv_b, cls_token, pos_emb):
            y = jax.lax.conv_general_dilated(images, conv_w, window_strides=(PATCH, PATCH), padding='VALID', dimension_numbers=('NCHW', 'OIHW', 'NCHW'))
            y = y + conv_b[None, :, None, None]
            patches = y.reshape(y.shape[0], D_MODEL, -1).transpose(0, 2, 1)
            cls = jnp.broadcast_to(cls_token, (images.shape[0], 1, D_MODEL))
            return jnp.concatenate([cls, patches], axis=1) + pos_emb

        def _block(x, ln1w, wqkv, wo, ln2w, wg, wu, wd):
            Bx, Tx, C = x.shape
            h = rmsnorm(x, ln1w)
            qkv = (h @ wqkv.T).reshape(Bx, Tx, 3, N_HEADS, D_HEAD)
            q, k, v = jnp.moveaxis(qkv, 2, 0)
            scale = 1.0 / float(np.sqrt(D_HEAD))
            attn = jnp.einsum('bthd,bshd->bhts', q, k) * scale
            attn = jax.nn.softmax(attn, axis=-1)
            out = jnp.einsum('bhts,bshd->bthd', attn, v).reshape(Bx, Tx, C)
            x = x + out @ wo.T
            h2 = rmsnorm(x, ln2w)
            ff = jax.nn.silu(h2 @ wg.T) * (h2 @ wu.T) @ wd.T
            return x + ff
        key = jax.random.key(seed)
        ks = jax.random.split(key, 16)
        std = 0.02
        d = {'images': jax.random.normal(ks[0], (B, 3, IMG, IMG), dtype=jnp.float32), 'conv_w': jax.random.normal(ks[1], (D_MODEL, 3, PATCH, PATCH), dtype=jnp.float32) * std, 'conv_b': jnp.zeros((D_MODEL,), dtype=jnp.float32), 'cls_token': jax.random.normal(ks[2], (1, 1, D_MODEL), dtype=jnp.float32) * std, 'pos_emb': jax.random.normal(ks[3], (1, T, D_MODEL), dtype=jnp.float32) * std, 'ln_f': jnp.ones((D_MODEL,), dtype=jnp.float32)}
        ki = 4
        for i in range(2):
            d[f'ln1_{i}'] = jnp.ones((D_MODEL,), dtype=jnp.float32)
            d[f'qkv_{i}'] = jax.random.normal(ks[ki + 0], (3 * D_MODEL, D_MODEL), dtype=jnp.float32) * std
            d[f'wo_{i}'] = jax.random.normal(ks[ki + 1], (D_MODEL, D_MODEL), dtype=jnp.float32) * std
            d[f'ln2_{i}'] = jnp.ones((D_MODEL,), dtype=jnp.float32)
            d[f'gate_{i}'] = jax.random.normal(ks[ki + 2], (D_FF, D_MODEL), dtype=jnp.float32) * std
            d[f'up_{i}'] = jax.random.normal(ks[ki + 3], (D_FF, D_MODEL), dtype=jnp.float32) * std
            d[f'down_{i}'] = jax.random.normal(ks[ki + 4], (D_MODEL, D_FF), dtype=jnp.float32) * std
            ki += 5
        return d
    _L0_tok_all = _L0_tok_setup()
    _L0_tok_in = {k: v for k, v in _L0_tok_all.items() if k in ('conv_w', 'conv_b', 'cls_token', 'pos_emb', 'ln_f', 'ln1_0', 'qkv_0', 'wo_0', 'ln2_0', 'gate_0', 'up_0', 'down_0', 'ln1_1', 'qkv_1', 'wo_1', 'ln2_1', 'gate_1', 'up_1', 'down_1')}
    del _L0_tok_all

    def _L0_attn_setup():
        import jax, jax.numpy as jnp
        import numpy as np
        GAMMA = 0.9
        NUM_HEADS = 8
        SCALE_BASE = 512.0
        GN_EPS = 1e-05

        def xpos(x):
            B, S, D = x.shape
            half = D // 2
            scale_vec = (jnp.arange(0, D, 2, dtype=jnp.float32) + 0.4 * D) / (1.4 * D)
            power = jnp.arange(S, dtype=jnp.float32) / SCALE_BASE
            scale = scale_vec[None, :] ** power[:, None]
            inv_freq = 1.0 / 10000.0 ** (jnp.arange(half, dtype=jnp.float32) / half)
            sinusoid = jnp.arange(S, dtype=jnp.float32)[:, None] * inv_freq[None, :]
            sin_s = jnp.repeat(jnp.sin(sinusoid) * scale, 2, axis=-1)
            cos_s = jnp.repeat(jnp.cos(sinusoid) * scale, 2, axis=-1)
            x1, x2 = (x[..., ::2], x[..., 1::2])
            rot = jnp.stack([-x2, x1], axis=-1).reshape(x.shape)
            return x * cos_s[None] + rot * sin_s[None]

        def group_norm(x, weight, bias, num_groups):
            N, C = x.shape
            xg = x.reshape(N, num_groups, C // num_groups)
            mu = jnp.mean(xg, axis=-1, keepdims=True)
            var = jnp.var(xg, axis=-1, keepdims=True)
            xn = ((xg - mu) * jax.lax.rsqrt(var + GN_EPS)).reshape(N, C)
            return xn * weight[None, :] + bias[None, :]

        def decay_matrix(S):
            n = jnp.arange(S, dtype=jnp.float32)[:, None]
            m = jnp.arange(S, dtype=jnp.float32)[None, :]
            return jnp.where(n >= m, GAMMA ** (n - m), 0.0)
        key = jax.random.key(seed)
        ks = jax.random.split(key, 6)
        B, S, Din, Dm = (2, 512, 128, 128)
        s = 1.0 / np.sqrt(Din)
        return {'X': jax.random.normal(ks[0], (B, S, Din), dtype=jnp.float32), 'Wq': jax.random.uniform(ks[1], (Din, Dm), jnp.float32, -s, s), 'Wk': jax.random.uniform(ks[2], (Din, Dm), jnp.float32, -s, s), 'Wv': jax.random.uniform(ks[3], (Din, Dm), jnp.float32, -s, s), 'gn_weight': jnp.ones((Dm,), jnp.float32), 'gn_bias': jnp.zeros((Dm,), jnp.float32)}
    _L0_attn_all = _L0_attn_setup()
    _L0_attn_in = {k: v for k, v in _L0_attn_all.items() if k in ('Wq', 'Wk', 'Wv', 'gn_weight', 'gn_bias')}
    del _L0_attn_all

    def _L0_ffn_setup():
        import jax, jax.numpy as jnp
        import numpy as np
        EPS = 1e-05
        TOP_K = 2

        def layer_norm(x, g, b):
            m = x.mean(-1, keepdims=True)
            v = ((x - m) ** 2).mean(-1, keepdims=True)
            return (x - m) / jnp.sqrt(v + EPS) * g + b
        key = jax.random.key(seed)
        ks = jax.random.split(key, 8)
        B, S, D, E, H = (8, 128, 128, 8, 512)
        x = jax.random.normal(ks[0], (B, S, D), dtype=jnp.float32)
        Wg = jax.random.normal(ks[1], (D, E), dtype=jnp.float32) * 0.02
        W1 = jax.random.normal(ks[2], (E, D, H), dtype=jnp.float32) * 0.02
        b1 = jnp.zeros((E, H), dtype=jnp.float32)
        W2 = jax.random.normal(ks[3], (E, H, D), dtype=jnp.float32) * 0.02
        b2 = jnp.zeros((E, D), dtype=jnp.float32)
        ln_g = jnp.ones((D,), dtype=jnp.float32)
        ln_b = jnp.zeros((D,), dtype=jnp.float32)
        out_g = jnp.ones((D,), dtype=jnp.float32)
        out_b = jnp.zeros((D,), dtype=jnp.float32)
        return {'x': x, 'Wg': Wg, 'W1': W1, 'b1': b1, 'W2': W2, 'b2': b2, 'ln_g': ln_g, 'ln_b': ln_b, 'out_g': out_g, 'out_b': out_b}
    _L0_ffn_all = _L0_ffn_setup()
    _L0_ffn_in = {k: v for k, v in _L0_ffn_all.items() if k in ('Wg', 'W1', 'b1', 'W2', 'b2', 'ln_g', 'ln_b', 'out_g', 'out_b')}
    del _L0_ffn_all

    def _L1_attn_setup():
        import jax, jax.numpy as jnp
        import numpy as np
        B, N, D_IN = (8, 512, 128)
        H = 256
        D_EMB = 128
        D_ATTN = 64
        key = jax.random.key(seed)
        ks = jax.random.split(key, 9)
        s = lambda fi, fo: (2.0 / (fi + fo)) ** 0.5
        return {'x': jax.random.normal(ks[0], (B, N, D_IN), dtype=jnp.float32), 'We1': jax.random.normal(ks[1], (D_IN, H), dtype=jnp.float32) * s(D_IN, H), 'be1': jnp.zeros((H,), dtype=jnp.float32), 'We2': jax.random.normal(ks[2], (H, D_EMB), dtype=jnp.float32) * s(H, D_EMB), 'be2': jnp.zeros((D_EMB,), dtype=jnp.float32), 'Wk1': jax.random.normal(ks[3], (D_IN, H), dtype=jnp.float32) * s(D_IN, H), 'bk1': jnp.zeros((H,), dtype=jnp.float32), 'Wk2': jax.random.normal(ks[4], (H, 2 * D_ATTN), dtype=jnp.float32) * s(H, 2 * D_ATTN), 'bk2': jnp.zeros((2 * D_ATTN,), dtype=jnp.float32)}
    _L1_attn_all = _L1_attn_setup()
    _L1_attn_in = {k: v for k, v in _L1_attn_all.items() if k in ('We1', 'be1', 'We2', 'be2', 'Wk1', 'bk1', 'Wk2', 'bk2')}
    del _L1_attn_all

    def _L1_ffn_setup():
        import jax, jax.numpy as jnp
        import numpy as np
        TOP_K = 2

        def quick_gelu(x):
            return x * jax.nn.sigmoid(1.702 * x)
        key = jax.random.key(seed)
        ks = jax.random.split(key, 6)
        B, S, H, I, E = (8, 1024, 128, 256, 8)
        s_h = 1.0 / np.sqrt(H).astype(np.float32)
        s_i = 1.0 / np.sqrt(I).astype(np.float32)
        return {'hidden_states': jax.random.normal(ks[0], (B, S, H), jnp.float32), 'router_w': jax.random.normal(ks[1], (H, E), jnp.float32) * s_h, 'router_b': jnp.zeros((E,), jnp.float32), 'gate_up_proj': jax.random.normal(ks[2], (E, H, 2 * I), jnp.float32) * s_h, 'gate_up_proj_bias': jnp.zeros((E, 2 * I), jnp.float32), 'down_proj': jax.random.normal(ks[3], (E, I, H), jnp.float32) * s_i, 'down_proj_bias': jnp.zeros((E, H), jnp.float32)}
    _L1_ffn_all = _L1_ffn_setup()
    _L1_ffn_in = {k: v for k, v in _L1_ffn_all.items() if k in ('router_w', 'router_b', 'gate_up_proj', 'gate_up_proj_bias', 'down_proj', 'down_proj_bias')}
    del _L1_ffn_all
    return {'x': x, 'L0_tok_conv_w': _L0_tok_in['conv_w'], 'L0_tok_conv_b': _L0_tok_in['conv_b'], 'L0_tok_cls_token': _L0_tok_in['cls_token'], 'L0_tok_pos_emb': _L0_tok_in['pos_emb'], 'L0_tok_ln_f': _L0_tok_in['ln_f'], 'L0_tok_ln1_0': _L0_tok_in['ln1_0'], 'L0_tok_qkv_0': _L0_tok_in['qkv_0'], 'L0_tok_wo_0': _L0_tok_in['wo_0'], 'L0_tok_ln2_0': _L0_tok_in['ln2_0'], 'L0_tok_gate_0': _L0_tok_in['gate_0'], 'L0_tok_up_0': _L0_tok_in['up_0'], 'L0_tok_down_0': _L0_tok_in['down_0'], 'L0_tok_ln1_1': _L0_tok_in['ln1_1'], 'L0_tok_qkv_1': _L0_tok_in['qkv_1'], 'L0_tok_wo_1': _L0_tok_in['wo_1'], 'L0_tok_ln2_1': _L0_tok_in['ln2_1'], 'L0_tok_gate_1': _L0_tok_in['gate_1'], 'L0_tok_up_1': _L0_tok_in['up_1'], 'L0_tok_down_1': _L0_tok_in['down_1'], 'L0_attn_Wq': _L0_attn_in['Wq'], 'L0_attn_Wk': _L0_attn_in['Wk'], 'L0_attn_Wv': _L0_attn_in['Wv'], 'L0_attn_gn_weight': _L0_attn_in['gn_weight'], 'L0_attn_gn_bias': _L0_attn_in['gn_bias'], 'L0_ffn_Wg': _L0_ffn_in['Wg'], 'L0_ffn_W1': _L0_ffn_in['W1'], 'L0_ffn_b1': _L0_ffn_in['b1'], 'L0_ffn_W2': _L0_ffn_in['W2'], 'L0_ffn_b2': _L0_ffn_in['b2'], 'L0_ffn_ln_g': _L0_ffn_in['ln_g'], 'L0_ffn_ln_b': _L0_ffn_in['ln_b'], 'L0_ffn_out_g': _L0_ffn_in['out_g'], 'L0_ffn_out_b': _L0_ffn_in['out_b'], 'L1_attn_We1': _L1_attn_in['We1'], 'L1_attn_be1': _L1_attn_in['be1'], 'L1_attn_We2': _L1_attn_in['We2'], 'L1_attn_be2': _L1_attn_in['be2'], 'L1_attn_Wk1': _L1_attn_in['Wk1'], 'L1_attn_bk1': _L1_attn_in['bk1'], 'L1_attn_Wk2': _L1_attn_in['Wk2'], 'L1_attn_bk2': _L1_attn_in['bk2'], 'L1_ffn_router_w': _L1_ffn_in['router_w'], 'L1_ffn_router_b': _L1_ffn_in['router_b'], 'L1_ffn_gate_up_proj': _L1_ffn_in['gate_up_proj'], 'L1_ffn_gate_up_proj_bias': _L1_ffn_in['gate_up_proj_bias'], 'L1_ffn_down_proj': _L1_ffn_in['down_proj'], 'L1_ffn_down_proj_bias': _L1_ffn_in['down_proj_bias']}

def reference(x, L0_tok_conv_w, L0_tok_conv_b, L0_tok_cls_token, L0_tok_pos_emb, L0_tok_ln_f, L0_tok_ln1_0, L0_tok_qkv_0, L0_tok_wo_0, L0_tok_ln2_0, L0_tok_gate_0, L0_tok_up_0, L0_tok_down_0, L0_tok_ln1_1, L0_tok_qkv_1, L0_tok_wo_1, L0_tok_ln2_1, L0_tok_gate_1, L0_tok_up_1, L0_tok_down_1, L0_attn_Wq, L0_attn_Wk, L0_attn_Wv, L0_attn_gn_weight, L0_attn_gn_bias, L0_ffn_Wg, L0_ffn_W1, L0_ffn_b1, L0_ffn_W2, L0_ffn_b2, L0_ffn_ln_g, L0_ffn_ln_b, L0_ffn_out_g, L0_ffn_out_b, L1_attn_We1, L1_attn_be1, L1_attn_We2, L1_attn_be2, L1_attn_Wk1, L1_attn_bk1, L1_attn_Wk2, L1_attn_bk2, L1_ffn_router_w, L1_ffn_router_b, L1_ffn_gate_up_proj, L1_ffn_gate_up_proj_bias, L1_ffn_down_proj, L1_ffn_down_proj_bias):
    import jax
    import jax.numpy as jnp

    def _L0_tok_ref(images, conv_w, conv_b, cls_token, pos_emb, ln_f, ln1_0, qkv_0, wo_0, ln2_0, gate_0, up_0, down_0, ln1_1, qkv_1, wo_1, ln2_1, gate_1, up_1, down_1):
        import jax, jax.numpy as jnp
        import numpy as np
        D_MODEL = 128
        N_HEADS = 8
        D_HEAD = D_MODEL // N_HEADS
        D_FF = 344
        PATCH = 16
        IMG = 224
        N_PATCHES = (IMG // PATCH) ** 2
        T = N_PATCHES + 1
        B = 64
        EPS = 1e-06

        def rmsnorm(x, w):
            xf = x.astype(jnp.float32)
            norm = jax.lax.rsqrt(jnp.mean(xf * xf, axis=-1, keepdims=True) + EPS)
            return (xf * norm).astype(x.dtype) * w

        def _patch_embed(images, conv_w, conv_b, cls_token, pos_emb):
            y = jax.lax.conv_general_dilated(images, conv_w, window_strides=(PATCH, PATCH), padding='VALID', dimension_numbers=('NCHW', 'OIHW', 'NCHW'))
            y = y + conv_b[None, :, None, None]
            patches = y.reshape(y.shape[0], D_MODEL, -1).transpose(0, 2, 1)
            cls = jnp.broadcast_to(cls_token, (images.shape[0], 1, D_MODEL))
            return jnp.concatenate([cls, patches], axis=1) + pos_emb

        def _block(x, ln1w, wqkv, wo, ln2w, wg, wu, wd):
            Bx, Tx, C = x.shape
            h = rmsnorm(x, ln1w)
            qkv = (h @ wqkv.T).reshape(Bx, Tx, 3, N_HEADS, D_HEAD)
            q, k, v = jnp.moveaxis(qkv, 2, 0)
            scale = 1.0 / float(np.sqrt(D_HEAD))
            attn = jnp.einsum('bthd,bshd->bhts', q, k) * scale
            attn = jax.nn.softmax(attn, axis=-1)
            out = jnp.einsum('bhts,bshd->bthd', attn, v).reshape(Bx, Tx, C)
            x = x + out @ wo.T
            h2 = rmsnorm(x, ln2w)
            ff = jax.nn.silu(h2 @ wg.T) * (h2 @ wu.T) @ wd.T
            return x + ff
        x = _patch_embed(images, conv_w, conv_b, cls_token, pos_emb)
        x = _block(x, ln1_0, qkv_0, wo_0, ln2_0, gate_0, up_0, down_0)
        x = _block(x, ln1_1, qkv_1, wo_1, ln2_1, gate_1, up_1, down_1)
        return rmsnorm(x, ln_f)

    def _L0_attn_ref(X, Wq, Wk, Wv, gn_weight, gn_bias):
        import jax, jax.numpy as jnp
        import numpy as np
        GAMMA = 0.9
        NUM_HEADS = 8
        SCALE_BASE = 512.0
        GN_EPS = 1e-05

        def xpos(x):
            B, S, D = x.shape
            half = D // 2
            scale_vec = (jnp.arange(0, D, 2, dtype=jnp.float32) + 0.4 * D) / (1.4 * D)
            power = jnp.arange(S, dtype=jnp.float32) / SCALE_BASE
            scale = scale_vec[None, :] ** power[:, None]
            inv_freq = 1.0 / 10000.0 ** (jnp.arange(half, dtype=jnp.float32) / half)
            sinusoid = jnp.arange(S, dtype=jnp.float32)[:, None] * inv_freq[None, :]
            sin_s = jnp.repeat(jnp.sin(sinusoid) * scale, 2, axis=-1)
            cos_s = jnp.repeat(jnp.cos(sinusoid) * scale, 2, axis=-1)
            x1, x2 = (x[..., ::2], x[..., 1::2])
            rot = jnp.stack([-x2, x1], axis=-1).reshape(x.shape)
            return x * cos_s[None] + rot * sin_s[None]

        def group_norm(x, weight, bias, num_groups):
            N, C = x.shape
            xg = x.reshape(N, num_groups, C // num_groups)
            mu = jnp.mean(xg, axis=-1, keepdims=True)
            var = jnp.var(xg, axis=-1, keepdims=True)
            xn = ((xg - mu) * jax.lax.rsqrt(var + GN_EPS)).reshape(N, C)
            return xn * weight[None, :] + bias[None, :]

        def decay_matrix(S):
            n = jnp.arange(S, dtype=jnp.float32)[:, None]
            m = jnp.arange(S, dtype=jnp.float32)[None, :]
            return jnp.where(n >= m, GAMMA ** (n - m), 0.0)
        B, S, Din = X.shape
        Dm = Wq.shape[1]
        H = NUM_HEADS
        hd = Dm // H
        q = xpos(X @ Wq)
        k = xpos(X @ Wk)
        k = group_norm(k.reshape(-1, Dm), gn_weight, gn_bias, H).reshape(B, S, Dm)
        v = X @ Wv
        q = q.reshape(B, S, H, hd).transpose(0, 2, 1, 3)
        k = k.reshape(B, S, H, hd).transpose(0, 2, 1, 3)
        v = v.reshape(B, S, H, hd).transpose(0, 2, 1, 3)
        q = q * jax.nn.sigmoid(q)
        scores = jnp.einsum('bhsd,bhtd->bhst', q, k)
        msr = scores * decay_matrix(S)[None, None]
        out = jnp.einsum('bhst,bhtd->bhsd', msr, v)
        out = out.transpose(0, 2, 1, 3).reshape(B, S, Dm)
        out = out + X
        return jax.nn.relu(out)

    def _L0_ffn_ref(x, Wg, W1, b1, W2, b2, ln_g, ln_b, out_g, out_b):
        import jax, jax.numpy as jnp
        import numpy as np
        EPS = 1e-05
        TOP_K = 2

        def layer_norm(x, g, b):
            m = x.mean(-1, keepdims=True)
            v = ((x - m) ** 2).mean(-1, keepdims=True)
            return (x - m) / jnp.sqrt(v + EPS) * g + b
        xn = layer_norm(x, ln_g, ln_b)
        logits = jnp.einsum('bsd,de->bse', xn, Wg)
        probs = jax.nn.softmax(logits, axis=-1)
        top_p, top_i = jax.lax.top_k(probs, TOP_K)
        conf = top_p / top_p.sum(-1, keepdims=True)
        h = jax.nn.gelu(jnp.einsum('bsd,edh->bseh', xn, W1) + b1)
        o = jnp.einsum('bseh,ehd->bsed', h, W2) + b2
        sel = jnp.take_along_axis(o, top_i[..., None], axis=2)
        combined = jnp.einsum('bskd,bsk->bsd', sel, conf)
        return layer_norm(x + combined, out_g, out_b)

    def _L1_attn_ref(x, We1, be1, We2, be2, Wk1, bk1, Wk2, bk2):
        import jax, jax.numpy as jnp
        import numpy as np
        B, N, D_IN = (8, 512, 128)
        H = 256
        D_EMB = 128
        D_ATTN = 64
        embs = jax.nn.relu(x @ We1 + be1) @ We2 + be2
        kq = jax.nn.relu(x @ Wk1 + bk1) @ Wk2 + bk2
        K, Q = (kq[..., :D_ATTN], kq[..., D_ATTN:])
        scores = jnp.einsum('bqd,bkd->bqk', Q, K)
        A = jax.nn.softmax(scores, axis=-1)
        return jnp.einsum('bqk,bkd->bqd', A, embs)

    def _L1_ffn_ref(hidden_states, router_w, router_b, gate_up_proj, gate_up_proj_bias, down_proj, down_proj_bias):
        import jax, jax.numpy as jnp
        import numpy as np
        TOP_K = 2

        def quick_gelu(x):
            return x * jax.nn.sigmoid(1.702 * x)
        B, S, H = hidden_states.shape
        E = router_b.shape[0]
        x = hidden_states.reshape(-1, H)
        T = x.shape[0]
        logits = x @ router_w + router_b
        top_w, sel = jax.lax.top_k(logits, TOP_K)
        top_w = jax.nn.softmax(top_w, axis=-1)
        tok_w = jnp.zeros((T, E), x.dtype).at[jnp.arange(T)[:, None], sel].add(top_w)

        def body(acc, params):
            Wgu, bgu, Wd, bd, w_e = params
            gu = x @ Wgu + bgu
            gate, up = jnp.split(gu, 2, axis=-1)
            act = (up + 1.0) * quick_gelu(gate)
            out = act @ Wd + bd
            return (acc + out * w_e[:, None], None)
        acc0 = jnp.zeros((T, H), x.dtype)
        acc, _ = jax.lax.scan(body, acc0, (gate_up_proj, gate_up_proj_bias, down_proj, down_proj_bias, tok_w.T))
        return acc.reshape(B, S, H)
    h = _L0_tok_ref(x, L0_tok_conv_w, L0_tok_conv_b, L0_tok_cls_token, L0_tok_pos_emb, L0_tok_ln_f, L0_tok_ln1_0, L0_tok_qkv_0, L0_tok_wo_0, L0_tok_ln2_0, L0_tok_gate_0, L0_tok_up_0, L0_tok_down_0, L0_tok_ln1_1, L0_tok_qkv_1, L0_tok_wo_1, L0_tok_ln2_1, L0_tok_gate_1, L0_tok_up_1, L0_tok_down_1)
    h = h + _L0_attn_ref(_layernorm(h, axis=-1), L0_attn_Wq, L0_attn_Wk, L0_attn_Wv, L0_attn_gn_weight, L0_attn_gn_bias)
    h = h + _L0_ffn_ref(_layernorm(h, axis=-1), L0_ffn_Wg, L0_ffn_W1, L0_ffn_b1, L0_ffn_W2, L0_ffn_b2, L0_ffn_ln_g, L0_ffn_ln_b, L0_ffn_out_g, L0_ffn_out_b)
    h = h + _L1_attn_ref(_layernorm(h, axis=-1), L1_attn_We1, L1_attn_be1, L1_attn_We2, L1_attn_be2, L1_attn_Wk1, L1_attn_bk1, L1_attn_Wk2, L1_attn_bk2)
    h = h + _L1_ffn_ref(_layernorm(h, axis=-1), L1_ffn_router_w, L1_ffn_router_b, L1_ffn_gate_up_proj, L1_ffn_gate_up_proj_bias, L1_ffn_down_proj, L1_ffn_down_proj_bias)
    return h

_drawn_inputs = setup_inputs


def setup_inputs(seed=0):
    import zlib

    import numpy as np

    out = dict(_drawn_inputs(seed))
    spreads = {'L0_tok_conv_b': (0.0, 0.1),
     'L0_tok_ln_f': (1.0, 0.2),
     'L0_tok_ln1_0': (1.0, 0.6),
     'L0_tok_ln2_0': (1.0, 0.6),
     'L0_tok_ln1_1': (1.0, 0.6),
     'L0_tok_ln2_1': (1.0, 0.6),
     'L0_attn_gn_weight': (1.0, 0.2),
     'L0_attn_gn_bias': (0.0, 0.1),
     'L0_ffn_b1': (0.0, 0.497),
     'L0_ffn_b2': (0.0, 0.1),
     'L0_ffn_ln_g': (1.0, 0.6),
     'L0_ffn_ln_b': (0.0, 0.424),
     'L0_ffn_out_g': (1.0, 0.2),
     'L0_ffn_out_b': (0.0, 0.1),
     'L1_attn_be1': (0.0, 0.1),
     'L1_attn_be2': (0.0, 0.1),
     'L1_attn_bk1': (0.0, 0.1),
     'L1_attn_bk2': (0.0, 0.1),
     'L1_ffn_router_b': (0.0, 0.1),
     'L1_ffn_gate_up_proj_bias': (0.0, 0.281),
     'L1_ffn_down_proj_bias': (0.0, 0.315)}
    factors = {}
    for name, (base, spread) in spreads.items():
        noise = np.random.default_rng([zlib.crc32(name.encode()), seed]).standard_normal(out[name].shape)
        drawn = base * np.exp(spread * noise) if base else spread * noise
        out[name] = jnp.asarray(drawn.astype(out[name].dtype))
    for name, factor in factors.items():
        out[name] = (out[name] * factor).astype(out[name].dtype)
    return out
```

```python
from contextlib import ExitStack

import numpy as np
import concourse.bass as bass
from concourse import mybir

ALU = mybir.AluOpType
ACT = mybir.ActivationFunctionType
AX = mybir.AxisListType
F32 = mybir.dt.float32
F32R = mybir.dt.float32r
U32 = mybir.dt.uint32

D = 128
BATCH = 64
PAIRS = BATCH // 2
PATCH = 16
SIDE = 14
PATCHES = SIDE * SIDE
T = PATCHES + 1
TP = T + 1
N = 2 * TP
C = TP // 2
HEADS, HD = 8, 16
FF = 344
FF_TILES = [(0, 128), (128, 128), (256, 88)]
EXPERTS = 8
H0T = 4
H1T = 2
KROWS = (C, C - 1)

NORMS_A = [(None, 1, 1e-6)] * 5 + [("all", 1, 1e-5), ("group", 8, 1e-5)]
NORMS_B = [("all", 1, 1e-5)] * 5

STAGES_A = ["embed"]
for _i in range(2):
    STAGES_A += [f"norm_a{2 * _i}", f"qkv{_i}", f"maxima{_i}", f"heads{_i}_0", f"heads{_i}_1",
                 f"proj{_i}", f"norm_a{2 * _i + 1}", f"ff{_i}"]
STAGES_A += ["norm_a4", "norm_a5", "ret_in", "norm_a6", "ret_qk", "ret0", "ret1", "ret_out"]
STAGES_B = (["take", "norm_b0", "norm_b1", "split0", "route0"] + [f"moe0_{e}" for e in range(EXPERTS)]
            + ["sum0", "norm_b2", "add0", "norm_b3", "att_in", "att_max", "att_pv", "att_out", "norm_b4", "split1",
               "route1"] + [f"moe1_{e}" for e in range(EXPERTS)] + ["store"])


def merged():
    return ["take"] + STAGES_A + STAGES_B[1:]


def tower(nc, x, w, out):
    def chunk(c):
        return slice(c * C, (c + 1) * C)

    with ExitStack() as ctx:
        def sb(name, shape, dt=F32):
            return ctx.enter_context(nc.sbuf_tensor(name, shape, dt))

        sems = []

        def sem(name):
            sems.append(ctx.enter_context(nc.semaphore(name)))
            return sems[-1]

        small = {name: sb("w_" + name, list(ap.shape)) for name, ap in w.items() if name not in SPLIT}
        split = {name: (sb("h_" + name, list(w[name].shape), F32R), sb("l_" + name, list(w[name].shape), F32R))
                 for name in SPLIT}
        ident = small["ident"]
        neg_half = sb("neg_half", [C, 4 * HEADS])
        bu1 = sb("bu1", [D, EXPERTS * H1T])

        img = sb("img", [128, SIDE, SIDE * PATCH])
        xa = sb("xa", [D, N])
        ha = sb("ha", [D, N])
        epsa, rsa = sb("epsa", [C, 4 * HEADS]), sb("rsa", [C, 4 * HEADS])
        qs, ks = sb("qs", [D, 2, N]), sb("ks", [D, 2, N])
        qr, kr = sb("qr", [D, 2, N], F32R), sb("kr", [D, 2, N], F32R)
        vp = sb("vp", [C, 4, HEADS, HD + 2])
        mp = sb("mp", [C, 4, 2, D])
        shared_a = sb("shared_a", [D, 8 * N])
        pt = shared_a[0:C, :].rearrange("p (g k h t) -> p g k h t", g=2, k=2, h=4)
        gu = shared_a[:, 0:3 * N].rearrange("p (a n) -> p a n", a=3)
        ot = shared_a[:, 3 * N:4 * N]
        th = shared_a[:, 4 * N:6 * N].rearrange("p (a n) -> p a n", a=2)
        sqa, xca = shared_a[:, 6 * N:7 * N], shared_a[:, 7 * N:8 * N]
        rec = sb("rec", [C, 2, HEADS])
        on = sb("on", [C, 4, D])
        xra, t1, t2, qeo = ha, qs[:, 0, :], qs[:, 1, :], ks
        hout = sb("hout", [D, N])

        hb = sb("hb", [D, N])
        x1 = sb("x1", [D, N])
        x2 = sb("x2", [D, N])
        x2h, x2l = sb("x2h", [D, N], F32R), sb("x2l", [D, N], F32R)
        epsb, rsb = sb("epsb", [C, 4 * HEADS]), sb("rsb", [C, 4 * HEADS])
        lg = sb("lg", [C, 4, EXPERTS])
        m8, i8 = sb("m8", [C, 4, 8]), sb("i8", [C, 4, 8], U32)
        i8f = sb("i8f", [C, 4, 2])
        dl, dth = sb("dl", [C, 4]), sb("dth", [C, 4])
        cw = sb("cw", [C, 2, 4])
        w1t, w2t = sb("w1t", [C, 4, EXPERTS]), sb("w2t", [C, 4, EXPERTS])
        wtok = sb("wtok", [C, 4, EXPERTS])
        wb = sb("wb", [D, 2, N])
        g = sb("g", [D, 3, N])
        gs = sb("gs", [D, 2, N])
        sqb, xcb = gs[:, 0, :], gs[:, 1, :]
        to = sb("to", [D, 2, N])
        acc = sb("acc", [D, N])
        e1, k1 = gs, to
        ks2, qs2, kr2, qr2 = g[:, 0, :], g[:, 1, :], x2h, x2l
        mp2 = sb("mp2", [C, 4, D])
        vt = sb("vt", [C, 4, D + 2])
        ptb = wb[0:C, :, :].rearrange("p a (k t) -> p (a k) t", k=2)
        recb = sb("recb", [C, 4])
        outs = sb("outs", [C, 4, D])
        ps = ctx.enter_context(nc.psum_tensor("ps", [128, 8, 512], F32))

        with ExitStack() as setup:
            loaded = setup.enter_context(nc.semaphore("loaded"))
            stage_ready = setup.enter_context(nc.semaphore("stage_ready"))
            high_done = setup.enter_context(nc.semaphore("high_done"))
            low_done = setup.enter_context(nc.semaphore("low_done"))
            preset = setup.enter_context(nc.semaphore("preset"))
            STEP = 1024
            stage = shared_a[:, 0:2 * STEP].rearrange("p (a n) -> p a n", a=2)
            pieces = [(n, a) for n in SPLIT for a in range(0, w[n].shape[1], STEP)]
            with nc.Block() as block:
                @block.sync
                def _(sp):
                    for b in range(2):
                        for ch in range(3):
                            sp.dma_start(img[64 * b + 16 * ch:64 * b + 16 * ch + 16, :, :],
                                         x[b, ch].rearrange("(i py) w -> py i w", py=PATCH)).then_inc(loaded, 16)
                    for name, ap in w.items():
                        if name not in SPLIT:
                            sp.dma_start(small[name][:], ap).then_inc(loaded, 16)
                    sp.wait_ge(loaded, 16 * (6 + len(small)))

                @block.scalar
                def _(act):
                    for n, (name, a) in enumerate(pieces):
                        if n >= 2:
                            act.wait_ge(low_done, n - 1)
                        act.dma_start(stage[:, n % 2, :], w[name][:, a:a + STEP]).then_inc(stage_ready, 16)
                        act.wait_ge(stage_ready, 16 * (n + 1))

                @block.vector
                def _(dve):
                    for n, (name, a) in enumerate(pieces):
                        high, low = (s[:, a:a + STEP] for s in split[name])
                        dve.wait_ge(stage_ready, 16 * (n + 1))
                        dve.tensor_copy(high, stage[:, n % 2, :]).then_inc(high_done, 1)
                        dve.wait_ge(high_done, n + 1)
                        dve.tensor_tensor(low, stage[:, n % 2, :], high.bitcast(F32), ALU.subtract).then_inc(low_done, 1)
                    dve.wait_ge(loaded, 16 * (6 + len(small)))
                    pos = small["pos"]
                    dve.tensor_scalar(pos[:, 1:T], pos[:, 1:T], small["cols"][:, COL["conv_b"]:COL["conv_b"] + 1], None,
                                      ALU.add)
                    dve.tensor_scalar(pos[:, 0:1], pos[:, 0:1], small["cols"][:, COL["cls"]:COL["cls"] + 1], None, ALU.add)
                    dve.tensor_scalar(bu1[:, :], small["bu"][:, :], 1.0, None, ALU.add).then_inc(preset, 1)

                @block.gpsimd
                def _(pool):
                    pool.memset(mp[:], 0.0)
                    pool.memset(mp2[:], 0.0)
                    pool.memset(vp[:], 1.0)
                    pool.memset(vt[:], 1.0)
                    pool.memset(neg_half[:], -0.5).then_inc(preset, 1)

        img_loaded, out_stored = sem("img_loaded"), sem("out_stored")
        embed_mm, embed_x = sem("embed_mm"), sem("embed_x")
        norm_sems = {s: {k: sem(f"norm_{s}_{k}") for k in ("centered", "square", "kept", "stat", "eps", "rsqrt", "spread",
                                                           "out", "final")} for s in "ab"}
        group_spread, rows_done = sem("group_spread"), sem("rows_done")
        qk_mm, qk_kept, qk_round, v_mm, v_kept = (sem(n) for n in ("qk_mm", "qk_kept", "qk_round", "v_mm", "v_kept"))
        sq_mm, max_done, max_t, q_aug = (sem(n) for n in ("sq_mm", "max_done", "max_t", "q_aug"))
        st_mm, exp_done, pv_mm, rec_done, on_done = (sem(n) for n in ("st_mm", "exp_done", "pv_mm", "rec_done", "on_done"))
        ot_mm, ot_kept, proj_mm, x_proj = (sem(n) for n in ("ot_mm", "ot_kept", "proj_mm", "x_proj"))
        ff_mm, ff_tanh, ff_gate, ff_act, down_mm, x_ff = (sem(n) for n in ("ff_mm", "ff_tanh", "ff_gate", "ff_act", "down_mm", "x_ff"))
        rot_mm, rot_part, rot_sum, rv_mm, rv_kept = (sem(n) for n in ("rot_mm", "rot_part", "rot_sum", "rv_mm", "rv_kept"))
        rq_tanh, rq_gate, rq_done = (sem(n) for n in ("rq_tanh", "rq_gate", "rq_done"))
        rs_mm, decayed, ro_mm, ro_kept, rt_mm, ret_sum, a_done = (
            sem(n) for n in ("rs_mm", "decayed", "ro_mm", "ro_kept", "rt_mm", "ret_sum", "a_done"))
        taken, high_x, split_x = sem("taken"), sem("high_x"), sem("split_x")
        lg_mm, lg_kept, top_done, idx_done, idx_f, gap_done, gap_tanh, conf_done, pick_done, w_done, wb_mm, wb_kept = (
            sem(n) for n in ("lg_mm", "lg_kept", "top_done", "idx_done", "idx_f", "gap_done", "gap_tanh", "conf_done",
                             "pick_done", "w_done", "wb_mm", "wb_kept"))
        hid_mm, hid_act, hid_up, exp_mm, exp_scaled, acc_done = (
            sem(n) for n in ("hid_mm", "hid_act", "hid_up", "exp_mm", "exp_scaled", "acc_done"))
        x1_sum, hb_add = sem("x1_sum"), sem("hb_add")
        ai_mm, ai_relu, akq_mm, akq_kept, akq_round, av_mm, av_kept = (
            sem(n) for n in ("ai_mm", "ai_relu", "akq_mm", "akq_kept", "akq_round", "av_mm", "av_kept"))
        am_mm, am_max, am_t, am_aug, as_mm, as_exp, ao_mm, ao_rec, ao_norm, at_mm = (
            sem(n) for n in ("am_mm", "am_max", "am_t", "am_aug", "as_mm", "as_exp", "ao_mm", "ao_rec", "ao_norm", "at_mm"))
        y_done, y_mm, y_kept = sem("y_done"), sem("y_mm"), sem("y_kept")

        cols = small["cols"]

        def col(name, k=0):
            return cols[:, COL[name] + k:COL[name] + k + 1]

        def heads_of(bank, rows=C):
            return ps[0:rows, bank:bank + 2, 0:2 * TP].rearrange("p n (h t) -> p n h t", h=2)

        def norm_io(s, n):
            if s == "a":
                return [(xa, ha, col("ln1", 0), None, (embed_x, 2)), (xa, ha, col("ln2", 0), None, (x_proj, 1)),
                        (xa, ha, col("ln1", 1), None, (x_ff, 1)), (xa, ha, col("ln2", 1), None, (x_proj, 2)),
                        (xa, hout, col("ln_f"), None, (x_ff, 2)), (hout, xra, None, None, (norm_sems["a"]["final"], 5)),
                        (t1, t1, col("gn_w"), col("gn_b"), (rot_sum, 2))][n]
            return [(hb, x1, None, None, (taken, 1)), (x1, x2, col("ln_g"), col("ln_b"), (norm_sems["b"]["final"], 1)),
                    (x1, x1, col("out_g"), col("out_b"), (x1_sum, 1)), (hb, x2, None, None, (hb_add, 1)),
                    (hb, x2, None, None, (hb_add, 2))][n]

        NORMS = {"a": NORMS_A, "b": NORMS_B}
        BUF = {"a": (sqa, xca, epsa, rsa, 0, 1, 2), "b": (sqb, xcb, epsb, rsb, 4, 5, 6)}

        def centered_before(s, n):
            return sum(c is not None for c, _, _ in NORMS[s][:n])

        def stage_norm_pe(pe, s, n):
            sq, xc, eps_t, rs, bank_c, bank_s, bank_b = BUF[s]
            S = norm_sems[s]
            cen, groups, eps = NORMS[s][n]
            src, _, _, _, (ready, count) = norm_io(s, n)
            if cen is not None:
                pe.wait_ge(ready, count)
                pe.matmul(ps[:, bank_c, 0:N], small["cen_" + cen][:], src[:, :], start=True, stop=True)\
                    .then_inc(S["centered"], 1)
            pe.wait_ge(S["square"], n + 1)
            rhs = small["stat_all"][:, 0:1] if groups == 1 else small["stat_group"][:, :]
            for c in range(4):
                mm = pe.matmul(ps[0:C, bank_s, c * groups:(c + 1) * groups], sq[:, chunk(c)], rhs, start=True, stop=True)
            mm.then_inc(S["stat"], 1)
            if groups == 1:
                pe.wait_ge(S["rsqrt"], n + 1)
            else:
                pe.wait_ge(group_spread, 1)
            for c in range(4):
                one = rs[:, c:c + 1].to_broadcast([C, D]) if groups == 1 else shared_a[0:C, c * D:(c + 1) * D]
                mm = pe.matmul(ps[:, bank_b, chunk(c)], one, ident[0:C, 0:C], start=True, stop=True)
            mm.then_inc(S["spread"], 1)

        def stage_norm_act(act, s, n):
            sq, xc, eps_t, rs, bank_c, bank_s, bank_b = BUF[s]
            S = norm_sems[s]
            src, _, _, _, (ready, count) = norm_io(s, n)
            if NORMS[s][n][0] is None:
                act.wait_ge(ready, count)
                act.activation(sq[:, :], src[:, :], ACT.Square).then_inc(S["square"], 1)
            else:
                act.wait_ge(S["centered"], centered_before(s, n) + 1)
                act.activation(sq[:, :], ps[:, bank_c, 0:N], ACT.Square).then_inc(S["square"], 1)
                act.activation(xc[:, :], ps[:, bank_c, 0:N], ACT.Identity).then_inc(S["kept"], 1)

        def stage_norm_dve(dve, s, n):
            sq, xc, eps_t, rs, bank_c, bank_s, bank_b = BUF[s]
            S = norm_sems[s]
            cen, groups, eps = NORMS[s][n]
            src, dst, weight, bias, _ = norm_io(s, n)
            dve.wait_ge(S["stat"], n + 1)
            dve.tensor_scalar(eps_t[:, 0:4 * groups], ps[0:C, bank_s, 0:4 * groups], eps, None, ALU.add)\
                .then_inc(S["eps"], 1)
            dve.wait_ge(S["spread"], n + 1)
            if cen is not None:
                dve.wait_ge(S["kept"], centered_before(s, n) + 1)
                src = xc
            out_sem = S["out"] if bias is not None else S["final"]
            if weight is None:
                dve.tensor_tensor(dst[:, :], src[:, :], ps[:, bank_b, 0:N], ALU.mult).then_inc(out_sem, 1)
            else:
                dve.scalar_tensor_tensor(out=dst[:, :], in0=src[:, :], scalar=weight, in1=ps[:, bank_b, 0:N],
                                         op0=ALU.mult, op1=ALU.mult).then_inc(out_sem, 1)
            if bias is not None:
                before = {("a", 6): 0, ("b", 1): 0, ("b", 2): 1}[s, n]
                dve.wait_ge(S["out"], before + 1)
                dve.tensor_scalar(dst[:, :], dst[:, :], bias, None, ALU.add).then_inc(S["final"], 1)

        def stage_norm_pool(pool, s, n):
            sq, xc, eps_t, rs, bank_c, bank_s, bank_b = BUF[s]
            S = norm_sems[s]
            groups = NORMS[s][n][1]
            pool.wait_ge(S["eps"], n + 1)
            pool.tensor_tensor(rs[:, 0:4 * groups], eps_t[:, 0:4 * groups], neg_half[:, 0:4 * groups], ALU.pow)\
                .then_inc(S["rsqrt"], 1)
            if groups > 1:
                pool.wait_ge(S["rsqrt"], n + 1)
                pool.tensor_copy(shared_a[0:C, 0:4 * D].rearrange("p (g d) -> p g d", d=D // groups),
                                 rs[:, 0:4 * groups].unsqueeze(2).to_broadcast([C, 4 * groups, D // groups]))\
                    .then_inc(group_spread, 1)

        final_a, final_b = norm_sems["a"]["final"], norm_sems["b"]["final"]

        def body(order, pair_a, pair_b, prefetch):
            with nc.Block(no_gpsimd_drain=True) as block:
                @block.sync
                def _(sp):
                    if prefetch is not None:
                        sp.wait_ge(embed_mm, 2)
                        for b in range(2):
                            for ch in range(3):
                                sp.dma_start(img[64 * b + 16 * ch:64 * b + 16 * ch + 16, :, :],
                                             x[2 * prefetch + b, ch].rearrange("(i py) w -> py i w", py=PATCH))\
                                    .then_inc(img_loaded, 16)
                        sp.wait_ge(img_loaded, 96)
                    if pair_b is not None:
                        sp.wait_ge(y_kept, 1)
                        for k in range(2):
                            sp.dma_start(out[bass.ts(pair_b, 2), k * C:k * C + KROWS[k], :].rearrange("b t d -> t b d"),
                                         outs[:, :, :].rearrange("p (b k) d -> p b k d", k=2)[0:KROWS[k], :, k, :])\
                                .then_inc(out_stored, 16)
                        sp.wait_ge(out_stored, 32)

                @block.tensor
                def _(pe):
                    def embed():
                        for px in range(PATCH):
                            for b in range(2):
                                r = slice(64 * b, 64 * b + 48)
                                mm = pe.matmul(ps[:, b, 0:PATCHES].rearrange("p (i j) -> p i j", i=SIDE),
                                               small["wp"][r, px * D:(px + 1) * D], img[r, :, px::PATCH],
                                               start=(px == 0), stop=(px == PATCH - 1))
                                if px == PATCH - 1:
                                    mm.then_inc(embed_mm, 1)

                    def row_groups(n):
                        return n + 1

                    def qkv(i):
                        pe.wait_ge(final_a, 2 * i + 1)
                        for j in range(4):
                            if j >= 1:
                                pe.wait_ge(qk_kept, 4 * i + j)
                                pe.wait_ge(qk_round, 4 * i + j)
                            pe.matmul(ps[:, j % 2, 0:N], small[f"wqk{i}"][:, j * D:(j + 1) * D], ha[:, :],
                                      start=True, stop=True).then_inc(qk_mm, 1)
                        for c in range(4):
                            mm = pe.matmul(ps[0:C, 2, c * D:(c + 1) * D], ha[:, chunk(c)], small[f"wv{i}"][:, :],
                                           start=True, stop=True)
                        mm.then_inc(v_mm, 1)

                    def maxima(i):
                        pe.wait_ge(qk_round, 4 * i + 4)
                        pe.wait_ge(qk_kept, 4 * i + 4)
                        pe.wait_ge(v_kept, 2 * i + 2)
                        for u in range(8):
                            hg, c = divmod(u, 4)
                            bank = 2 * (u % 2)
                            if u >= 2:
                                pe.wait_ge(max_done, 8 * i + u - 1)
                            for h in range(4):
                                r = slice(32 * h, 32 * h + 32)
                                if h == 2:
                                    pe.wait_ge(rows_done, row_groups(16 * i + u))
                                mm = pe.matmul(ps[0:C, bank + h % 2, (h // 2) * TP:(h // 2 + 1) * TP],
                                               qr[r, hg, chunk(c)], kr[r, hg, (c // 2) * TP:(c // 2 + 1) * TP],
                                               start=True, stop=True)
                                if h == 1:
                                    mm.then_inc(rows_done, 1)
                            mm.then_inc(sq_mm, 1)
                        for hg in range(2):
                            pe.wait_ge(max_done, 8 * i + 8)
                            for c in range(4):
                                mm = pe.transpose(ps[:, hg, chunk(c)], mp[:, c, hg, :], ident[0:C, 0:C])
                            mm.then_inc(max_t, 1)

                    def heads(i, b):
                        pe.wait_ge(q_aug, 2 * i + 2)
                        for u in range(4):
                            hg, kk = divmod(u, 2)
                            n = 8 * i + 4 * b + u
                            bank = 2 * (u % 2)
                            if u >= 2 or b:
                                pe.wait_ge(exp_done, n - 1)
                            if u < 2 and b:
                                pe.wait_ge(on_done, 2 * i + 1)
                            for h in range(4):
                                r = slice(32 * h, 32 * h + 32)
                                if h == 2:
                                    pe.wait_ge(rows_done, row_groups(16 * i + 8 + 4 * b + u))
                                mm = pe.matmul(ps[0:C, bank + h % 2, (h // 2) * TP:(h // 2 + 1) * TP],
                                               ks[r, hg, chunk(2 * b + kk)], qs[r, hg, b * TP:(b + 1) * TP],
                                               start=True, stop=True)
                                if h == 1:
                                    mm.then_inc(rows_done, 1)
                            mm.then_inc(st_mm, 1)
                        pe.wait_ge(exp_done, 8 * i + 4 * b + 4)
                        for qc in range(2):
                            for h in range(HEADS):
                                for kk in range(2):
                                    rows = KROWS[kk]
                                    mm = pe.matmul(ps[0:C, qc, h * 18:(h + 1) * 18],
                                                   pt[0:rows, h // 4, kk, h % 4, chunk(qc)],
                                                   vp[0:rows, 2 * b + kk, h, :], start=(kk == 0), stop=(kk == 1))
                        mm.then_inc(pv_mm, 1)

                    def proj(i):
                        pe.wait_ge(on_done, 2 * i + 2)
                        for c in range(4):
                            mm = pe.transpose(ps[:, 2, chunk(c)], on[:, c, :], ident[0:C, 0:C])
                        mm.then_inc(ot_mm, 1)
                        pe.wait_ge(ot_kept, i + 1)
                        pe.matmul(ps[:, 3, 0:N], small[f"wo{i}"][:, :], ot[:, :], start=True, stop=True).then_inc(proj_mm, 1)

                    def ff(i):
                        pe.wait_ge(final_a, 2 * i + 2)
                        for t, (a, m) in enumerate(FF_TILES):
                            if t >= 1:
                                pe.wait_ge(ff_act, 3 * i + t)
                            pe.matmul(ps[0:m, 0, 0:N], small[f"wg{i}"][:, a:a + m], ha[:, :], start=True, stop=True)
                            pe.matmul(ps[0:m, 1, 0:N], small[f"wu{i}"][:, a:a + m], ha[:, :], start=True, stop=True)\
                                .then_inc(ff_mm, 1)
                        for t, (a, m) in enumerate(FF_TILES):
                            pe.wait_ge(ff_act, 3 * i + t + 1)
                            mm = pe.matmul(ps[:, 2, 0:N], small[f"wd{i}"][0:m, t * D:(t + 1) * D], gu[0:m, t, :],
                                           start=(t == 0), stop=(t == 2))
                        mm.then_inc(down_mm, 1)

                    def ret_in():
                        pe.wait_ge(final_a, 6)
                        for j in range(2):
                            for r in range(2):
                                if j:
                                    pe.wait_ge(rot_part, 1 + r)
                                pe.matmul(ps[:, r, 0:N], small["rqk"][:, (2 * j + r) * D:(2 * j + r + 1) * D], xra[:, :],
                                          start=True, stop=True).then_inc(rot_mm, 1)
                        for c in range(4):
                            mm = pe.matmul(ps[0:C, 3, c * D:(c + 1) * D], xra[:, chunk(c)], small["rv"][:, :],
                                           start=True, stop=True)
                        mm.then_inc(rv_mm, 1)

                    def ret(b):
                        if b == 0:
                            pe.wait_ge(final_a, 7)
                            pe.wait_ge(rq_done, 2)
                            pe.wait_ge(rv_kept, 1)
                        for hg in range(2):
                            u = 2 * b + hg
                            if u:
                                pe.wait_ge(decayed, 2 * u)
                            for h in range(4):
                                hh = 4 * hg + h
                                r = slice(32 * (hh // 2), 32 * (hh // 2) + 32)
                                pe.matmul(ps[0:C, h // 2, (h % 2) * TP:(h % 2 + 1) * TP], t1[r, chunk(2 * b)],
                                          qeo[r, hh % 2, b * TP:(b + 1) * TP], start=True, stop=True)
                                if h == 2:
                                    pe.wait_ge(rows_done, row_groups(32 + u))
                                mm = pe.matmul(ps[0:C, 2, h * C:(h + 1) * C], t1[r, chunk(2 * b + 1)],
                                               qeo[r, hh % 2, b * TP + C:(b + 1) * TP], start=True, stop=True)
                                if h == 1:
                                    mm.then_inc(rows_done, 1)
                            mm.then_inc(rs_mm, 1)
                            pe.wait_ge(decayed, 2 * u + 2)
                            for h in range(4):
                                hh = 4 * hg + h
                                v = slice(hh * HD, (hh + 1) * HD)
                                o = slice(2 * b * D + hh * HD, 2 * b * D + (hh + 1) * HD)
                                o1 = slice((2 * b + 1) * D + hh * HD, (2 * b + 1) * D + (hh + 1) * HD)
                                pe.matmul(ps[0:C, 3, o], pt[:, hg, 0, h, 0:C], on[:, 2 * b, v], start=True, stop=True)
                                pe.matmul(ps[0:C, 3, o1], pt[:, hg, 0, h, C:TP], on[:, 2 * b, v], start=True, stop=False)
                                mm = pe.matmul(ps[0:C, 3, o1], pt[0:C - 1, hg, 1, h, 0:C], on[0:C - 1, 2 * b + 1, v],
                                               start=False, stop=True)
                        if b:
                            mm.then_inc(ro_mm, 1)

                    def ret_out():
                        pe.wait_ge(ro_kept, 1)
                        for c in range(4):
                            mm = pe.transpose(ps[:, 0, chunk(c)], shared_a[0:C, c * D:(c + 1) * D],
                                              ident[0:C, 0:C])
                        mm.then_inc(rt_mm, 1)

                    def route(m):
                        pe.wait_ge(final_b, (2, 5)[m])
                        if m:
                            pe.wait_ge(at_mm, 1)
                        for c in range(4):
                            mm = pe.matmul(ps[0:C, 6, c * EXPERTS:(c + 1) * EXPERTS], x2[:, chunk(c)],
                                           small[f"route{m}"][:, :], start=True, stop=True)
                        mm.then_inc(lg_mm, 1)

                    def weights(m, e):
                        pe.wait_ge(w_done, m + 1)
                        if e >= 2:
                            pe.wait_ge(exp_scaled, EXPERTS * m + e - 1)
                        for c in range(4):
                            mm = pe.matmul(ps[:, 6 + e % 2, chunk(c)], wtok[:, c, e:e + 1].to_broadcast([C, D]),
                                           ident[0:C, 0:C], start=True, stop=True)
                        mm.then_inc(wb_mm, 1)

                    def hidden(name, tile, bank):
                        hi, lo = split[name]
                        s = slice(tile * D, (tile + 1) * D)
                        pe.matmul(ps[:, bank, 0:N], hi[:, s], x2h[:, :], start=True, stop=False)
                        pe.matmul(ps[:, bank, 0:N], lo[:, s], x2h[:, :], start=False, stop=False)
                        return pe.matmul(ps[:, bank, 0:N], hi[:, s], x2l[:, :], start=False, stop=True)

                    def up0(n):
                        if n >= 2:
                            pe.wait_ge(hid_act, n - 1)
                        hidden("W1", n, 4 + n % 2).then_inc(hid_mm, 1)

                    def down(m, n, tiles, base):
                        e, t = divmod(n, tiles)
                        if t == 0:
                            pe.wait_ge(wb_kept, EXPERTS * m + e + 1)
                        pe.wait_ge(*((hid_act, n + 1) if m == 0 else (hid_up, n + 1)))
                        pe.matmul(ps[:, 6 + e % 2, 0:N], small[("W2", "Wd")[m]][:, n * D:(n + 1) * D],
                                  g[:, (base + n) % 3, :], start=(t == 0), stop=(t == tiles - 1)).then_inc(exp_mm, 1)

                    def moe0(e):
                        if e == 0:
                            pe.wait_ge(split_x, 1)
                            up0(0)
                            up0(1)
                        weights(0, e)
                        for n in range(H0T * e, H0T * e + H0T):
                            if n + 2 < H0T * EXPERTS:
                                up0(n + 2)
                            down(0, n, H0T, 0)

                    def up1(n):
                        e, t = divmod(n, H1T)
                        if n >= 1:
                            pe.wait_ge(hid_up, n)
                        hidden("Wgu", 4 * e + t, 4)
                        hidden("Wgu", 4 * e + 2 + t, 5).then_inc(hid_mm, 1)

                    def moe1(e):
                        base = H0T * EXPERTS
                        if e == 0:
                            pe.wait_ge(split_x, 2)
                            up1(0)
                        weights(1, e)
                        for n in range(H1T * e, H1T * e + H1T):
                            if n + 1 < H1T * EXPERTS:
                                up1(n + 1)
                            down(1, n, H1T, base)

                    def att_in():
                        pe.wait_ge(final_b, 4)
                        for j in range(4):
                            if j >= 2:
                                pe.wait_ge(ai_relu, j - 1)
                            pe.matmul(ps[:, 4 + j % 2, 0:N], small["we1k1"][:, j * D:(j + 1) * D], x2[:, :],
                                      start=True, stop=True).then_inc(ai_mm, 1)
                        pe.wait_ge(ai_relu, 4)
                        for j in range(2):
                            for t in range(2):
                                mm = pe.matmul(ps[:, 6 + j, 0:N], small["wk2"][:, (2 * t + j) * D:(2 * t + j + 1) * D],
                                               k1[:, t, :], start=(t == 0), stop=(t == 1))
                            mm.then_inc(akq_mm, 1)
                        for c in range(4):
                            for t in range(2):
                                mm = pe.matmul(ps[0:C, 4, c * D:(c + 1) * D], e1[:, t, chunk(c)],
                                               small["we2"][:, t * D:(t + 1) * D], start=(t == 0), stop=(t == 1))
                        mm.then_inc(av_mm, 1)

                    def att_max():
                        pe.wait_ge(akq_round, 2)
                        for c in range(4):
                            mm = pe.matmul(ps[0:C, 6 + c // 2, (c % 2) * TP:(c % 2 + 1) * TP], qr2[:, chunk(c)],
                                           kr2[:, (c // 2) * TP:(c // 2 + 1) * TP], start=True, stop=True)
                        mm.then_inc(am_mm, 1)
                        pe.wait_ge(am_max, 1)
                        for c in range(4):
                            mm = pe.transpose(ps[:, 5, chunk(c)], mp2[:, c, :], ident[0:C, 0:C])
                        mm.then_inc(am_t, 1)

                    def att_pv():
                        pe.wait_ge(am_aug, 1)
                        pe.wait_ge(av_kept, 1)
                        for b in range(2):
                            for kk in range(2):
                                mm = pe.matmul(ps[0:C, 6 + b, kk * TP:(kk + 1) * TP], ks2[:, chunk(2 * b + kk)],
                                               qs2[:, b * TP:(b + 1) * TP], start=True, stop=True)
                        mm.then_inc(as_mm, 1)
                        pe.wait_ge(as_exp, 1)
                        for b in range(2):
                            for qc in range(2):
                                for kk in range(2):
                                    rows = KROWS[kk]
                                    mm = pe.matmul(ps[0:C, 4 + b, qc * 130:(qc + 1) * 130], ptb[0:rows, 2 * b + kk, chunk(qc)],
                                                   vt[0:rows, 2 * b + kk, :], start=(kk == 0), stop=(kk == 1))
                        mm.then_inc(ao_mm, 1)

                    def att_out():
                        pe.wait_ge(ao_norm, 1)
                        for c in range(4):
                            mm = pe.transpose(ps[:, 6, chunk(c)], outs[:, c, :], ident[0:C, 0:C])
                        mm.then_inc(at_mm, 1)

                    def store():
                        pe.wait_ge(y_done, 1)
                        for c in range(4):
                            mm = pe.transpose(ps[0:C, 4, c * D:(c + 1) * D], hb[:, chunk(c)], ident[:, :])
                        mm.then_inc(y_mm, 1)

                    steps = {"embed": embed, "ret_in": ret_in, "ret0": lambda: ret(0), "ret1": lambda: ret(1),
                             "ret_out": ret_out, "route0": lambda: route(0), "route1": lambda: route(1),
                             "att_in": att_in, "att_max": att_max, "att_pv": att_pv, "att_out": att_out, "store": store}
                    for stage in order:
                        walk(stage, steps, {"norm_": lambda s, n: stage_norm_pe(pe, s, n), "qkv": qkv, "maxima": maxima,
                                            "heads": heads, "proj": proj, "ff": ff, "moe0_": moe0, "moe1_": moe1})

                @block.scalar
                def _(act):
                    def keep(dst, src, done, bias=0.0, func=ACT.Identity, scale=1.0):
                        act.activation(dst, src, func, bias=bias, scale=scale).then_inc(done, 1)

                    def qkv(i):
                        for j in range(4):
                            act.wait_ge(qk_mm, 4 * i + j + 1)
                            keep((qs if j < 2 else ks)[:, j % 2, :], ps[:, j % 2, 0:N], qk_kept,
                                 bias=0.0 if j < 2 else col("one16"))
                        act.wait_ge(v_mm, i + 1)
                        v = ps[0:C, 2, :].rearrange("p (c h d) -> p c h d", c=4, h=HEADS)
                        for half in range(2):
                            keep(vp[:, 2 * half:2 * half + 2, :, 0:HD], v[:, 2 * half:2 * half + 2], v_kept)

                    def heads(i, b):
                        for u in range(4):
                            hg, kk = divmod(u, 2)
                            act.wait_ge(st_mm, 8 * i + 4 * b + u + 1)
                            if u == 0 and (b or i):
                                act.wait_ge(pv_mm, 2 * i + b)
                            keep(pt[:, hg, kk, :, :].rearrange("p (h n) t -> p n h t", h=2), heads_of(2 * (u % 2)), exp_done,
                                 func=ACT.Exp, scale=HD ** -0.5)

                    def proj(i):
                        act.wait_ge(ot_mm, i + 1)
                        keep(ot[:, :], ps[:, 2, 0:N], ot_kept)

                    def ff(i):
                        for t, (a, m) in enumerate(FF_TILES):
                            act.wait_ge(ff_mm, 3 * i + t + 1)
                            if t >= 2:
                                act.wait_ge(ff_gate, 3 * i + t - 1)
                            keep(th[0:m, t % 2, :], ps[0:m, 0, 0:N], ff_tanh, func=ACT.Tanh, scale=0.5)

                    def ret_in():
                        act.wait_ge(rv_mm, 1)
                        keep(on[:, :, :].rearrange("p c d -> p (c d)"), ps[0:C, 3, :], rv_kept)

                    def ret_qk():
                        act.wait_ge(rot_sum, 1)
                        keep(th[:, 0, :], t2[:, :], rq_tanh, func=ACT.Tanh, scale=0.5)

                    def ret_out():
                        act.wait_ge(ro_mm, 1)
                        keep(shared_a[0:C, 0:4 * D], ps[0:C, 3, :], ro_kept)

                    def take():
                        keep(hb[:, :], hout[:, :], taken)

                    def splitx(m):
                        act.wait_ge(final_b, (2, 5)[m])
                        keep(x2h[:, :], x2[:, :], high_x)

                    def route(m):
                        act.wait_ge(gap_done, m + 1)
                        keep(dth[:, :], dl[:, :], gap_tanh, func=ACT.Tanh, scale=0.5)

                    def weights(m, e):
                        act.wait_ge(wb_mm, EXPERTS * m + e + 1)
                        keep(wb[:, e % 2, :], ps[:, 6 + e % 2, 0:N], wb_kept)

                    def moe0(e):
                        weights(0, e)
                        for n in range(H0T * e, H0T * e + H0T):
                            act.wait_ge(hid_mm, n + 1)
                            if n >= 3:
                                act.wait_ge(exp_mm, n - 2)
                            keep(g[:, n % 3, :], ps[:, 4 + n % 2, 0:N], hid_act, func=ACT.Gelu_apprx_tanh,
                                 bias=small["b1"][:, n:n + 1])

                    def moe1(e):
                        base = H0T * EXPERTS
                        weights(1, e)
                        for n in range(H1T * e, H1T * e + H1T):
                            act.wait_ge(hid_mm, base + n + 1)
                            if n >= 2:
                                act.wait_ge(hid_up, n - 1)
                            keep(gs[:, n % 2, :], ps[:, 4, 0:N], hid_act, func=ACT.Gelu_apprx_sigmoid,
                                 bias=small["bg"][:, n:n + 1])

                    def att_in():
                        for j in range(4):
                            act.wait_ge(ai_mm, j + 1)
                            keep((e1 if j < 2 else k1)[:, j % 2, :], ps[:, 4 + j % 2, 0:N], ai_relu, func=ACT.Relu,
                                 bias=col("be1k1", j))
                        for j in range(2):
                            act.wait_ge(akq_mm, j + 1)
                            keep((ks2, qs2)[j][:, :], ps[:, 6 + j, 0:N], akq_kept, bias=col("bkq", j))
                        act.wait_ge(av_mm, 1)
                        keep(vt[:, :, 0:D], ps[0:C, 4, :].rearrange("p (c d) -> p c d", c=4), av_kept)

                    def att_pv():
                        act.wait_ge(as_mm, 1)
                        keep(ptb[:, :, :].rearrange("p (b k) t -> p b k t", k=2), heads_of(6), as_exp, func=ACT.Exp)

                    def store():
                        act.wait_ge(y_mm, 1)
                        keep(outs[:, :, :].rearrange("p c d -> p (c d)"), ps[0:C, 4, :], y_kept)

                    steps = {"ret_in": ret_in, "ret_qk": ret_qk, "ret_out": ret_out, "take": take,
                             "split0": lambda: splitx(0), "split1": lambda: splitx(1),
                             "route0": lambda: route(0), "route1": lambda: route(1), "att_in": att_in, "att_pv": att_pv,
                             "store": store}
                    for stage in order:
                        walk(stage, steps, {"norm_": lambda s, n: stage_norm_act(act, s, n), "qkv": qkv, "heads": heads,
                                            "proj": proj, "ff": ff, "moe0_": moe0, "moe1_": moe1})

                @block.vector
                def _(dve):
                    def embed():
                        both = xa[:, :].rearrange("p (b t) -> p b t", b=2)
                        pos = small["pos"]
                        dve.tensor_copy(both[:, :, 0:TP:T], pos[:, 0:TP:T].unsqueeze(1).to_broadcast([D, 2, 2]))
                        for b in range(2):
                            dve.wait_ge(embed_mm, b + 1)
                            dve.tensor_tensor(both[:, b, 1:T], ps[:, b, 0:PATCHES], pos[:, 1:T], ALU.add).then_inc(embed_x, 1)

                    def qkv(i):
                        for j in range(4):
                            dve.wait_ge(qk_kept, 4 * i + j + 1)
                            dve.tensor_copy((qr if j < 2 else kr)[:, j % 2, :], ps[:, j % 2, 0:N]).then_inc(qk_round, 1)

                    def maxima(i):
                        for u in range(8):
                            hg, c = divmod(u, 4)
                            dve.wait_ge(sq_mm, 8 * i + u + 1)
                            m = mp[:, c, hg, :].rearrange("p (h n r) -> p n h r", n=2, h=2)[:, :, :, HD]
                            dve.tensor_reduce(m, heads_of(2 * (u % 2))[:, :, :, 0:T], AX.X, ALU.max, negate=True)\
                                .then_inc(max_done, 1)
                        for hg in range(2):
                            dve.wait_ge(max_t, 2 * i + hg + 1)
                            dve.tensor_tensor(qs[:, hg, :], qs[:, hg, :], ps[:, hg, 0:N], ALU.add).then_inc(q_aug, 1)

                    def heads(i, b):
                        dve.wait_ge(pv_mm, 2 * i + b + 1)
                        o = ps[0:C, 0:2, 0:HEADS * 18].rearrange("p q (h d) -> p q h d", h=HEADS)
                        dve.reciprocal(rec[:, :, :], o[:, :, :, HD]).then_inc(rec_done, 1)
                        dve.wait_ge(rec_done, 2 * i + b + 1)
                        dve.tensor_tensor(on[:, 2 * b:2 * b + 2, :].rearrange("p q (h d) -> p q h d", h=HEADS),
                                          o[:, :, :, 0:HD], rec[:, :, :].unsqueeze(3).to_broadcast([C, 2, HEADS, HD]),
                                          ALU.mult).then_inc(on_done, 1)

                    def proj(i):
                        dve.wait_ge(proj_mm, i + 1)
                        dve.tensor_tensor(xa[:, :], xa[:, :], ps[:, 3, 0:N], ALU.add).then_inc(x_proj, 1)

                    def ff(i):
                        for t, (a, m) in enumerate(FF_TILES):
                            n = 3 * i + t + 1
                            dve.wait_ge(ff_tanh, n)
                            dve.scalar_tensor_tensor(out=gu[0:m, t, :], in0=th[0:m, t % 2, :], scalar=1.0,
                                                     in1=ps[0:m, 0, 0:N], op0=ALU.add, op1=ALU.mult).then_inc(ff_gate, 1)
                            dve.wait_ge(ff_gate, n)
                            dve.tensor_tensor(gu[0:m, t, :], gu[0:m, t, :], ps[0:m, 1, 0:N], ALU.mult).then_inc(ff_act, 1)
                        dve.wait_ge(down_mm, i + 1)
                        dve.scalar_tensor_tensor(out=xa[:, :], in0=ps[:, 2, 0:N], scalar=0.5, in1=xa[:, :],
                                                 op0=ALU.mult, op1=ALU.add).then_inc(x_ff, 1)

                    def table(name):
                        return small[name][:, :].unsqueeze(1).to_broadcast([D, 2, TP])

                    def pair3(t):
                        return t.rearrange("p (b t) -> p b t", b=2)

                    def ret_in():
                        for j, dst in enumerate((t2, t1)):
                            dve.wait_ge(rot_mm, 2 * j + 1)
                            dve.tensor_tensor(pair3(dst[:, :]), pair3(ps[:, 0, 0:N]), table("cos"), ALU.mult)\
                                .then_inc(rot_part, 1)
                            dve.wait_ge(rot_mm, 2 * j + 2)
                            if j:
                                dve.wait_ge(rot_sum, 1)
                            dve.tensor_tensor(pair3(sqa[:, :]), pair3(ps[:, 1, 0:N]), table("sin"), ALU.mult)\
                                .then_inc(rot_part, 1)
                            dve.wait_ge(rot_part, 2 * j + 2)
                            dve.tensor_tensor(dst[:, :], dst[:, :], sqa[:, :], ALU.add).then_inc(rot_sum, 1)

                    def ret_qk():
                        dve.wait_ge(rq_tanh, 1)
                        dve.scalar_tensor_tensor(out=t2[:, :], in0=th[:, 0, :], scalar=1.0, in1=t2[:, :],
                                                 op0=ALU.add, op1=ALU.mult).then_inc(rq_gate, 1)
                        dve.wait_ge(rq_gate, 1)
                        for e in range(2):
                            dve.tensor_scalar(qeo[:, e, :], t2[:, :], col("evenodd", e), None, ALU.mult).then_inc(rq_done, 1)

                    def ret(b):
                        decay = small["decay"]
                        for hg in range(2):
                            u = 2 * b + hg
                            dve.wait_ge(rs_mm, u + 1)
                            for n in range(2):
                                ins = dve.tensor_tensor(pt[:, hg, 0, 2 * n:2 * n + 2, :],
                                                        ps[0:C, n, 0:2 * TP].rearrange("p (h t) -> p h t", h=2),
                                                        decay[:, :].unsqueeze(1).to_broadcast([C, 2, TP]), ALU.mult)
                            ins.then_inc(decayed, 1)
                            dve.tensor_tensor(pt[:, hg, 1, :, 0:C], ps[0:C, 2, 0:4 * C].rearrange("p (h t) -> p h t", h=4),
                                              decay[:, 0:C].unsqueeze(1).to_broadcast([C, 4, C]), ALU.mult)\
                                .then_inc(decayed, 1)

                    def ret_out():
                        dve.wait_ge(rt_mm, 1)
                        dve.tensor_tensor(xra[:, :], xra[:, :], ps[:, 0, 0:N], ALU.add).then_inc(ret_sum, 1)
                        dve.wait_ge(ret_sum, 1)
                        if pair_b is not None:
                            dve.wait_ge(taken, 1)
                        dve.scalar_tensor_tensor(out=hout[:, :], in0=xra[:, :], scalar=0.0, in1=hout[:, :],
                                                 op0=ALU.max, op1=ALU.add).then_inc(a_done, 1)

                    def splitx(m):
                        dve.wait_ge(high_x, m + 1)
                        dve.tensor_tensor(x2l[:, :], x2[:, :], x2h[:, :].bitcast(F32), ALU.subtract).then_inc(split_x, 1)

                    def route(m):
                        dve.wait_ge(lg_mm, m + 1)
                        dve.tensor_tensor(lg[:, :, :], ps[0:C, 6, 0:4 * EXPERTS].rearrange("p (c e) -> p c e", c=4),
                                          small["rb"][:, m * EXPERTS:(m + 1) * EXPERTS].unsqueeze(1).to_broadcast([C, 4, EXPERTS]),
                                          ALU.add).then_inc(lg_kept, 1)
                        dve.wait_ge(lg_kept, m + 1)
                        for c in range(4):
                            dve.max(m8[:, c, :], lg[:, c, :]).then_inc(top_done, 1)
                        dve.wait_ge(top_done, 4 * m + 4)
                        dve.tensor_tensor(dl[:, :], m8[:, :, 1], m8[:, :, 0], ALU.subtract).then_inc(gap_done, 1)
                        for c in range(4):
                            dve.max_index(i8[:, c, :], m8[:, c, :], lg[:, c, :]).then_inc(idx_done, 1)
                        dve.wait_ge(idx_done, 4 * m + 4)
                        dve.tensor_copy(i8f[:, :, :], i8[:, :, 0:2]).then_inc(idx_f, 1)
                        dve.wait_ge(gap_tanh, m + 1)
                        dve.tensor_scalar(cw[:, 0, :], dth[:, :], -0.5, 0.5, ALU.mult, ALU.add)
                        dve.tensor_scalar(cw[:, 1, :], dth[:, :], 0.5, 0.5, ALU.mult, ALU.add).then_inc(conf_done, 1)
                        dve.wait_ge(conf_done, m + 1)
                        dve.wait_ge(idx_f, m + 1)
                        for k, dst in enumerate((w1t, w2t)):
                            for c in range(4):
                                dve.tensor_scalar(dst[:, c, :], small["iota"][:, :], i8f[:, c, k:k + 1], cw[:, k, c:c + 1],
                                                  ALU.is_equal, ALU.mult).then_inc(pick_done, 1)
                        dve.wait_ge(pick_done, 8 * m + 8)
                        dve.tensor_tensor(wtok[:, :, :], w1t[:, :, :], w2t[:, :, :], ALU.add).then_inc(w_done, 1)

                    def scaled(m, e, tiles, base):
                        dve.wait_ge(exp_mm, base + tiles * (e + 1))
                        n = EXPERTS * m + e
                        if n >= 2:
                            dve.wait_ge(acc_done, n - 1)
                        dve.scalar_tensor_tensor(out=to[:, e % 2, :], in0=ps[:, 6 + e % 2, 0:N],
                                                 scalar=small["b2bd"][:, n:n + 1], in1=wb[:, e % 2, :],
                                                 op0=ALU.add, op1=ALU.mult).then_inc(exp_scaled, 1)

                    def moe0(e):
                        scaled(0, e, H0T, 0)

                    def moe1(e):
                        base = H0T * EXPERTS
                        for n in range(H1T * e, H1T * e + H1T):
                            dve.wait_ge(hid_act, base + n + 1)
                            k = (base + n) % 3
                            dve.wait_ge(exp_mm, base + n - 2)
                            dve.scalar_tensor_tensor(out=g[:, k, :], in0=ps[:, 5, 0:N], scalar=bu1[:, n:n + 1],
                                                     in1=gs[:, n % 2, :], op0=ALU.add, op1=ALU.mult).then_inc(hid_up, 1)
                        scaled(1, e, H1T, base)

                    def sum0():
                        dve.wait_ge(acc_done, EXPERTS)
                        dve.tensor_tensor(x1[:, :], x1[:, :], acc[:, :], ALU.add).then_inc(x1_sum, 1)

                    def add0():
                        dve.wait_ge(final_b, 3)
                        dve.tensor_tensor(hb[:, :], hb[:, :], x1[:, :], ALU.add).then_inc(hb_add, 1)

                    def att_in():
                        for j in range(2):
                            dve.wait_ge(akq_kept, j + 1)
                            dve.tensor_copy((kr2, qr2)[j][:, :], (ks2, qs2)[j][:, :]).then_inc(akq_round, 1)

                    def att_max():
                        dve.wait_ge(am_mm, 1)
                        dve.tensor_reduce(mp2[:, :, 64].rearrange("p (b k) -> p b k", k=2), heads_of(6)[:, :, :, 0:T], AX.X,
                                          ALU.max, negate=True).then_inc(am_max, 1)
                        dve.wait_ge(am_t, 1)
                        dve.tensor_tensor(qs2[:, :], qs2[:, :], ps[:, 5, 0:N], ALU.add).then_inc(am_aug, 1)

                    def att_pv():
                        dve.wait_ge(ao_mm, 1)
                        o = ps[0:C, 4:6, 0:260].rearrange("p b (q d) -> p b q d", q=2)
                        dve.reciprocal(recb[:, :].rearrange("p (b q) -> p b q", b=2), o[:, :, :, D]).then_inc(ao_rec, 1)
                        dve.wait_ge(ao_rec, 1)
                        dve.tensor_tensor(outs[:, :, :].rearrange("p (b q) d -> p b q d", b=2), o[:, :, :, 0:D],
                                          recb[:, :].rearrange("p (b q) -> p b q", b=2).unsqueeze(3).to_broadcast([C, 2, 2, D]),
                                          ALU.mult).then_inc(ao_norm, 1)

                    def att_out():
                        dve.wait_ge(at_mm, 1)
                        dve.scalar_tensor_tensor(out=hb[:, :], in0=ps[:, 6, 0:N], scalar=col("be2"), in1=hb[:, :],
                                                 op0=ALU.add, op1=ALU.add).then_inc(hb_add, 1)

                    def store():
                        dve.wait_ge(acc_done, 2 * EXPERTS)
                        dve.tensor_tensor(hb[:, :], hb[:, :], acc[:, :], ALU.add).then_inc(y_done, 1)

                    steps = {"embed": embed, "ret_in": ret_in, "ret_qk": ret_qk, "ret0": lambda: ret(0),
                             "ret1": lambda: ret(1), "ret_out": ret_out, "split0": lambda: splitx(0),
                             "split1": lambda: splitx(1), "route0": lambda: route(0), "route1": lambda: route(1),
                             "sum0": sum0, "add0": add0, "att_in": att_in, "att_max": att_max, "att_pv": att_pv,
                             "att_out": att_out, "store": store}
                    for stage in order:
                        walk(stage, steps, {"norm_": lambda s, n: stage_norm_dve(dve, s, n), "qkv": qkv, "maxima": maxima,
                                            "heads": heads, "proj": proj, "ff": ff, "moe0_": moe0, "moe1_": moe1})

                @block.gpsimd
                def _(pool):
                    def add(m, e):
                        n = EXPERTS * m + e
                        pool.wait_ge(exp_scaled, n + 1)
                        if e == 0:
                            pool.tensor_copy(acc[:, :], to[:, 0, :]).then_inc(acc_done, 1)
                        else:
                            pool.wait_ge(acc_done, n)
                            pool.tensor_tensor(acc[:, :], acc[:, :], to[:, e % 2, :], ALU.add).then_inc(acc_done, 1)

                    for stage in order:
                        walk(stage, {}, {"norm_": lambda s, n: stage_norm_pool(pool, s, n), "moe0_": lambda e: add(0, e),
                                         "moe1_": lambda e: add(1, e)})

            nc.sync.sem_clear(range(sems[0].num, sems[-1].num + 1))
            nc.all_engine_barrier()

        assert [s.num for s in sems] == list(range(sems[0].num, sems[0].num + len(sems)))
        body(STAGES_A, 0, None, 1)
        with nc.Fori(0, PAIRS - 2) as i:
            body(merged(), i + 1, i, i + 2)
        body(merged(), PAIRS - 1, PAIRS - 2, None)
        body(STAGES_B, None, PAIRS - 1, None)


def walk(stage, steps, families):
    if stage in steps:
        steps[stage]()
        return
    if stage.startswith("norm_"):
        families["norm_"](stage[5], int(stage[6:]))
        return
    for family, step in families.items():
        rest = stage[len(family):]
        if stage.startswith(family) and rest.replace("_", "").isdigit():
            step(*(int(n) for n in rest.split("_")))
            return


SPLIT = ("W1", "Wgu")
COLUMNS = (("conv_b", 1), ("cls", 1), ("ln1", 2), ("ln2", 2), ("ln_f", 1), ("gn_w", 1), ("gn_b", 1), ("ln_g", 1),
           ("ln_b", 1), ("out_g", 1), ("out_b", 1), ("be2", 1), ("be1k1", 4), ("bkq", 2), ("one16", 1), ("evenodd", 2))
COL = {name: sum(n for _, n in COLUMNS[:k]) for k, (name, _) in enumerate(COLUMNS)}
COL_TOTAL = sum(n for _, n in COLUMNS)


def constants():
    c = {"ident": np.eye(D, dtype=np.float32)}
    c["cen_all"] = (np.eye(D) - 1.0 / D).astype(np.float32)
    same = np.arange(D)[:, None] // HD == np.arange(D)[None, :] // HD
    c["cen_group"] = (np.eye(D) - same / HD).astype(np.float32)
    c["stat_all"] = np.full((D, 2), 1.0 / D, np.float32)
    c["stat_group"] = ((np.arange(D)[:, None] // HD == np.arange(HEADS)[None, :]) / HD).astype(np.float32)
    s, d = np.arange(T, dtype=np.float64), np.arange(D)
    scale = ((d // 2 * 2 + 0.4 * D) / (1.4 * D))[:, None] ** (s / 512.0)[None, :]
    angle = (1.0 / 10000.0 ** ((d // 2) / (D // 2)))[:, None] * s[None, :]
    sign = np.where(d % 2 == 0, -1.0, 1.0)[:, None]
    c["cos"], c["sin"] = np.zeros((D, TP), np.float32), np.zeros((D, TP), np.float32)
    c["cos"][:, :T] = np.cos(angle) * scale
    c["sin"][:, :T] = np.sin(angle) * scale * sign
    gap = np.arange(TP)[None, :] - np.arange(C)[:, None]
    c["decay"] = np.where(gap >= 0, 0.5 * 0.9 ** np.maximum(gap, 0), 0.0).astype(np.float32)
    c["iota"] = np.tile(np.arange(EXPERTS, dtype=np.float32), (C, 1))
    return c


def layout(a):
    f = {k: np.asarray(v) for k, v in a.items()}
    out = constants()

    def rows(m):
        return m.reshape(-1, D, m.shape[-1]).transpose(1, 0, 2).reshape(D, -1)

    wp = f["L0_tok_conv_w"].transpose(1, 2, 3, 0).reshape(3 * PATCH, PATCH * D)
    out["wp"] = np.zeros((128, PATCH * D), np.float32)
    out["wp"][0:48], out["wp"][64:112] = wp, wp
    out["pos"] = np.zeros((D, TP), np.float32)
    out["pos"][:, :T] = f["L0_tok_pos_emb"][0].T
    for i in range(2):
        qkv = f[f"L0_tok_qkv_{i}"].T
        padded = np.zeros((D, 2 * HEADS, 32), np.float32)
        padded[:, :, :HD] = qkv[:, :2 * D].reshape(D, 2 * HEADS, HD)
        out[f"wqk{i}"] = padded.reshape(D, 4 * D)
        out[f"wv{i}"] = qkv[:, 2 * D:]
        out[f"wo{i}"] = f[f"L0_tok_wo_{i}"].T
        out[f"wg{i}"], out[f"wu{i}"] = f[f"L0_tok_gate_{i}"].T, f[f"L0_tok_up_{i}"].T
        down = np.zeros((3 * D, D), np.float32)
        down[:FF] = f[f"L0_tok_down_{i}"].T
        out[f"wd{i}"] = rows(down)
    swap = np.arange(D) ^ 1
    out["rqk"] = np.concatenate([m for n in ("Wq", "Wk") for m in (f["L0_attn_" + n], f["L0_attn_" + n][:, swap])], 1)
    out["rv"] = f["L0_attn_Wv"]
    out["route0"], out["route1"] = f["L0_ffn_Wg"], f["L1_ffn_router_w"]
    rb = np.zeros((C, 2 * EXPERTS), np.float32)
    rb[:, EXPERTS:] = f["L1_ffn_router_b"][None, :]
    out["rb"] = rb
    out["W1"] = f["L0_ffn_W1"].transpose(1, 0, 2).reshape(D, -1)
    out["W2"] = rows(f["L0_ffn_W2"].reshape(-1, D))
    out["Wgu"] = f["L1_ffn_gate_up_proj"].transpose(1, 0, 2).reshape(D, -1)
    out["Wd"] = rows(f["L1_ffn_down_proj"].reshape(-1, D))
    out["b1"] = f["L0_ffn_b1"].reshape(-1, D).T
    bgu = f["L1_ffn_gate_up_proj_bias"].reshape(EXPERTS, 2, H1T, D)
    out["bg"], out["bu"] = bgu[:, 0].reshape(-1, D).T, bgu[:, 1].reshape(-1, D).T
    out["b2bd"] = np.concatenate([f["L0_ffn_b2"].T, f["L1_ffn_down_proj_bias"].T], 1)
    out["we1k1"] = np.concatenate([f["L1_attn_We1"], f["L1_attn_Wk1"]], 1)
    out["we2"] = rows(f["L1_attn_We2"])
    wk2 = np.zeros((2 * D, 2, D), np.float32)
    wk2[:, 0, :64], wk2[:, 1, :64] = f["L1_attn_Wk2"][:, :64], f["L1_attn_Wk2"][:, 64:]
    out["wk2"] = rows(wk2.reshape(2 * D, 2 * D))
    cols = np.zeros((D, COL_TOTAL), np.float32)

    def put(name, *vectors):
        for k, v in enumerate(vectors):
            cols[:, COL[name] + k] = v

    put("conv_b", f["L0_tok_conv_b"])
    put("cls", f["L0_tok_cls_token"].reshape(D))
    put("ln1", f["L0_tok_ln1_0"], f["L0_tok_ln1_1"])
    put("ln2", f["L0_tok_ln2_0"], f["L0_tok_ln2_1"])
    put("ln_f", f["L0_tok_ln_f"])
    put("gn_w", f["L0_attn_gn_weight"])
    put("gn_b", f["L0_attn_gn_bias"])
    put("ln_g", f["L0_ffn_ln_g"])
    put("ln_b", f["L0_ffn_ln_b"])
    put("out_g", f["L0_ffn_out_g"])
    put("out_b", f["L0_ffn_out_b"])
    put("be2", f["L1_attn_be2"])
    put("be1k1", *f["L1_attn_be1"].reshape(2, D), *f["L1_attn_bk1"].reshape(2, D))
    bk, bq, one = np.zeros(D, np.float32), np.zeros(D, np.float32), np.zeros(D, np.float32)
    bk[:64], bq[:64] = f["L1_attn_bk2"][:64], f["L1_attn_bk2"][64:]
    bk[64] = 1.0
    put("bkq", bk, bq)
    one[HD::32] = 1.0
    put("one16", one)
    even = (np.arange(D) // HD % 2 == 0).astype(np.float32)
    put("evenodd", even, 1.0 - even)
    out["cols"] = cols
    return {k: np.ascontiguousarray(v) for k, v in out.items()}


def kernel(**inputs):
    import concourse.bacc as bacc
    from concourse.bass_utils import run_bass_kernel_spmd
    arrays = {"x": np.ascontiguousarray(inputs.pop("x")), **layout(inputs)}
    nc = bacc.Bacc("TRN2", target_bir_lowering=False, num_devices=1)
    aps = {k: nc.dram_tensor(k + "_dram", v.shape, F32, kind="ExternalInput").ap() for k, v in arrays.items()}
    out = nc.dram_tensor("out_dram", (BATCH, T, D), F32, kind="ExternalOutput").ap()
    tower(nc, aps.pop("x"), aps, out)
    r = run_bass_kernel_spmd(nc, [{k + "_dram": v for k, v in arrays.items()}], core_ids=[0])
    return r.results[0]["out_dram"]
```

```python
from contextlib import ExitStack

import numpy as np
import concourse.bass as bass
from concourse import mybir

ALU = mybir.AluOpType
ACT = mybir.ActivationFunctionType
AX = mybir.AxisListType
F32 = mybir.dt.float32
F32R = mybir.dt.float32r
U32 = mybir.dt.uint32

D = 128
BATCH = 64
PAIRS = BATCH // 2
PATCH = 16
SIDE = 14
PATCHES = SIDE * SIDE
T = PATCHES + 1
TP = T + 1
N = 2 * TP
C = TP // 2
HEADS, HD = 8, 16
FF = 344
FF_TILES = [(0, 128), (128, 128), (256, 88)]
EXPERTS = 8
H0T = 4
H1T = 2
KROWS = (C, C - 1)
HALF = SIDE // 2
TILES = HEADS // 2
STACK = 3 * HD
ROWS = STACK + 2
VW = HD + 2
RQ = ((0, TP), (C - 1, C + 1))
UNITS = 8
BATCH_PIECES = 16

NORMS_A = [(None, 1, 1e-6)] * 5 + [("all", 1, 1e-5), ("group", 8, 1e-5)]
NORMS_B = [("all", 1, 1e-5)] * 5



def norm(stream, n):
    return [("norm", stream, n, part) for part in range(3)]


def vit_in(i):
    return norm("a", 2 * i) + [("qkv", i, part) for part in range(5)]


def vit_scores(i):
    return [("maxima", i, part) for part in range(5)]


def vit_heads(i):
    return [("heads", i, u) for u in range(UNITS + 1)]


def vit_out(i):
    return ([("heads", i, UNITS + 1), ("proj", i)] + norm("a", 2 * i + 1)
            + [("ff", i, part) for part in range(4)])


RETENTION = (norm("a", 4) + norm("a", 5) + [("ret_in", part) for part in range(3)] + norm("a", 6)
             + [("ret_qk",)] + [("ret", r) for r in range(BATCH_PIECES // 2 + 1)] + [("ret_out",)])
BEFORE_0 = norm("b", 0) + norm("b", 1) + [("split", 0), ("route", 0, 0), ("route", 0, 1)]
MIXTURE_0 = [("moe0", n) for n in range(-1, H0T * EXPERTS + 1)]
BETWEEN = ([("sum0",)] + norm("b", 2) + [("add0",)] + norm("b", 3)
           + [("att_in", part) for part in range(3)] + [("att_max", 0), ("att_max", 1), ("att_pv", 0), ("att_pv", 1),
              ("att_out",)] + norm("b", 4) + [("split", 1), ("route", 1, 0), ("route", 1, 1)])
MIXTURE_1 = [("moe1", n) for n in range(-1, H1T * EXPERTS + 2)]

SECTIONS = [
    ([("embed", q) for q in range(4)], BEFORE_0),
    (vit_in(0) + vit_scores(0), MIXTURE_0[:15]),
    (vit_heads(0), []),
    (vit_out(0) + vit_in(1), MIXTURE_0[15:]),
    (vit_scores(1) + vit_heads(1), BETWEEN),
    (vit_out(1) + RETENTION, MIXTURE_1 + [("store",)]),
]


def merged():
    order = [("take",)]
    for a, b in SECTIONS:
        at = sorted([((k + 1) / (len(a) + 1), 0, step) for k, step in enumerate(a)]
                    + [((k + 1) / (len(b) + 1), 1, step) for k, step in enumerate(b)], key=lambda x: x[:2])
        order += [step for _, _, step in at]
    return order


def only(stream):
    return ([("take",)] if stream else []) + [step for section in SECTIONS for step in section[stream]]


def tower(nc, x, w, out):
    def chunk(c):
        return slice(c * C, (c + 1) * C)

    with ExitStack() as ctx:
        def sb(name, shape, dt=F32):
            return ctx.enter_context(nc.sbuf_tensor(name, shape, dt))

        sems = []

        def sem(name):
            sems.append(ctx.enter_context(nc.semaphore(name)))
            return sems[-1]

        small = {name: sb("w_" + name, list(ap.shape)) for name, ap in w.items() if name not in SPLIT}
        split = {name: (sb("h_" + name, list(w[name].shape), F32R), sb("l_" + name, list(w[name].shape), F32R))
                 for name in SPLIT}
        ident = small["ident"]
        neg_half = sb("neg_half", [C, 4 * HEADS])
        bu1 = sb("bu1", [D, EXPERTS * H1T])

        img = sb("img", [128, 2, HALF, SIDE * PATCH])
        xa = sb("xa", [D, N])
        ha = sb("ha", [D, N])
        epsa, rsa = sb("epsa", [C, 4 * HEADS]), sb("rsa", [C, 4 * HEADS])
        qst, kst = sb("qst", [D, TILES, N], F32R), sb("kst", [D, TILES, N], F32R)
        vp = sb("vp", [C, 4 * HEADS * VW + 32 - VW])
        vph = vp[:, 0:4 * HEADS * VW].rearrange("p (c h d) -> p c h d", c=4, h=HEADS)
        mp = sb("mp", [C, 4, 2, D])
        shared_a = sb("shared_a", [D, 8 * N])
        pt = shared_a[0:C, 0:4 * N].rearrange("p (s h t) -> p s h t", s=2, h=4)
        th = shared_a[:, 4 * N:6 * N].rearrange("p (a n) -> p a n", a=2)
        high = th.bitcast(F32R)
        oe = th
        on = shared_a[:, 6 * N:8 * N].rearrange("p (a n) -> p a n", a=2)
        gu = shared_a[:, 0:3 * N].rearrange("p (a n) -> p a n", a=3)
        sqa, xca = shared_a[:, 6 * N:7 * N], shared_a[:, 7 * N:8 * N]
        rt = shared_a[0:C, 0:3 * N].rearrange("p (s h t) -> p s h t", s=3, h=2)
        rv2 = sb("rv2", [C, 2, 4, D])
        xra, t1, t2 = ha, shared_a[:, 3 * N:4 * N], shared_a[:, 5 * N:6 * N]
        qeo = shared_a[:, 6 * N:8 * N].rearrange("p (a n) -> p a n", a=2)
        hout = sb("hout", [D, N])

        hb = sb("hb", [D, N])
        x1 = sb("x1", [D, N])
        x2 = sb("x2", [D, N])
        x2h, x2l = sb("x2h", [D, N], F32R), sb("x2l", [D, N], F32R)
        epsb, rsb = sb("epsb", [C, 4 * HEADS]), sb("rsb", [C, 4 * HEADS])
        lg = sb("lg", [C, 4, EXPERTS])
        m8, i8 = sb("m8", [C, 4, 8]), sb("i8", [C, 4, 8], U32)
        i8f = sb("i8f", [C, 4, 2])
        dl, dth = sb("dl", [C, 4]), sb("dth", [C, 4])
        cw = sb("cw", [C, 2, 4])
        w1t, w2t = sb("w1t", [C, 4, EXPERTS]), sb("w2t", [C, 4, EXPERTS])
        wtok = sb("wtok", [C, 4, EXPERTS])
        wb = sb("wb", [D, 2, N])
        g = sb("g", [D, 3, N])
        gs = sb("gs", [D, 2, N])
        sqb, xcb = gs[:, 0, :], gs[:, 1, :]
        to = sb("to", [D, 2, N])
        acc = sb("acc", [D, N])
        e1, k1 = gs, to
        ks2, qs2, kr2, qr2 = g[:, 0, :], g[:, 1, :], x2h, x2l
        mp2 = sb("mp2", [C, 4, D])
        vt = sb("vt", [C, 4, D + 2])
        ptb = wb[0:C, :, :].rearrange("p a (k t) -> p (a k) t", k=2)
        recb = sb("recb", [C, 4])
        outs = sb("outs", [C, 4, D])
        ps = ctx.enter_context(nc.psum_tensor("ps", [128, 8, 512], F32))

        def load_half(sp, image, q, slot, done):
            for s in range(2):
                for ch in range(3):
                    sp.dma_start(img[64 * s + 16 * ch:64 * s + 16 * ch + 16, slot, :, 0:SIDE * PATCH - 8 * s],
                                 x[image + q // 2, ch, (q % 2) * HALF * PATCH:(q % 2 + 1) * HALF * PATCH, 8 * s:]
                                 .rearrange("(i py) w -> py i w", py=PATCH)).then_inc(done, 16)

        with ExitStack() as setup:
            loaded = setup.enter_context(nc.semaphore("loaded"))
            stage_ready = setup.enter_context(nc.semaphore("stage_ready"))
            high_done = setup.enter_context(nc.semaphore("high_done"))
            low_done = setup.enter_context(nc.semaphore("low_done"))
            preset = setup.enter_context(nc.semaphore("preset"))
            STEP = 1024
            stage = shared_a[:, 0:2 * STEP].rearrange("p (a n) -> p a n", a=2)
            pieces = [(n, a) for n in SPLIT for a in range(0, w[n].shape[1], STEP)]
            img_clear = setup.enter_context(nc.semaphore("img_clear"))
            with nc.Block() as block:
                @block.sync
                def _(sp):
                    sp.wait_ge(img_clear, 1)
                    for r in range(2):
                        load_half(sp, 0, r, r, loaded)
                    for name, ap in w.items():
                        if name not in SPLIT:
                            sp.dma_start(small[name][:], ap).then_inc(loaded, 16)
                    sp.wait_ge(loaded, 16 * (12 + len(small)))

                @block.scalar
                def _(act):
                    for n, (name, a) in enumerate(pieces):
                        if n >= 2:
                            act.wait_ge(low_done, n - 1)
                        act.dma_start(stage[:, n % 2, :], w[name][:, a:a + STEP]).then_inc(stage_ready, 16)
                        act.wait_ge(stage_ready, 16 * (n + 1))

                @block.vector
                def _(dve):
                    dve.memset(img[:], 0.0).then_inc(img_clear, 1)
                    for n, (name, a) in enumerate(pieces):
                        top, low = (s[:, a:a + STEP] for s in split[name])
                        dve.wait_ge(stage_ready, 16 * (n + 1))
                        dve.tensor_copy(top, stage[:, n % 2, :]).then_inc(high_done, 1)
                        dve.wait_ge(high_done, n + 1)
                        dve.tensor_tensor(low, stage[:, n % 2, :], top.bitcast(F32), ALU.subtract).then_inc(low_done, 1)
                    dve.wait_ge(loaded, 16 * (12 + len(small)))
                    pos = small["pos"]
                    dve.tensor_scalar(pos[:, 1:T], pos[:, 1:T], small["cols"][:, COL["conv_b"]:COL["conv_b"] + 1], None,
                                      ALU.add)
                    dve.tensor_scalar(pos[:, 0:1], pos[:, 0:1], small["cols"][:, COL["cls"]:COL["cls"] + 1], None, ALU.add)
                    dve.tensor_scalar(bu1[:, :], small["bu"][:, :], 1.0, None, ALU.add).then_inc(preset, 1)

                @block.gpsimd
                def _(pool):
                    pool.memset(mp[:], 0.0)
                    pool.memset(rv2[:], 0.0)
                    pool.memset(mp2[:], 0.0)
                    pool.memset(vp[:], 1.0)
                    pool.memset(vt[:], 1.0)
                    pool.memset(neg_half[:], -0.5).then_inc(preset, 1)

        img_loaded, out_stored = (sem("img_loaded_0"), sem("img_loaded_1")), sem("out_stored")
        embed_mm, embed_x = sem("embed_mm"), sem("embed_x")
        norm_sems = {s: {k: sem(f"norm_{s}_{k}") for k in ("centered", "square", "kept", "stat", "eps", "rsqrt", "spread",
                                                           "out", "final")} for s in "ab"}
        group_spread = sem("group_spread")
        qk_mm, qk_high, stacked, v_mm, v_kept = (sem(n) for n in ("qk_mm", "qk_high", "stacked", "v_mm", "v_kept"))
        sq_mm, max_done, max_t, q_aug = (sem(n) for n in ("sq_mm", "max_done", "max_t", "q_aug"))
        st_mm, exp_done, pv_mm, o_kept, sum_mm, rec_done, on_done = (
            sem(n) for n in ("st_mm", "exp_done", "pv_mm", "o_kept", "sum_mm", "rec_done", "on_done"))
        proj_mm, x_proj = sem("proj_mm"), sem("x_proj")
        ff_mm, ff_tanh, ff_gate, ff_act, down_mm, x_ff = (sem(n) for n in ("ff_mm", "ff_tanh", "ff_gate", "ff_act", "down_mm", "x_ff"))
        rot_mm, rot_part, rot_sum, rv_mm, rv_kept = (sem(n) for n in ("rot_mm", "rot_part", "rot_sum", "rv_mm", "rv_kept"))
        rq_tanh, rq_gate, rq_done = (sem(n) for n in ("rq_tanh", "rq_gate", "rq_done"))
        rs_mm, decayed, ro_mm, ret_sum, a_done = (sem(n) for n in ("rs_mm", "decayed", "ro_mm", "ret_sum", "a_done"))
        taken, high_x, split_x = sem("taken"), sem("high_x"), sem("split_x")
        lg_mm, lg_kept, top_done, idx_done, idx_f, gap_done, gap_tanh, conf_done, pick_done, w_done, wb_mm, wb_kept = (
            sem(n) for n in ("lg_mm", "lg_kept", "top_done", "idx_done", "idx_f", "gap_done", "gap_tanh", "conf_done",
                             "pick_done", "w_done", "wb_mm", "wb_kept"))
        hid_mm, hid_act, hid_up, exp_mm, exp_scaled, acc_done = (
            sem(n) for n in ("hid_mm", "hid_act", "hid_up", "exp_mm", "exp_scaled", "acc_done"))
        x1_sum, hb_add = sem("x1_sum"), sem("hb_add")
        ai_mm, ai_relu, akq_mm, akq_kept, akq_round, av_mm, av_kept = (
            sem(n) for n in ("ai_mm", "ai_relu", "akq_mm", "akq_kept", "akq_round", "av_mm", "av_kept"))
        am_mm, am_max, am_t, am_aug, as_mm, as_exp, ao_mm, ao_rec, ao_norm, at_mm = (
            sem(n) for n in ("am_mm", "am_max", "am_t", "am_aug", "as_mm", "as_exp", "ao_mm", "ao_rec", "ao_norm", "at_mm"))
        y_done, y_mm, y_kept = sem("y_done"), sem("y_mm"), sem("y_kept")

        cols = small["cols"]

        def col(name, k=0):
            return cols[:, COL[name] + k:COL[name] + k + 1]

        def heads_of(bank, rows=C):
            return ps[0:rows, bank:bank + 2, 0:2 * TP].rearrange("p n (h t) -> p n h t", h=2)

        def norm_io(s, n):
            if s == "a":
                return [(xa, ha, col("ln1", 0), None, (embed_x, 4)), (xa, ha, col("ln2", 0), None, (x_proj, 1)),
                        (xa, ha, col("ln1", 1), None, (x_ff, 1)), (xa, ha, col("ln2", 1), None, (x_proj, 2)),
                        (xa, hout, col("ln_f"), None, (x_ff, 2)), (hout, xra, None, None, (norm_sems["a"]["final"], 5)),
                        (t1, t1, col("gn_w"), col("gn_b"), (rot_sum, 2))][n]
            return [(hb, x1, None, None, (taken, 1)), (x1, x2, col("ln_g"), col("ln_b"), (norm_sems["b"]["final"], 1)),
                    (x1, x1, col("out_g"), col("out_b"), (x1_sum, 1)), (hb, x2, None, None, (hb_add, 1)),
                    (hb, x2, None, None, (hb_add, 2))][n]

        NORMS = {"a": NORMS_A, "b": NORMS_B}
        BUF = {"a": (sqa, xca, epsa, rsa, 0, 1, 2), "b": (sqb, xcb, epsb, rsb, 4, 5, 6)}

        def centered_before(s, n):
            return sum(c is not None for c, _, _ in NORMS[s][:n])

        def norm_pe(pe, s, n, part):
            sq, xc, eps_t, rs, bank_c, bank_s, bank_b = BUF[s]
            S = norm_sems[s]
            cen, groups, eps = NORMS[s][n]
            src, _, _, _, (ready, count) = norm_io(s, n)
            if part == 0:
                if cen is not None:
                    pe.wait_ge(ready, count)
                    pe.matmul(ps[:, bank_c, 0:N], small["cen_" + cen][:], src[:, :], start=True, stop=True)\
                        .then_inc(S["centered"], 1)
                return
            if part == 2:
                if groups == 1:
                    pe.wait_ge(S["rsqrt"], n + 1)
                else:
                    pe.wait_ge(group_spread, 1)
                for c in range(4):
                    one = rs[:, c:c + 1].to_broadcast([C, D]) if groups == 1 else shared_a[0:C, c * D:(c + 1) * D]
                    mm = pe.matmul(ps[:, bank_b, chunk(c)], one, ident[0:C, 0:C], start=True, stop=True)
                mm.then_inc(S["spread"], 1)
                return
            pe.wait_ge(S["square"], n + 1)
            rhs = small["stat_all"][:, 0:1] if groups == 1 else small["stat_group"][:, :]
            for c in range(4):
                mm = pe.matmul(ps[0:C, bank_s, c * groups:(c + 1) * groups], sq[:, chunk(c)], rhs, start=True, stop=True)
            mm.then_inc(S["stat"], 1)

        def norm_act(act, s, n, part):
            sq, xc, eps_t, rs, bank_c, bank_s, bank_b = BUF[s]
            S = norm_sems[s]
            src, _, _, _, (ready, count) = norm_io(s, n)
            if part:
                return
            if NORMS[s][n][0] is None:
                act.wait_ge(ready, count)
                act.activation(sq[:, :], src[:, :], ACT.Square).then_inc(S["square"], 1)
            else:
                act.wait_ge(S["centered"], centered_before(s, n) + 1)
                act.activation(sq[:, :], ps[:, bank_c, 0:N], ACT.Square).then_inc(S["square"], 1)
                act.activation(xc[:, :], ps[:, bank_c, 0:N], ACT.Identity).then_inc(S["kept"], 1)

        def norm_dve(dve, s, n, part):
            sq, xc, eps_t, rs, bank_c, bank_s, bank_b = BUF[s]
            S = norm_sems[s]
            cen, groups, eps = NORMS[s][n]
            src, dst, weight, bias, _ = norm_io(s, n)
            if part == 0:
                return
            if part == 1:
                dve.wait_ge(S["stat"], n + 1)
                dve.tensor_scalar(eps_t[:, 0:4 * groups], ps[0:C, bank_s, 0:4 * groups], eps, None, ALU.add)\
                    .then_inc(S["eps"], 1)
                return
            dve.wait_ge(S["spread"], n + 1)
            if cen is not None:
                dve.wait_ge(S["kept"], centered_before(s, n) + 1)
                src = xc
            out_sem = S["out"] if bias is not None else S["final"]
            if weight is None:
                dve.tensor_tensor(dst[:, :], src[:, :], ps[:, bank_b, 0:N], ALU.mult).then_inc(out_sem, 1)
            else:
                dve.scalar_tensor_tensor(out=dst[:, :], in0=src[:, :], scalar=weight, in1=ps[:, bank_b, 0:N],
                                         op0=ALU.mult, op1=ALU.mult).then_inc(out_sem, 1)
            if bias is not None:
                before = {("a", 6): 0, ("b", 1): 0, ("b", 2): 1}[s, n]
                dve.wait_ge(S["out"], before + 1)
                dve.tensor_scalar(dst[:, :], dst[:, :], bias, None, ALU.add).then_inc(S["final"], 1)

        def norm_pool(pool, s, n, part):
            sq, xc, eps_t, rs, bank_c, bank_s, bank_b = BUF[s]
            S = norm_sems[s]
            groups = NORMS[s][n][1]
            if part != 1:
                return
            pool.wait_ge(S["eps"], n + 1)
            pool.tensor_tensor(rs[:, 0:4 * groups], eps_t[:, 0:4 * groups], neg_half[:, 0:4 * groups], ALU.pow)\
                .then_inc(S["rsqrt"], 1)
            if groups > 1:
                pool.wait_ge(S["rsqrt"], n + 1)
                pool.tensor_copy(shared_a[0:C, 0:4 * D].rearrange("p (g d) -> p g d", d=D // groups),
                                 rs[:, 0:4 * groups].unsqueeze(2).to_broadcast([C, 4 * groups, D // groups]))\
                    .then_inc(group_spread, 1)

        final_a, final_b = norm_sems["a"]["final"], norm_sems["b"]["final"]

        def body(order, pair_a, pair_b, prefetch):
            with nc.Block(no_gpsimd_drain=True) as block:
                @block.sync
                def _(sp):
                    for q in range(4):
                        if q < 2 and pair_a is not None:
                            sp.wait_ge(embed_mm, q + 1)
                            load_half(sp, 2 * pair_a, q + 2, q % 2, img_loaded[q % 2])
                        if q >= 2 and prefetch is not None:
                            sp.wait_ge(embed_mm, q + 1)
                            load_half(sp, 2 * prefetch, q - 2, q % 2, img_loaded[q % 2])
                    if pair_a is not None:
                        for slot in range(2):
                            sp.wait_ge(img_loaded[slot], 96 * (1 if prefetch is None else 2))
                    if pair_b is not None:
                        sp.wait_ge(y_kept, 1)
                        for k in range(2):
                            sp.dma_start(out[bass.ts(pair_b, 2), k * C:k * C + KROWS[k], :].rearrange("b t d -> t b d"),
                                         outs[:, :, :].rearrange("p (b k) d -> p b k d", k=2)[0:KROWS[k], :, k, :])\
                                .then_inc(out_stored, 16)
                        sp.wait_ge(out_stored, 32)

                @block.tensor
                def _(pe):
                    def embed(q):
                        if q >= 2:
                            pe.wait_ge(img_loaded[q % 2], 96)
                        for px in range(PATCH // 2):
                            mm = pe.matmul(ps[:, q, 0:HALF * SIDE].rearrange("p (i j) -> p i j", i=HALF),
                                           small["wp"][:, px * D:(px + 1) * D], img[:, q % 2, :, px::PATCH],
                                           start=(px == 0), stop=(px == PATCH // 2 - 1))
                        mm.then_inc(embed_mm, 1)

                    def qkv(i, part):
                        if part < 4:
                            pe.wait_ge(final_a, 2 * i + 1)
                            for j in (2 * part, 2 * part + 1):
                                if j >= 4:
                                    pe.wait_ge(stacked, 8 * i + j - 3)
                                pe.matmul(ps[:, j % 4, 0:N], small[f"wqk{i}"][:, j * D:(j + 1) * D], ha[:, :],
                                          start=True, stop=True).then_inc(qk_mm, 1)
                            return
                        pe.wait_ge(stacked, 8 * i + 5)
                        for c in range(4):
                            mm = pe.matmul(ps[0:C, 0, c * D:(c + 1) * D], ha[:, chunk(c)], small[f"wv{i}"][:, :],
                                           start=True, stop=True)
                        mm.then_inc(v_mm, 1)

                    def stacks(bank, dst, left, left_cols, right, right_cols, four):
                        for t in range(2):
                            for j in range(2):
                                r = slice(64 * j, 64 * j + ROWS)
                                mm = pe.matmul(ps[0:C, bank + j, t * TP:(t + 1) * TP], left[r, 2 * four + t, left_cols],
                                               right[r, 2 * four + t, right_cols], start=True, stop=True)
                        mm.then_inc(dst, 1)

                    def maxima(i, part):
                        if part == 4:
                            pe.wait_ge(max_done, 8 * i + 8)
                            for four in range(2):
                                for c in range(4):
                                    mm = pe.transpose(ps[:, four, chunk(c)], mp[:, c, four, :], ident[0:C, 0:C])
                                mm.then_inc(max_t, 1)
                            return
                        if part == 0:
                            pe.wait_ge(stacked, 8 * i + 8)
                            pe.wait_ge(v_kept, 2 * i + 2)
                        for u in (2 * part, 2 * part + 1):
                            four, c = divmod(u, 4)
                            if u >= 2:
                                pe.wait_ge(max_done, 8 * i + u - 1)
                            stacks(2 * (u % 2), sq_mm, qst, chunk(c), kst, slice(c // 2 * TP, (c // 2 + 1) * TP), four)

                    def heads(i, u):
                        if u == 0:
                            pe.wait_ge(q_aug, 4 * i + 4)
                        elif u <= UNITS:
                            pe.wait_ge(exp_done, 8 * i + u)
                        if u < UNITS:
                            four, b, kk = u // 4, u // 2 % 2, u % 2
                            stacks(0, st_mm, kst, chunk(2 * b + kk), qst, slice(b * TP, (b + 1) * TP), four)
                        if 1 <= u <= UNITS:
                            four, b, kk = (u - 1) // 4, (u - 1) // 2 % 2, (u - 1) % 2
                            rows = KROWS[kk]
                            for h in range(4):
                                at = ((2 * b + kk) * HEADS + 4 * four + h) * VW
                                mm = pe.matmul(ps[32 * h:32 * h + 32, 2 + four, b * TP:(b + 1) * TP],
                                               vp[0:rows, at:at + 32], pt[0:rows, (u - 1) % 2, h, :],
                                               start=(kk == 0), stop=(kk == 1), tile_position=(0, 32 * h))
                            if u % 4 == 0:
                                mm.then_inc(pv_mm, 1)
                        if u in (5, UNITS + 1):
                            four = u // UNITS
                            pe.wait_ge(o_kept, 2 * i + four + 1)
                            pe.matmul(ps[:, 2 + four, 0:N], small["sums"][:, :], oe[:, four, :], start=True, stop=True)\
                                .then_inc(sum_mm, 1)

                    def proj(i):
                        for four in range(2):
                            pe.wait_ge(on_done, 2 * i + four + 1)
                            mm = pe.matmul(ps[:, 0, 0:N], small[f"wo{i}"][:, four * D:(four + 1) * D], on[:, four, :],
                                           start=(four == 0), stop=(four == 1))
                        mm.then_inc(proj_mm, 1)

                    def ff(i, t):
                        if t < 3:
                            a, m = FF_TILES[t]
                            if t == 0:
                                pe.wait_ge(final_a, 2 * i + 2)
                            if t == 2:
                                pe.wait_ge(ff_act, 3 * i + 1)
                            bank = 2 * (t % 2)
                            pe.matmul(ps[0:m, bank, 0:N], small[f"wg{i}"][:, a:a + m], ha[:, :], start=True, stop=True)
                            pe.matmul(ps[0:m, bank + 1, 0:N], small[f"wu{i}"][:, a:a + m], ha[:, :], start=True, stop=True)\
                                .then_inc(ff_mm, 1)
                            return
                        for t, (a, m) in enumerate(FF_TILES):
                            pe.wait_ge(ff_act, 3 * i + (2, 2, 3)[t])
                            mm = pe.matmul(ps[:, 2, 0:N], small[f"wd{i}"][0:m, t * D:(t + 1) * D], gu[0:m, t, :],
                                           start=(t == 0), stop=(t == 2))
                        mm.then_inc(down_mm, 1)

                    def ret_in(j):
                        if j < 2:
                            pe.wait_ge(final_a, 6)
                            for r in range(2):
                                if j:
                                    pe.wait_ge(rot_part, 1 + r)
                                pe.matmul(ps[:, r, 0:N], small["rqk"][:, (2 * j + r) * D:(2 * j + r + 1) * D], xra[:, :],
                                          start=True, stop=True).then_inc(rot_mm, 1)
                            return
                        for c in range(4):
                            mm = pe.matmul(ps[0:C, 3, c * D:(c + 1) * D], xra[:, chunk(c)], small["rv"][:, :],
                                           start=True, stop=True)
                        mm.then_inc(rv_mm, 1)

                    def ret(r):
                        if r == 0:
                            pe.wait_ge(final_a, 7)
                            pe.wait_ge(rq_done, 2)
                            pe.wait_ge(rv_kept, 2)
                        for k in (2 * r, 2 * r + 1):
                            if k < BATCH_PIECES:
                                b, m, kk = k // 8, k // 2 % 4, k % 2
                                if k >= 3:
                                    pe.wait_ge(decayed, k - 2)
                                rows = slice(32 * m, 32 * m + 32)
                                first, width = RQ[kk]
                                for h in range(2):
                                    mm = pe.matmul(ps[0:C, k % 3, h * TP:h * TP + width], t1[rows, chunk(2 * b + kk)],
                                                   qeo[rows, h, b * TP + first:(b + 1) * TP], start=True, stop=True)
                                mm.then_inc(rs_mm, 1)
                            k -= 2
                            if k >= 0:
                                b, m, kk = k // 8, k // 2 % 4, k % 2
                                first, width = RQ[kk]
                                pe.wait_ge(decayed, k + 1)
                                for h in range(2):
                                    mm = pe.matmul(ps[32 * m:32 * m + 32, 3, b * TP + first:(b + 1) * TP],
                                                   rv2[0:KROWS[kk], h, 2 * b + kk, 32 * m:32 * m + 32],
                                                   rt[0:KROWS[kk], k % 3, h, 0:width],
                                                   start=(kk == 0 and h == 0), stop=(kk == 1 and h == 1),
                                                   tile_position=(0, 32 * m))
                                if k == BATCH_PIECES - 1:
                                    mm.then_inc(ro_mm, 1)

                    def route(m, part):
                        if part:
                            weights(m, 0)
                            return
                        pe.wait_ge(final_b, (2, 5)[m])
                        for c in range(4):
                            mm = pe.matmul(ps[0:C, 6, c * EXPERTS:(c + 1) * EXPERTS], x2[:, chunk(c)],
                                           small[f"route{m}"][:, :], start=True, stop=True)
                        mm.then_inc(lg_mm, 1)

                    def weights(m, e):
                        pe.wait_ge(w_done, m + 1)
                        if e >= 2:
                            pe.wait_ge(exp_scaled, EXPERTS * m + e - 1)
                        for c in range(4):
                            mm = pe.matmul(ps[:, 6 + e % 2, chunk(c)], wtok[:, c, e:e + 1].to_broadcast([C, D]),
                                           ident[0:C, 0:C], start=True, stop=True)
                        mm.then_inc(wb_mm, 1)

                    def hidden(name, tile, bank):
                        hi, lo = split[name]
                        s = slice(tile * D, (tile + 1) * D)
                        pe.matmul(ps[:, bank, 0:N], hi[:, s], x2h[:, :], start=True, stop=False)
                        pe.matmul(ps[:, bank, 0:N], lo[:, s], x2h[:, :], start=False, stop=False)
                        return pe.matmul(ps[:, bank, 0:N], hi[:, s], x2l[:, :], start=False, stop=True)

                    def up0(n):
                        if n >= 2:
                            pe.wait_ge(hid_act, n - 1)
                        hidden("W1", n, 4 + n % 2).then_inc(hid_mm, 1)

                    def down(m, n, tiles, base):
                        e, t = divmod(n, tiles)
                        if t == 0:
                            pe.wait_ge(wb_kept, EXPERTS * m + e + 1)
                        pe.wait_ge(*((hid_act, n + 1) if m == 0 else (hid_up, n + 1)))
                        pe.matmul(ps[:, 6 + e % 2, 0:N], small[("W2", "Wd")[m]][:, n * D:(n + 1) * D],
                                  g[:, (base + n) % 3, :], start=(t == 0), stop=(t == tiles - 1)).then_inc(exp_mm, 1)

                    def moe0(n):
                        e, t = divmod(n, H0T)
                        if n == -1:
                            pe.wait_ge(split_x, 1)
                            up0(0)
                            up0(1)
                            return
                        if n + 2 < H0T * EXPERTS:
                            up0(n + 2)
                        if n < H0T * EXPERTS:
                            if t == 2 and e + 1 < EXPERTS:
                                weights(0, e + 1)
                            down(0, n, H0T, 0)

                    def up1(n):
                        e, t = divmod(n, H1T)
                        if n >= 1:
                            pe.wait_ge(hid_up, n)
                        hidden("Wgu", 4 * e + t, 4)
                        hidden("Wgu", 4 * e + 2 + t, 5).then_inc(hid_mm, 1)

                    def moe1(n):
                        e, t = divmod(n - 1, H1T)
                        if n == -1:
                            pe.wait_ge(split_x, 2)
                        if 0 <= n - 1 < H1T * EXPERTS:
                            if t == 1 and e + 1 < EXPERTS:
                                weights(1, e + 1)
                            down(1, n - 1, H1T, H0T * EXPERTS)
                        if n + 1 < H1T * EXPERTS:
                            up1(n + 1)

                    def att_in(part):
                        if part < 2:
                            pe.wait_ge(final_b, 4)
                            for j in (2 * part, 2 * part + 1):
                                if part:
                                    pe.wait_ge(ai_relu, j - 1)
                                pe.matmul(ps[:, 4 + j % 2, 0:N], small["we1k1"][:, j * D:(j + 1) * D], x2[:, :],
                                          start=True, stop=True).then_inc(ai_mm, 1)
                            return
                        pe.wait_ge(ai_relu, 4)
                        for j in range(2):
                            for t in range(2):
                                mm = pe.matmul(ps[:, 6 + j, 0:N], small["wk2"][:, (2 * t + j) * D:(2 * t + j + 1) * D],
                                               k1[:, t, :], start=(t == 0), stop=(t == 1))
                            mm.then_inc(akq_mm, 1)
                        for c in range(4):
                            for t in range(2):
                                mm = pe.matmul(ps[0:C, 4, c * D:(c + 1) * D], e1[:, t, chunk(c)],
                                               small["we2"][:, t * D:(t + 1) * D], start=(t == 0), stop=(t == 1))
                        mm.then_inc(av_mm, 1)

                    def att_max(part):
                        if part == 0:
                            pe.wait_ge(akq_round, 2)
                            for c in range(4):
                                mm = pe.matmul(ps[0:C, 6 + c // 2, (c % 2) * TP:(c % 2 + 1) * TP], qr2[:, chunk(c)],
                                               kr2[:, (c // 2) * TP:(c // 2 + 1) * TP], start=True, stop=True)
                            mm.then_inc(am_mm, 1)
                            return
                        pe.wait_ge(am_max, 1)
                        for c in range(4):
                            mm = pe.transpose(ps[:, 5, chunk(c)], mp2[:, c, :], ident[0:C, 0:C])
                        mm.then_inc(am_t, 1)

                    def att_pv(part):
                        if part == 0:
                            pe.wait_ge(am_aug, 1)
                            pe.wait_ge(av_kept, 1)
                            for b in range(2):
                                for kk in range(2):
                                    mm = pe.matmul(ps[0:C, 6 + b, kk * TP:(kk + 1) * TP], ks2[:, chunk(2 * b + kk)],
                                                   qs2[:, b * TP:(b + 1) * TP], start=True, stop=True)
                            mm.then_inc(as_mm, 1)
                            return
                        pe.wait_ge(as_exp, 1)
                        for b in range(2):
                            for qc in range(2):
                                for kk in range(2):
                                    rows = KROWS[kk]
                                    mm = pe.matmul(ps[0:C, 4 + b, qc * 130:(qc + 1) * 130], ptb[0:rows, 2 * b + kk, chunk(qc)],
                                                   vt[0:rows, 2 * b + kk, :], start=(kk == 0), stop=(kk == 1))
                        mm.then_inc(ao_mm, 1)

                    def att_out():
                        pe.wait_ge(ao_norm, 1)
                        for c in range(4):
                            mm = pe.transpose(ps[:, 6, chunk(c)], outs[:, c, :], ident[0:C, 0:C])
                        mm.then_inc(at_mm, 1)

                    def store():
                        pe.wait_ge(y_done, 1)
                        for c in range(4):
                            mm = pe.transpose(ps[0:C, 4, c * D:(c + 1) * D], hb[:, chunk(c)], ident[:, :])
                        mm.then_inc(y_mm, 1)

                    walk(order, {"norm": lambda *a: norm_pe(pe, *a), "embed": embed, "qkv": qkv, "maxima": maxima,
                                 "heads": heads, "proj": proj, "ff": ff, "ret_in": ret_in, "ret": ret,
                                 "route": route, "moe0": moe0, "moe1": moe1, "att_in": att_in, "att_max": att_max,
                                 "att_pv": att_pv, "att_out": att_out, "store": store})

                @block.scalar
                def _(act):
                    def keep(dst, src, done, bias=0.0, func=ACT.Identity, scale=1.0):
                        act.activation(dst, src, func, bias=bias, scale=scale).then_inc(done, 1)

                    def qkv(i, part):
                        if part < 4:
                            for j in (2 * part, 2 * part + 1):
                                act.wait_ge(qk_mm, 8 * i + j + 1)
                                if j >= 2:
                                    act.wait_ge(stacked, 8 * i + j - 1)
                                keep(high[:, j % 2, :], ps[:, j % 4, 0:N], qk_high,
                                     bias=0.0 if j < 4 else col("ones_row", j % 2))
                            return
                        act.wait_ge(v_mm, i + 1)
                        v = ps[0:C, 0, :].rearrange("p (c h d) -> p c h d", c=4, h=HEADS)
                        for half in range(2):
                            keep(vph[:, 2 * half:2 * half + 2, :, 0:HD], v[:, 2 * half:2 * half + 2], v_kept)

                    def heads(i, u):
                        if u < UNITS:
                            act.wait_ge(st_mm, 8 * i + u + 1)
                            keep(pt[:, u % 2, :, :].rearrange("p (t j) n -> p j t n", j=2), heads_of(0), exp_done,
                                 func=ACT.Exp, scale=HD ** -0.5)
                        if u in (4, UNITS):
                            four = u // 4 - 1
                            act.wait_ge(pv_mm, 2 * i + four + 1)
                            keep(oe[:, four, :], ps[:, 2 + four, 0:N], o_kept)

                    def ff(i, t):
                        if t < 3:
                            m = FF_TILES[t][1]
                            act.wait_ge(ff_mm, 3 * i + t + 1)
                            if t >= 2:
                                act.wait_ge(ff_gate, 3 * i + t - 1)
                            keep(th[0:m, t % 2, :], ps[0:m, 2 * (t % 2), 0:N], ff_tanh, func=ACT.Tanh, scale=0.5)

                    def ret_in(part):
                        if part == 2:
                            act.wait_ge(rv_mm, 1)
                            for h in range(2):
                                v = (t.rearrange("p (m h d) -> p m h d", h=2, d=HD)[:, :, h, :]
                                     for t in (rv2[:, h, :, :].rearrange("p c d -> p (c d)"), ps[0:C, 3, :]))
                                keep(*v, rv_kept)

                    def ret_qk():
                        act.wait_ge(rot_sum, 1)
                        keep(th[:, 0, :], t2[:, :], rq_tanh, func=ACT.Tanh, scale=0.5)

                    def take():
                        keep(hb[:, :], hout[:, :], taken)

                    def splitx(m):
                        act.wait_ge(final_b, (2, 5)[m])
                        keep(x2h[:, :], x2[:, :], high_x)

                    def route(m, part):
                        if part == 0:
                            act.wait_ge(gap_done, m + 1)
                            keep(dth[:, :], dl[:, :], gap_tanh, func=ACT.Tanh, scale=0.5)
                        else:
                            weights(m, 0)

                    def weights(m, e):
                        act.wait_ge(wb_mm, EXPERTS * m + e + 1)
                        if e >= 2:
                            act.wait_ge(exp_scaled, EXPERTS * m + e - 1)
                        keep(wb[:, e % 2, :], ps[:, 6 + e % 2, 0:N], wb_kept)

                    def moe0(n):
                        e, t = divmod(n, H0T)
                        n += 1
                        if n < H0T * EXPERTS:
                            act.wait_ge(hid_mm, n + 1)
                            if n >= 3:
                                act.wait_ge(exp_mm, n - 2)
                            keep(g[:, n % 3, :], ps[:, 4 + n % 2, 0:N], hid_act, func=ACT.Gelu_apprx_tanh,
                                 bias=small["b1"][:, n:n + 1])
                        if t == 2 and e + 1 < EXPERTS:
                            weights(0, e + 1)

                    def moe1(n):
                        e, t = divmod(n - 1, H1T)
                        if n >= 1 and t == 1 and e + 1 < EXPERTS:
                            weights(1, e + 1)
                        n += 1
                        if n < H1T * EXPERTS:
                            act.wait_ge(hid_mm, H0T * EXPERTS + n + 1)
                            if n >= 2:
                                act.wait_ge(hid_up, n - 1)
                            keep(gs[:, n % 2, :], ps[:, 4, 0:N], hid_act, func=ACT.Gelu_apprx_sigmoid,
                                 bias=small["bg"][:, n:n + 1])

                    def att_in(part):
                        if part < 2:
                            for j in (2 * part, 2 * part + 1):
                                act.wait_ge(ai_mm, j + 1)
                                keep((e1 if j < 2 else k1)[:, j % 2, :], ps[:, 4 + j % 2, 0:N], ai_relu, func=ACT.Relu,
                                     bias=col("be1k1", j))
                            return
                        for j in range(2):
                            act.wait_ge(akq_mm, j + 1)
                            keep((ks2, qs2)[j][:, :], ps[:, 6 + j, 0:N], akq_kept, bias=col("bkq", j))
                        act.wait_ge(av_mm, 1)
                        keep(vt[:, :, 0:D], ps[0:C, 4, :].rearrange("p (c d) -> p c d", c=4), av_kept)

                    def att_pv(part):
                        if part == 0:
                            act.wait_ge(as_mm, 1)
                            keep(ptb[:, :, :].rearrange("p (b k) t -> p b k t", k=2), heads_of(6), as_exp, func=ACT.Exp)

                    def store():
                        act.wait_ge(y_mm, 1)
                        keep(outs[:, :, :].rearrange("p c d -> p (c d)"), ps[0:C, 4, :], y_kept)

                    walk(order, {"norm": lambda *a: norm_act(act, *a), "qkv": qkv, "heads": heads, "ff": ff,
                                 "ret_in": ret_in, "ret_qk": ret_qk, "take": take, "split": splitx,
                                 "route": route, "moe0": moe0, "moe1": moe1, "att_in": att_in, "att_pv": att_pv,
                                 "store": store})

                @block.vector
                def _(dve):
                    def embed(q):
                        both = xa[:, :].rearrange("p (b t) -> p b t", b=2)
                        pos = small["pos"]
                        if q == 0:
                            dve.tensor_copy(both[:, :, 0:TP:T], pos[:, 0:TP:T].unsqueeze(1).to_broadcast([D, 2, 2]))
                        dve.wait_ge(embed_mm, q + 1)
                        first = 1 + (q % 2) * HALF * SIDE
                        dve.tensor_tensor(both[:, q // 2, first:first + HALF * SIDE], ps[:, q, 0:HALF * SIDE],
                                          pos[:, first:first + HALF * SIDE], ALU.add).then_inc(embed_x, 1)

                    def qkv(i, part):
                        if part == 4:
                            return
                        for j in (2 * part, 2 * part + 1):
                            dve.wait_ge(qk_high, 8 * i + j + 1)
                            dve.scalar_tensor_tensor(out=(qst, kst)[j // 4][:, j % 4, :], in0=high[:, j % 2, :].bitcast(F32),
                                                     scalar=col("parts", j // 4), in1=ps[:, j % 4, 0:N],
                                                     op0=ALU.mult, op1=ALU.add).then_inc(stacked, 1)

                    def maxima(i, part):
                        if part == 4:
                            for t in range(TILES):
                                dve.wait_ge(max_t, 2 * i + t // 2 + 1)
                                dve.tensor_tensor(qst[:, t, :], qst[:, t, :].bitcast(F32), ps[:, t // 2, 0:N], ALU.add)\
                                    .then_inc(q_aug, 1)
                            return
                        for u in (2 * part, 2 * part + 1):
                            four, c = divmod(u, 4)
                            dve.wait_ge(sq_mm, 8 * i + u + 1)
                            m = mp[:, c, four, :].rearrange("p (j r) -> p j r", j=2)[:, :, STACK:STACK + 2]
                            dve.tensor_reduce(m, heads_of(2 * (u % 2))[:, :, :, 0:T], AX.X, ALU.max, negate=True)\
                                .then_inc(max_done, 1)

                    def heads(i, u):
                        if u in (5, UNITS + 1):
                            four = u // UNITS
                            n = 2 * i + four + 1
                            dve.wait_ge(sum_mm, n)
                            dve.reciprocal(on[:, four, :], ps[:, 2 + four, 0:N]).then_inc(rec_done, 1)
                            dve.wait_ge(rec_done, n)
                            dve.tensor_tensor(on[:, four, :], on[:, four, :], oe[:, four, :], ALU.mult).then_inc(on_done, 1)

                    def proj(i):
                        dve.wait_ge(proj_mm, i + 1)
                        dve.tensor_tensor(xa[:, :], xa[:, :], ps[:, 0, 0:N], ALU.add).then_inc(x_proj, 1)

                    def ff(i, t):
                        if t < 3:
                            m = FF_TILES[t][1]
                            n = 3 * i + t + 1
                            dve.wait_ge(ff_tanh, n)
                            dve.scalar_tensor_tensor(out=gu[0:m, t, :], in0=th[0:m, t % 2, :], scalar=1.0,
                                                     in1=ps[0:m, 2 * (t % 2), 0:N], op0=ALU.add, op1=ALU.mult)\
                                .then_inc(ff_gate, 1)
                            dve.wait_ge(ff_gate, n)
                            dve.tensor_tensor(gu[0:m, t, :], gu[0:m, t, :], ps[0:m, 2 * (t % 2) + 1, 0:N], ALU.mult)\
                                .then_inc(ff_act, 1)
                            return
                        dve.wait_ge(down_mm, i + 1)
                        dve.scalar_tensor_tensor(out=xa[:, :], in0=ps[:, 2, 0:N], scalar=0.5, in1=xa[:, :],
                                                 op0=ALU.mult, op1=ALU.add).then_inc(x_ff, 1)

                    def table(name):
                        return small[name][:, :].unsqueeze(1).to_broadcast([D, 2, TP])

                    def pair3(t):
                        return t.rearrange("p (b t) -> p b t", b=2)

                    def ret_in(j):
                        if j == 2:
                            return
                        dst = (t2, t1)[j]
                        dve.wait_ge(rot_mm, 2 * j + 1)
                        dve.tensor_tensor(pair3(dst[:, :]), pair3(ps[:, 0, 0:N]), table("cos"), ALU.mult)\
                            .then_inc(rot_part, 1)
                        dve.wait_ge(rot_mm, 2 * j + 2)
                        if j:
                            dve.wait_ge(rot_sum, 1)
                        dve.tensor_tensor(pair3(sqa[:, :]), pair3(ps[:, 1, 0:N]), table("sin"), ALU.mult)\
                            .then_inc(rot_part, 1)
                        dve.wait_ge(rot_part, 2 * j + 2)
                        dve.tensor_tensor(dst[:, :], dst[:, :], sqa[:, :], ALU.add).then_inc(rot_sum, 1)

                    def ret_qk():
                        dve.wait_ge(rq_tanh, 1)
                        dve.scalar_tensor_tensor(out=t2[:, :], in0=th[:, 0, :], scalar=1.0, in1=t2[:, :],
                                                 op0=ALU.add, op1=ALU.mult).then_inc(rq_gate, 1)
                        dve.wait_ge(rq_gate, 1)
                        for e in range(2):
                            dve.tensor_scalar(qeo[:, e, :], t2[:, :], col("evenodd", e), None, ALU.mult).then_inc(rq_done, 1)

                    def ret(r):
                        decay = small["decay"]
                        for k in (2 * r, 2 * r + 1):
                            if k < BATCH_PIECES:
                                width = RQ[k % 2][1]
                                start = (1, 0)[k % 2]
                                dve.wait_ge(rs_mm, k + 1)
                                dve.tensor_tensor(rt[:, k % 3, :, 0:width],
                                                  ps[0:C, k % 3, 0:2 * TP].rearrange("p (h t) -> p h t", h=2)[:, :, 0:width],
                                                  decay[:, start:start + width].unsqueeze(1).to_broadcast([C, 2, width]),
                                                  ALU.mult).then_inc(decayed, 1)

                    def ret_out():
                        dve.wait_ge(ro_mm, 1)
                        dve.tensor_tensor(xra[:, :], xra[:, :], ps[:, 3, 0:N], ALU.add).then_inc(ret_sum, 1)
                        dve.wait_ge(ret_sum, 1)
                        if pair_b is not None:
                            dve.wait_ge(taken, 1)
                        dve.scalar_tensor_tensor(out=hout[:, :], in0=xra[:, :], scalar=0.0, in1=hout[:, :],
                                                 op0=ALU.max, op1=ALU.add).then_inc(a_done, 1)

                    def splitx(m):
                        dve.wait_ge(high_x, m + 1)
                        dve.tensor_tensor(x2l[:, :], x2[:, :], x2h[:, :].bitcast(F32), ALU.subtract).then_inc(split_x, 1)

                    def route(m, part):
                        if part:
                            return
                        dve.wait_ge(lg_mm, m + 1)
                        dve.tensor_tensor(lg[:, :, :], ps[0:C, 6, 0:4 * EXPERTS].rearrange("p (c e) -> p c e", c=4),
                                          small["rb"][:, m * EXPERTS:(m + 1) * EXPERTS].unsqueeze(1).to_broadcast([C, 4, EXPERTS]),
                                          ALU.add).then_inc(lg_kept, 1)
                        dve.wait_ge(lg_kept, m + 1)
                        for c in range(4):
                            dve.max(m8[:, c, :], lg[:, c, :]).then_inc(top_done, 1)
                        dve.wait_ge(top_done, 4 * m + 4)
                        dve.tensor_tensor(dl[:, :], m8[:, :, 1], m8[:, :, 0], ALU.subtract).then_inc(gap_done, 1)
                        for c in range(4):
                            dve.max_index(i8[:, c, :], m8[:, c, :], lg[:, c, :]).then_inc(idx_done, 1)
                        dve.wait_ge(idx_done, 4 * m + 4)
                        dve.tensor_copy(i8f[:, :, :], i8[:, :, 0:2]).then_inc(idx_f, 1)
                        dve.wait_ge(gap_tanh, m + 1)
                        dve.tensor_scalar(cw[:, 0, :], dth[:, :], -0.5, 0.5, ALU.mult, ALU.add)
                        dve.tensor_scalar(cw[:, 1, :], dth[:, :], 0.5, 0.5, ALU.mult, ALU.add).then_inc(conf_done, 1)
                        dve.wait_ge(conf_done, m + 1)
                        dve.wait_ge(idx_f, m + 1)
                        for k, dst in enumerate((w1t, w2t)):
                            for c in range(4):
                                dve.tensor_scalar(dst[:, c, :], small["iota"][:, :], i8f[:, c, k:k + 1], cw[:, k, c:c + 1],
                                                  ALU.is_equal, ALU.mult).then_inc(pick_done, 1)
                        dve.wait_ge(pick_done, 8 * m + 8)
                        dve.tensor_tensor(wtok[:, :, :], w1t[:, :, :], w2t[:, :, :], ALU.add).then_inc(w_done, 1)

                    def scaled(m, e, tiles, base):
                        dve.wait_ge(exp_mm, base + tiles * (e + 1))
                        n = EXPERTS * m + e
                        if n >= 2:
                            dve.wait_ge(acc_done, n - 1)
                        dve.scalar_tensor_tensor(out=to[:, e % 2, :], in0=ps[:, 6 + e % 2, 0:N],
                                                 scalar=small["b2bd"][:, n:n + 1], in1=wb[:, e % 2, :],
                                                 op0=ALU.add, op1=ALU.mult).then_inc(exp_scaled, 1)

                    def moe0(n):
                        e, t = divmod(n, H0T)
                        if n >= 1 and t == 0:
                            scaled(0, e - 1, H0T, 0)

                    def moe1(n):
                        base = H0T * EXPERTS
                        e, t = divmod(n, H1T)
                        if n >= 2 and t == 1:
                            scaled(1, e - 1, H1T, base)
                        n += 1
                        if n < H1T * EXPERTS:
                            dve.wait_ge(hid_act, base + n + 1)
                            k = (base + n) % 3
                            dve.wait_ge(exp_mm, base + n - 2)
                            dve.scalar_tensor_tensor(out=g[:, k, :], in0=ps[:, 5, 0:N], scalar=bu1[:, n:n + 1],
                                                     in1=gs[:, n % 2, :], op0=ALU.add, op1=ALU.mult).then_inc(hid_up, 1)

                    def sum0():
                        dve.wait_ge(acc_done, EXPERTS)
                        dve.tensor_tensor(x1[:, :], x1[:, :], acc[:, :], ALU.add).then_inc(x1_sum, 1)

                    def add0():
                        dve.wait_ge(final_b, 3)
                        dve.tensor_tensor(hb[:, :], hb[:, :], x1[:, :], ALU.add).then_inc(hb_add, 1)

                    def att_in(part):
                        if part == 2:
                            for j in range(2):
                                dve.wait_ge(akq_kept, j + 1)
                                dve.tensor_copy((kr2, qr2)[j][:, :], (ks2, qs2)[j][:, :]).then_inc(akq_round, 1)

                    def att_max(part):
                        if part == 0:
                            dve.wait_ge(am_mm, 1)
                            dve.tensor_reduce(mp2[:, :, 64].rearrange("p (b k) -> p b k", k=2), heads_of(6)[:, :, :, 0:T],
                                              AX.X, ALU.max, negate=True).then_inc(am_max, 1)
                            return
                        dve.wait_ge(am_t, 1)
                        dve.tensor_tensor(qs2[:, :], qs2[:, :], ps[:, 5, 0:N], ALU.add).then_inc(am_aug, 1)

                    def att_pv(part):
                        if part == 0:
                            return
                        dve.wait_ge(ao_mm, 1)
                        o = ps[0:C, 4:6, 0:260].rearrange("p b (q d) -> p b q d", q=2)
                        dve.reciprocal(recb[:, :].rearrange("p (b q) -> p b q", b=2), o[:, :, :, D]).then_inc(ao_rec, 1)
                        dve.wait_ge(ao_rec, 1)
                        dve.tensor_tensor(outs[:, :, :].rearrange("p (b q) d -> p b q d", b=2), o[:, :, :, 0:D],
                                          recb[:, :].rearrange("p (b q) -> p b q", b=2).unsqueeze(3).to_broadcast([C, 2, 2, D]),
                                          ALU.mult).then_inc(ao_norm, 1)

                    def att_out():
                        dve.wait_ge(at_mm, 1)
                        dve.scalar_tensor_tensor(out=hb[:, :], in0=ps[:, 6, 0:N], scalar=col("be2"), in1=hb[:, :],
                                                 op0=ALU.add, op1=ALU.add).then_inc(hb_add, 1)

                    def store():
                        dve.wait_ge(acc_done, 2 * EXPERTS)
                        dve.tensor_tensor(hb[:, :], hb[:, :], acc[:, :], ALU.add).then_inc(y_done, 1)

                    walk(order, {"norm": lambda *a: norm_dve(dve, *a), "embed": embed, "qkv": qkv, "maxima": maxima,
                                 "heads": heads, "proj": proj, "ff": ff, "ret_in": ret_in, "ret_qk": ret_qk, "ret": ret,
                                 "ret_out": ret_out, "split": splitx, "route": route, "moe0": moe0, "moe1": moe1,
                                 "sum0": sum0, "add0": add0, "att_in": att_in, "att_max": att_max, "att_pv": att_pv,
                                 "att_out": att_out, "store": store})

                @block.gpsimd
                def _(pool):
                    def add(m, e):
                        n = EXPERTS * m + e
                        pool.wait_ge(exp_scaled, n + 1)
                        if e == 0:
                            pool.tensor_copy(acc[:, :], to[:, 0, :]).then_inc(acc_done, 1)
                        else:
                            pool.wait_ge(acc_done, n)
                            pool.tensor_tensor(acc[:, :], acc[:, :], to[:, e % 2, :], ALU.add).then_inc(acc_done, 1)

                    def moe0(n):
                        if n >= 1 and n % H0T == 0:
                            add(0, n // H0T - 1)

                    def moe1(n):
                        if n >= 2 and n % H1T == 1:
                            add(1, n // H1T - 1)

                    walk(order, {"norm": lambda *a: norm_pool(pool, *a), "moe0": moe0, "moe1": moe1})

            nc.sync.sem_clear(range(sems[0].num, sems[-1].num + 1))
            nc.all_engine_barrier()

        assert [s.num for s in sems] == list(range(sems[0].num, sems[0].num + len(sems)))
        body(only(0), 0, None, 1)
        with nc.Fori(0, PAIRS - 2) as i:
            body(merged(), i + 1, i, i + 2)
        body(merged(), PAIRS - 1, PAIRS - 2, None)
        body(only(1), None, PAIRS - 1, None)


def walk(order, steps):
    for name, *arguments in order:
        if name in steps:
            steps[name](*arguments)


SPLIT = ("W1", "Wgu")
COLUMNS = (("conv_b", 1), ("cls", 1), ("ln1", 2), ("ln2", 2), ("ln_f", 1), ("gn_w", 1), ("gn_b", 1), ("ln_g", 1),
           ("ln_b", 1), ("out_g", 1), ("out_b", 1), ("be2", 1), ("be1k1", 4), ("bkq", 2), ("ones_row", 2), ("parts", 2), ("evenodd", 2))
COL = {name: sum(n for _, n in COLUMNS[:k]) for k, (name, _) in enumerate(COLUMNS)}
COL_TOTAL = sum(n for _, n in COLUMNS)


def constants():
    c = {"ident": np.eye(D, dtype=np.float32)}
    c["cen_all"] = (np.eye(D) - 1.0 / D).astype(np.float32)
    same = np.arange(D)[:, None] // HD == np.arange(D)[None, :] // HD
    c["cen_group"] = (np.eye(D) - same / HD).astype(np.float32)
    c["stat_all"] = np.full((D, 2), 1.0 / D, np.float32)
    c["stat_group"] = ((np.arange(D)[:, None] // HD == np.arange(HEADS)[None, :]) / HD).astype(np.float32)
    s, d = np.arange(T, dtype=np.float64), np.arange(D)
    scale = ((d // 2 * 2 + 0.4 * D) / (1.4 * D))[:, None] ** (s / 512.0)[None, :]
    angle = (1.0 / 10000.0 ** ((d // 2) / (D // 2)))[:, None] * s[None, :]
    sign = np.where(d % 2 == 0, -1.0, 1.0)[:, None]
    c["cos"], c["sin"] = np.zeros((D, TP), np.float32), np.zeros((D, TP), np.float32)
    c["cos"][:, :T] = np.cos(angle) * scale
    c["sin"][:, :T] = np.sin(angle) * scale * sign
    gap = np.arange(TP + 1)[None, :] - 1 - np.arange(C)[:, None]
    c["decay"] = np.where(gap >= 0, 0.5 * 0.9 ** np.maximum(gap, 0), 0.0).astype(np.float32)
    row = np.arange(D)
    c["sums"] = ((row[:, None] % 32 == HD) & (row[:, None] // 32 == row[None, :] // 32)).astype(np.float32)
    c["iota"] = np.tile(np.arange(EXPERTS, dtype=np.float32), (C, 1))
    return c


def layout(a):
    f = {k: np.asarray(v) for k, v in a.items()}
    out = constants()

    def rows(m):
        return m.reshape(-1, D, m.shape[-1]).transpose(1, 0, 2).reshape(D, -1)

    wp = f["L0_tok_conv_w"].transpose(1, 2, 3, 0).reshape(3 * PATCH, PATCH * D)
    out["wp"] = np.zeros((128, PATCH // 2 * D), np.float32)
    out["wp"][0:48], out["wp"][64:112] = wp[:, :PATCH // 2 * D], wp[:, PATCH // 2 * D:]
    out["pos"] = np.zeros((D, TP), np.float32)
    out["pos"][:, :T] = f["L0_tok_pos_emb"][0].T
    for i in range(2):
        qkv = f[f"L0_tok_qkv_{i}"].T
        padded = np.zeros((D, 2 * HEADS, 64), np.float32)
        for part in range(3):
            padded[:, :, part * HD:(part + 1) * HD] = qkv[:, :2 * D].reshape(D, 2 * HEADS, HD)
        out[f"wqk{i}"] = padded.reshape(D, 8 * D)
        out[f"wv{i}"] = qkv[:, 2 * D:]
        wo = np.zeros((2, 4, 32, D), np.float32)
        wo[:, :, :HD] = f[f"L0_tok_wo_{i}"].T.reshape(2, 4, HD, D)
        out[f"wo{i}"] = rows(wo.reshape(2 * D, D))
        out[f"wg{i}"], out[f"wu{i}"] = f[f"L0_tok_gate_{i}"].T, f[f"L0_tok_up_{i}"].T
        down = np.zeros((3 * D, D), np.float32)
        down[:FF] = f[f"L0_tok_down_{i}"].T
        out[f"wd{i}"] = rows(down)
    swap = np.arange(D) ^ 1
    out["rqk"] = np.concatenate([m for n in ("Wq", "Wk") for m in (f["L0_attn_" + n], f["L0_attn_" + n][:, swap])], 1)
    out["rv"] = f["L0_attn_Wv"]
    out["route0"], out["route1"] = f["L0_ffn_Wg"], f["L1_ffn_router_w"]
    rb = np.zeros((C, 2 * EXPERTS), np.float32)
    rb[:, EXPERTS:] = f["L1_ffn_router_b"][None, :]
    out["rb"] = rb
    out["W1"] = f["L0_ffn_W1"].transpose(1, 0, 2).reshape(D, -1)
    out["W2"] = rows(f["L0_ffn_W2"].reshape(-1, D))
    out["Wgu"] = f["L1_ffn_gate_up_proj"].transpose(1, 0, 2).reshape(D, -1)
    out["Wd"] = rows(f["L1_ffn_down_proj"].reshape(-1, D))
    out["b1"] = f["L0_ffn_b1"].reshape(-1, D).T
    bgu = f["L1_ffn_gate_up_proj_bias"].reshape(EXPERTS, 2, H1T, D)
    out["bg"], out["bu"] = bgu[:, 0].reshape(-1, D).T, bgu[:, 1].reshape(-1, D).T
    out["b2bd"] = np.concatenate([f["L0_ffn_b2"].T, f["L1_ffn_down_proj_bias"].T], 1)
    out["we1k1"] = np.concatenate([f["L1_attn_We1"], f["L1_attn_Wk1"]], 1)
    out["we2"] = rows(f["L1_attn_We2"])
    wk2 = np.zeros((2 * D, 2, D), np.float32)
    wk2[:, 0, :64], wk2[:, 1, :64] = f["L1_attn_Wk2"][:, :64], f["L1_attn_Wk2"][:, 64:]
    out["wk2"] = rows(wk2.reshape(2 * D, 2 * D))
    cols = np.zeros((D, COL_TOTAL), np.float32)

    def put(name, *vectors):
        for k, v in enumerate(vectors):
            cols[:, COL[name] + k] = v

    put("conv_b", f["L0_tok_conv_b"])
    put("cls", f["L0_tok_cls_token"].reshape(D))
    put("ln1", f["L0_tok_ln1_0"], f["L0_tok_ln1_1"])
    put("ln2", f["L0_tok_ln2_0"], f["L0_tok_ln2_1"])
    put("ln_f", f["L0_tok_ln_f"])
    put("gn_w", f["L0_attn_gn_weight"])
    put("gn_b", f["L0_attn_gn_bias"])
    put("ln_g", f["L0_ffn_ln_g"])
    put("ln_b", f["L0_ffn_ln_b"])
    put("out_g", f["L0_ffn_out_g"])
    put("out_b", f["L0_ffn_out_b"])
    put("be2", f["L1_attn_be2"])
    put("be1k1", *f["L1_attn_be1"].reshape(2, D), *f["L1_attn_bk1"].reshape(2, D))
    bk, bq = np.zeros(D, np.float32), np.zeros(D, np.float32)
    bk[:64], bq[:64] = f["L1_attn_bk2"][:64], f["L1_attn_bk2"][64:]
    bk[64] = 1.0
    put("bkq", bk, bq)
    row = np.arange(D) % 64
    put("ones_row", *(row == STACK + t for t in range(2)))
    put("parts", -1.0 * (row // HD == 1), -1.0 * (row // HD == 2) + 1.0 * (row // 2 * 2 == STACK))
    even = (np.arange(D) // HD % 2 == 0).astype(np.float32)
    put("evenodd", even, 1.0 - even)
    out["cols"] = cols
    return {k: np.ascontiguousarray(v) for k, v in out.items()}


def kernel(**inputs):
    import concourse.bacc as bacc
    from concourse.bass_utils import run_bass_kernel_spmd
    arrays = {"x": np.ascontiguousarray(inputs.pop("x")), **layout(inputs)}
    nc = bacc.Bacc("TRN2", target_bir_lowering=False, num_devices=1)
    aps = {k: nc.dram_tensor(k + "_dram", v.shape, F32, kind="ExternalInput").ap() for k, v in arrays.items()}
    out = nc.dram_tensor("out_dram", (BATCH, T, D), F32, kind="ExternalOutput").ap()
    tower(nc, aps.pop("x"), aps, out)
    r = run_bass_kernel_spmd(nc, [{k + "_dram": v for k, v in arrays.items()}], core_ids=[0])
    return r.results[0]["out_dram"]
```

```python
from contextlib import ExitStack

import numpy as np
import concourse.bass as bass
from concourse import mybir

ALU = mybir.AluOpType
ACT = mybir.ActivationFunctionType
AX = mybir.AxisListType
F32 = mybir.dt.float32
F32R = mybir.dt.float32r
U32 = mybir.dt.uint32

D = 128
BATCH = 64
PAIRS = BATCH // 2
PATCH = 16
SIDE = 14
PATCHES = SIDE * SIDE
T = PATCHES + 1
TP = T + 1
N = 2 * TP
C = TP // 2
HEADS, HD = 8, 16
FF = 344
FF_TILES = [(0, 128), (128, 128), (256, 88)]
EXPERTS = 8
H0T = 4
H1T = 2
KROWS = (C, C - 1)
HALF = SIDE // 2
TILES = HEADS // 2
STACK = 3 * HD
ROWS = STACK + 2
VW = HD + 2
RQ = ((0, TP), (C - 1, C + 1))
UNITS = 8
BATCH_PIECES = 16

NORMS_A = [(None, 1, 1e-6)] * 5 + [("all", 1, 1e-5), ("group", 8, 1e-5)]
NORMS_B = [("all", 1, 1e-5)] * 5



def norm(stream, n):
    return [("norm", stream, n, part) for part in range(3)]


def vit_in(i):
    return [("qkv", i, part) for part in range(5)]


def vit_scores(i):
    return [("maxima", i, part) for part in range(5)]


def vit_heads(i):
    return [("heads", i, u) for u in range(UNITS + 1)]


def vit_out(i):
    return ([("heads", i, UNITS + 1), ("heads", i, UNITS + 2), ("proj", i)] + norm("a", 2 * i + 1)
            + [("ff", i, part) for part in range(4)])


RETENTION = (norm("a", 4) + norm("a", 5)[:2] + [("embed", 0)] + norm("a", 5)[2:]
             + [("ret_in", part) for part in range(3)] + norm("a", 6)[:2] + [("embed", 1)] + norm("a", 6)[2:]
             + [("ret_qk",)] + [("ret", r) for r in range(BATCH_PIECES // 2)])
BEFORE_0 = norm("b", 0) + norm("b", 1) + [("split", 0)] + [("route", 0, part) for part in range(3)]
MIXTURE_0 = [("moe0", n) for n in range(-1, H0T * EXPERTS + 1)]
BETWEEN = ([("sum0",)] + norm("b", 2) + [("add0",)] + norm("b", 3)
           + [("att_in", part) for part in range(3)] + [("att_max", 0), ("att_max", 1), ("att_pv", 0), ("att_pv", 1),
              ("att_out",)] + norm("b", 4) + [("split", 1)] + [("route", 1, part) for part in range(3)])
MIXTURE_1 = [("moe1", n) for n in range(-1, H1T * EXPERTS + 2)]

NEXT = norm("a", 0)
RETENTION_END = [NEXT[0], ("ret", BATCH_PIECES // 2), NEXT[1], ("ret_out",), NEXT[2]]

STREAM_A = (vit_in(0) + vit_scores(0) + vit_heads(0) + vit_out(0) + norm("a", 2) + vit_in(1) + vit_scores(1) + vit_heads(1)
            + vit_out(1) + RETENTION + RETENTION_END)
STREAM_B = BEFORE_0 + MIXTURE_0 + BETWEEN + MIXTURE_1 + [("store",)]

TURNS = (
    "ababaabababaabababaababaaaaaabbababababababaabababbabbabbbbababbaaababababbababbabbbbbaabbababababab"
    "aabababaababbabababababaabaaabbababbabbaabababbbbabababababbabaabaabbaaabaaa"
)
assert (TURNS.count("a"), TURNS.count("b")) == (len(STREAM_A), len(STREAM_B))


def merged(last=False):
    steps = {"a": iter(STREAM_A), "b": iter(STREAM_B)}
    order = [("take",)] + [next(steps[turn]) for turn in TURNS]
    return [step for step in order if not (last and (step[0] == "embed" or step in NEXT))]


def only(stream):
    return [("take",)] + STREAM_B if stream else STREAM_A


def tower(nc, x, w, out):
    def chunk(c):
        return slice(c * C, (c + 1) * C)

    with ExitStack() as ctx:
        def sb(name, shape, dt=F32):
            return ctx.enter_context(nc.sbuf_tensor(name, shape, dt))

        sems = []

        def sem(name):
            sems.append(ctx.enter_context(nc.semaphore(name)))
            return sems[-1]

        small = {name: sb("w_" + name, list(ap.shape)) for name, ap in w.items() if name not in SPLIT}
        split = {name: (sb("h_" + name, list(w[name].shape), F32R), sb("l_" + name, list(w[name].shape), F32R))
                 for name in SPLIT}
        ident = small["ident"]
        neg_half = sb("neg_half", [C, 4 * HEADS])
        bu1 = sb("bu1", [D, EXPERTS * H1T])

        img = sb("img", [128, 2, HALF, SIDE * PATCH])
        xa = sb("xa", [D, N])
        ha = sb("ha", [D, N])
        epsa, rsa = sb("epsa", [C, 4 * HEADS]), sb("rsa", [C, 4 * HEADS])
        qst, kst = sb("qst", [D, TILES, N], F32R), sb("kst", [D, TILES, N], F32R)
        vp = sb("vp", [C, 4 * HEADS * VW + 32 - VW])
        vph = vp[:, 0:4 * HEADS * VW].rearrange("p (c h d) -> p c h d", c=4, h=HEADS)
        mp = sb("mp", [C, 4, 2, D])
        shared_a = sb("shared_a", [D, 8 * N])
        pt = shared_a[0:C, 0:4 * N].rearrange("p (s h t) -> p s h t", s=2, h=4)
        th = shared_a[:, 4 * N:6 * N].rearrange("p (a n) -> p a n", a=2)
        high = th.bitcast(F32R)
        oe = th
        rec_wide = shared_a[0:C, 6 * N:6 * N + 4 * D].rearrange("p (c h r) -> p c h r", c=4, h=4)
        gu = shared_a[:, 0:3 * N].rearrange("p (a n) -> p a n", a=3)
        sqa, xca = shared_a[:, 6 * N:7 * N], shared_a[:, 7 * N:8 * N]
        rt = shared_a[0:C, 0:3 * N].rearrange("p (s h t) -> p s h t", s=3, h=2)
        rv2 = sb("rv2", [C, 2, 4, D])
        xra, t1, t2 = ha, shared_a[:, 3 * N:4 * N], shared_a[:, 5 * N:6 * N]
        qeo = shared_a[:, 6 * N:8 * N].rearrange("p (a n) -> p a n", a=2)
        rec = sb("rec", [C, 4, 4])
        hout = sb("hout", [D, N])

        hb = sb("hb", [D, N])
        x1 = sb("x1", [D, N])
        x2 = sb("x2", [D, N])
        x2h, x2l = sb("x2h", [D, N], F32R), sb("x2l", [D, N], F32R)
        epsb, rsb = sb("epsb", [C, 4 * HEADS]), sb("rsb", [C, 4 * HEADS])
        lg = sb("lg", [C, 4, EXPERTS])
        m8, i8 = sb("m8", [C, 4, 8]), sb("i8", [C, 4, 8], U32)
        i8f = sb("i8f", [C, 4, 2])
        dl, dth = sb("dl", [C, 4]), sb("dth", [C, 4])
        cw = sb("cw", [C, 2, 4])
        picks = sb("picks", [C, 4, 2, EXPERTS])
        wtok = sb("wtok", [C, 4, 2, EXPERTS])
        wst = sb("wst", [2 * EXPERTS, N], F32R)
        onehot = sb("onehot", [2 * EXPERTS, EXPERTS], F32R)
        wb = sb("wb", [D, 2, N])
        g = sb("g", [D, 3, N])
        gs = sb("gs", [D, 2, N])
        sqb, xcb = gs[:, 0, :], gs[:, 1, :]
        to = sb("to", [D, 2, N])
        acc = sb("acc", [D, N])
        wst_high = to[0:2 * EXPERTS, 1, :].bitcast(F32R)
        e1, k1 = gs, to
        ks2, qs2, kr2, qr2 = g[:, 0, :], g[:, 1, :], x2h, x2l
        mp2 = sb("mp2", [C, 4, 32])
        vt = sb("vt", [C, 4, D + 2])
        ptb = wb[0:C, :, :].rearrange("p a (k t) -> p (a k) t", k=2)
        recb = sb("recb", [C, 4])
        outs = sb("outs", [C, 4, D])
        ps = ctx.enter_context(nc.psum_tensor("ps", [128, 8, 512], F32))

        def load_half(sp, pair, half, done):
            for s in range(2):
                for b in range(2):
                    for ch in range(3):
                        sp.dma_start(img[64 * s + 16 * ch:64 * s + 16 * ch + 16, b, :, 0:SIDE * PATCH - 8 * s],
                                     x[2 * pair + b, ch, half * HALF * PATCH:(half + 1) * HALF * PATCH, 8 * s:]
                                     .rearrange("(i py) w -> py i w", py=PATCH)).then_inc(done, 16)

        with ExitStack() as setup:
            loaded = setup.enter_context(nc.semaphore("loaded"))
            stage_ready = setup.enter_context(nc.semaphore("stage_ready"))
            high_done = setup.enter_context(nc.semaphore("high_done"))
            low_done = setup.enter_context(nc.semaphore("low_done"))
            preset = setup.enter_context(nc.semaphore("preset"))
            STEP = 1024
            stage = shared_a[:, 0:2 * STEP].rearrange("p (a n) -> p a n", a=2)
            pieces = [(n, a) for n in SPLIT for a in range(0, w[n].shape[1], STEP)]
            with nc.Block() as block:
                @block.sync
                def _(sp):
                    for name, ap in w.items():
                        if name not in SPLIT:
                            sp.dma_start(small[name][:], ap).then_inc(loaded, 16)
                    sp.wait_ge(loaded, 16 * len(small))

                @block.scalar
                def _(act):
                    for n, (name, a) in enumerate(pieces):
                        if n >= 2:
                            act.wait_ge(low_done, n - 1)
                        act.dma_start(stage[:, n % 2, :], w[name][:, a:a + STEP]).then_inc(stage_ready, 16)
                        act.wait_ge(stage_ready, 16 * (n + 1))

                @block.vector
                def _(dve):
                    dve.memset(img[:], 0.0)
                    for n, (name, a) in enumerate(pieces):
                        top, low = (s[:, a:a + STEP] for s in split[name])
                        dve.wait_ge(stage_ready, 16 * (n + 1))
                        dve.tensor_copy(top, stage[:, n % 2, :]).then_inc(high_done, 1)
                        dve.wait_ge(high_done, n + 1)
                        dve.tensor_tensor(low, stage[:, n % 2, :], top.bitcast(F32), ALU.subtract).then_inc(low_done, 1)
                    dve.wait_ge(loaded, 16 * len(small))
                    pos = small["pos"]
                    dve.tensor_scalar(pos[:, 1:T], pos[:, 1:T], small["cols"][:, COL["conv_b"]:COL["conv_b"] + 1], None,
                                      ALU.add)
                    dve.tensor_scalar(pos[:, 0:1], pos[:, 0:1], small["cols"][:, COL["cls"]:COL["cls"] + 1], None, ALU.add)
                    dve.tensor_copy(onehot[:, :], small["two_eyes"][:, :])
                    dve.tensor_scalar(bu1[:, :], small["bu"][:, :], 1.0, None, ALU.add).then_inc(preset, 1)

                @block.gpsimd
                def _(pool):
                    pool.memset(mp[:], 0.0)
                    pool.memset(rv2[:], 0.0)
                    pool.memset(mp2[:], 0.0)
                    pool.memset(vp[:], 1.0)
                    pool.memset(vt[:], 1.0)
                    pool.memset(neg_half[:], -0.5).then_inc(preset, 1)

        img_loaded, out_stored = sem("img_loaded"), sem("out_stored")
        embed_mm, embed_x = sem("embed_mm"), sem("embed_x")
        norm_sems = {s: {k: sem(f"norm_{s}_{k}") for k in ("centered", "square", "kept", "stat", "eps", "rsqrt", "spread",
                                                           "out", "final")} for s in "ab"}
        group_spread = sem("group_spread")
        qk_mm, qk_high, stacked, v_mm, v_kept = (sem(n) for n in ("qk_mm", "qk_high", "stacked", "v_mm", "v_kept"))
        sq_mm, max_done, max_t, q_aug = (sem(n) for n in ("sq_mm", "max_done", "max_t", "q_aug"))
        st_mm, exp_done, pv_mm, o_kept, sum_mm, rec_done, on_done = (
            sem(n) for n in ("st_mm", "exp_done", "pv_mm", "o_kept", "sum_mm", "rec_done", "on_done"))
        proj_mm, x_proj = sem("proj_mm"), sem("x_proj")
        rec_spread, rec_mm = sem("rec_spread"), sem("rec_mm")
        ff_mm, ff_tanh, ff_gate, ff_act, down_mm, x_ff = (sem(n) for n in ("ff_mm", "ff_tanh", "ff_gate", "ff_act", "down_mm", "x_ff"))
        rot_mm, rot_part, rot_sum, rv_mm, rv_kept = (sem(n) for n in ("rot_mm", "rot_part", "rot_sum", "rv_mm", "rv_kept"))
        rq_tanh, rq_gate, rq_done = (sem(n) for n in ("rq_tanh", "rq_gate", "rq_done"))
        rs_mm, decayed, ro_mm, ret_sum, a_done = (sem(n) for n in ("rs_mm", "decayed", "ro_mm", "ret_sum", "a_done"))
        taken, high_x, split_x = sem("taken"), sem("high_x"), sem("split_x")
        w_turned, w_high, w_split = sem("w_turned"), sem("w_high"), sem("w_split")
        lg_mm, lg_kept, top_done, idx_done, idx_f, gap_done, gap_tanh, conf_done, pick_done, w_done, wb_mm, wb_kept = (
            sem(n) for n in ("lg_mm", "lg_kept", "top_done", "idx_done", "idx_f", "gap_done", "gap_tanh", "conf_done",
                             "pick_done", "w_done", "wb_mm", "wb_kept"))
        hid_mm, hid_act, up_mm, hid_up, exp_mm, exp_scaled, acc_done = (
            sem(n) for n in ("hid_mm", "hid_act", "up_mm", "hid_up", "exp_mm", "exp_scaled", "acc_done"))
        hb_add = sem("hb_add")
        ai_mm, ai_relu, akq_mm, akq_kept, akq_round, av_mm, av_kept = (
            sem(n) for n in ("ai_mm", "ai_relu", "akq_mm", "akq_kept", "akq_round", "av_mm", "av_kept"))
        am_mm, am_max, am_t, am_aug, as_mm, as_exp, ao_mm, ao_rec, ao_norm, at_mm = (
            sem(n) for n in ("am_mm", "am_max", "am_t", "am_aug", "as_mm", "as_exp", "ao_mm", "ao_rec", "ao_norm", "at_mm"))
        y_mm, y_kept = sem("y_mm"), sem("y_kept")

        cols = small["cols"]

        def col(name, k=0):
            return cols[:, COL[name] + k:COL[name] + k + 1]

        def heads_of(bank, rows=C):
            return ps[0:rows, bank:bank + 2, 0:2 * TP].rearrange("p n (h t) -> p n h t", h=2)

        def nth(s, n, alone):
            return n if s == "b" or alone else (n - 1) % len(NORMS_A)

        def norm_io(s, n):
            if s == "a":
                return [(xa, ha, col("ln1", 0), None, (embed_x, 2)), (xa, ha, col("ln2", 0), None, (x_proj, 1)),
                        (xa, ha, col("ln1", 1), None, (x_ff, 1)), (xa, ha, col("ln2", 1), None, (x_proj, 2)),
                        (xa, hout, col("ln_f"), None, (x_ff, 2)), (hout, xra, None, None, (norm_sems["a"]["final"], 4)),
                        (t1, t1, col("gn_w"), col("gn_b"), (rot_sum, 2))][n]
            return [(hb, x1, None, None, (taken, 1)), (x1, x2, col("ln_g"), col("ln_b"), (norm_sems["b"]["final"], 1)),
                    (x1, x1, col("out_g"), col("out_b"), (acc_done, EXPERTS)), (hb, x2, None, None, (hb_add, 1)),
                    (hb, x2, None, None, (hb_add, 2))][n]

        NORMS = {"a": NORMS_A, "b": NORMS_B}
        BUF = {"a": (sqa, xca, epsa, rsa, 0, 1, 2), "b": (sqb, xcb, epsb, rsb, 4, 5, 6)}

        def centered_before(s, n):
            return sum(c is not None for c, _, _ in NORMS[s][:n])

        def norm_pe(pe, alone, s, n, part):
            sq, xc, eps_t, rs, bank_c, bank_s, bank_b = BUF[s]
            S, turn = norm_sems[s], nth(s, n, alone)
            cen, groups, eps = NORMS[s][n]
            src, _, _, _, ready = norm_io(s, n)
            if part == 0:
                if cen is not None:
                    pe.wait_ge(*ready)
                    pe.matmul(ps[:, bank_c, 0:N], small["cen_" + cen][:], src[:, :], start=True, stop=True)\
                        .then_inc(S["centered"], 1)
                return
            if part == 2:
                if groups == 1:
                    pe.wait_ge(S["rsqrt"], turn + 1)
                else:
                    pe.wait_ge(group_spread, 1)
                for c in range(4):
                    one = rs[:, c:c + 1].to_broadcast([C, D]) if groups == 1 else shared_a[0:C, c * D:(c + 1) * D]
                    mm = pe.matmul(ps[:, bank_b, chunk(c)], one, ident[0:C, 0:C], start=True, stop=True)
                mm.then_inc(S["spread"], 1)
                return
            pe.wait_ge(S["square"], turn + 1)
            if (s, n) == ("a", 0):
                sq = th[:, 0, :]
                if not alone:
                    pe.wait_ge(decayed, BATCH_PIECES)
            rhs = small["stat_all"][:, 0:1] if groups == 1 else small["stat_group"][:, :]
            for c in range(4):
                mm = pe.matmul(ps[0:C, bank_s, c * groups:(c + 1) * groups], sq[:, chunk(c)], rhs, start=True, stop=True)
            mm.then_inc(S["stat"], 1)

        def norm_act(act, alone, s, n, part):
            sq, xc, eps_t, rs, bank_c, bank_s, bank_b = BUF[s]
            S, turn = norm_sems[s], nth(s, n, alone)
            src, _, _, _, ready = norm_io(s, n)
            if part:
                return
            if NORMS[s][n][0] is None:
                act.wait_ge(*ready)
                if (s, n) == ("a", 0):
                    sq = th[:, 0, :]
                    if not alone:
                        act.wait_ge(rq_gate, 1)
                act.activation(sq[:, :], src[:, :], ACT.Square).then_inc(S["square"], 1)
            else:
                act.wait_ge(S["centered"], centered_before(s, n) + 1)
                act.activation(sq[:, :], ps[:, bank_c, 0:N], ACT.Square).then_inc(S["square"], 1)
                act.activation(xc[:, :], ps[:, bank_c, 0:N], ACT.Identity).then_inc(S["kept"], 1)

        def norm_dve(dve, alone, s, n, part):
            sq, xc, eps_t, rs, bank_c, bank_s, bank_b = BUF[s]
            S, turn = norm_sems[s], nth(s, n, alone)
            cen, groups, eps = NORMS[s][n]
            src, dst, weight, bias, _ = norm_io(s, n)
            if part == 0:
                return
            if part == 1:
                dve.wait_ge(S["stat"], turn + 1)
                dve.tensor_scalar(eps_t[:, 0:4 * groups], ps[0:C, bank_s, 0:4 * groups], eps, None, ALU.add)\
                    .then_inc(S["eps"], 1)
                return
            dve.wait_ge(S["spread"], turn + 1)
            if (s, n) == ("a", 0) and not alone:
                dve.wait_ge(a_done, 1)
            if cen is not None:
                dve.wait_ge(S["kept"], centered_before(s, n) + 1)
                src = xc
            out_sem = S["out"] if bias is not None else S["final"]
            if weight is None:
                dve.tensor_tensor(dst[:, :], src[:, :], ps[:, bank_b, 0:N], ALU.mult).then_inc(out_sem, 1)
            else:
                dve.scalar_tensor_tensor(out=dst[:, :], in0=src[:, :], scalar=weight, in1=ps[:, bank_b, 0:N],
                                         op0=ALU.mult, op1=ALU.mult).then_inc(out_sem, 1)
            if bias is not None:
                before = {("a", 6): 0, ("b", 1): 0, ("b", 2): 1}[s, n]
                dve.wait_ge(S["out"], before + 1)
                dve.tensor_scalar(dst[:, :], dst[:, :], bias, None, ALU.add).then_inc(S["final"], 1)

        def norm_pool(pool, alone, s, n, part):
            sq, xc, eps_t, rs, bank_c, bank_s, bank_b = BUF[s]
            S, turn = norm_sems[s], nth(s, n, alone)
            groups = NORMS[s][n][1]
            if part != 1:
                return
            pool.wait_ge(S["eps"], turn + 1)
            pool.tensor_tensor(rs[:, 0:4 * groups], eps_t[:, 0:4 * groups], neg_half[:, 0:4 * groups], ALU.pow)\
                .then_inc(S["rsqrt"], 1)
            if groups > 1:
                pool.wait_ge(S["rsqrt"], turn + 1)
                pool.tensor_copy(shared_a[0:C, 0:4 * D].rearrange("p (g d) -> p g d", d=D // groups),
                                 rs[:, 0:4 * groups].unsqueeze(2).to_broadcast([C, 4 * groups, D // groups]))\
                    .then_inc(group_spread, 1)

        final_a, final_b = norm_sems["a"]["final"], norm_sems["b"]["final"]

        def body(order, pair_a, pair_b, pair_e):
            with nc.Block(no_gpsimd_drain=True) as block:
                @block.sync
                def _(sp):
                    if pair_e is not None:
                        load_half(sp, pair_e, 0, img_loaded)
                        sp.wait_ge(embed_mm, 1)
                        load_half(sp, pair_e, 1, img_loaded)
                        sp.wait_ge(img_loaded, 384)
                    if pair_b is not None:
                        sp.wait_ge(y_kept, 1)
                        for k in range(2):
                            sp.dma_start(out[bass.ts(pair_b, 2), k * C:k * C + KROWS[k], :].rearrange("b t d -> t b d"),
                                         outs[:, :, :].rearrange("p (b k) d -> p b k d", k=2)[0:KROWS[k], :, k, :])\
                                .then_inc(out_stored, 16)
                        sp.wait_ge(out_stored, 32)

                @block.tensor
                def _(pe):
                    def embed(half):
                        pe.wait_ge(img_loaded, 192 * (half + 1))
                        if half:
                            pe.wait_ge(embed_x, 1)
                            if pair_a is not None:
                                pe.wait_ge(rv_kept, 2)
                        for px in range(PATCH // 2):
                            mm = pe.matmul(ps[:, 3, 0:PATCHES].rearrange("p (b i j) -> p b i j", b=2, i=HALF),
                                           small["wp"][:, px * D:(px + 1) * D], img[:, :, :, px::PATCH],
                                           start=(px == 0), stop=(px == PATCH // 2 - 1))
                        mm.then_inc(embed_mm, 1)

                    def qkv(i, part):
                        if part < 4:
                            if i:
                                pe.wait_ge(final_a, nth("a", 2, False) + 1)
                            for j in (2 * part, 2 * part + 1):
                                if j >= 4:
                                    pe.wait_ge(stacked, 8 * i + j - 3)
                                pe.matmul(ps[:, j % 4, 0:N], small[f"wqk{i}"][:, j * D:(j + 1) * D], ha[:, :],
                                          start=True, stop=True).then_inc(qk_mm, 1)
                            return
                        pe.wait_ge(stacked, 8 * i + 5)
                        for c in range(4):
                            mm = pe.matmul(ps[0:C, 0, c * D:(c + 1) * D], ha[:, chunk(c)], small[f"wv{i}"][:, :],
                                           start=True, stop=True)
                        mm.then_inc(v_mm, 1)

                    def stacks(bank, j, left, left_cols, right, right_cols, four):
                        for t in range(2):
                            r = slice(64 * j, 64 * j + ROWS)
                            mm = pe.matmul(ps[0:C, bank, t * TP:(t + 1) * TP], left[r, 2 * four + t, left_cols],
                                           right[r, 2 * four + t, right_cols], start=True, stop=True)
                        return mm

                    def maxima(i, part):
                        if part == 4:
                            pe.wait_ge(max_done, 8 * i + 8)
                            for four in range(2):
                                for c in range(4):
                                    mm = pe.transpose(ps[:, four, chunk(c)], mp[:, c, four, :], ident[0:C, 0:C])
                                mm.then_inc(max_t, 1)
                            return
                        if part == 0:
                            pe.wait_ge(stacked, 8 * i + 8)
                            pe.wait_ge(v_kept, 2 * i + 2)
                        for u in (2 * part, 2 * part + 1):
                            four, c = divmod(u, 4)
                            if u >= 2:
                                pe.wait_ge(max_done, 8 * i + u - 1)
                            for j in range(2):
                                mm = stacks(2 * (u % 2) + j, j, qst, chunk(c), kst, slice(c // 2 * TP, (c // 2 + 1) * TP), four)
                            mm.then_inc(sq_mm, 1)

                    def heads(i, u):
                        if u == 0:
                            pe.wait_ge(q_aug, 4 * i + 4)
                        for j in range(2):
                            if 1 <= u <= UNITS:
                                pe.wait_ge(exp_done, 2 * (8 * i + u) - 1 + j)
                            if u < UNITS:
                                four, b, kk = u // 4, u // 2 % 2, u % 2
                                stacks(j, j, kst, chunk(2 * b + kk), qst, slice(b * TP, (b + 1) * TP), four).then_inc(st_mm, 1)
                        if 1 <= u <= UNITS:
                            four, b, kk = (u - 1) // 4, (u - 1) // 2 % 2, (u - 1) % 2
                            rows = KROWS[kk]
                            for h in range(4):
                                at = ((2 * b + kk) * HEADS + 4 * four + h) * VW
                                mm = pe.matmul(ps[32 * h:32 * h + 32, 2 + four, b * TP:(b + 1) * TP],
                                               vp[0:rows, at:at + 32], pt[0:rows, (u - 1) % 2, h, :],
                                               start=(kk == 0), stop=(kk == 1), tile_position=(0, 32 * h))
                            if u % 4 == 0:
                                mm.then_inc(pv_mm, 1)
                        if u in (5, UNITS + 1):
                            four = u // UNITS
                            pe.wait_ge(o_kept, 2 * i + four + 1)
                            for c in range(4):
                                mm = pe.matmul(ps[0:C, 2 + four, 4 * c:4 * c + 4], oe[:, four, chunk(c)], small["sums"][:, :],
                                               start=True, stop=True)
                            mm.then_inc(sum_mm, 1)
                        if u in (6, UNITS + 2):
                            four = u // UNITS
                            pe.wait_ge(rec_spread, 2 * i + four + 1)
                            for c in range(4):
                                mm = pe.matmul(ps[:, 2 + four, chunk(c)], rec_wide[:, c, :, :].rearrange("p h r -> p (h r)"),
                                               ident[0:C, 0:C], start=True, stop=True)
                            mm.then_inc(rec_mm, 1)

                    def proj(i):
                        for four in range(2):
                            pe.wait_ge(on_done, 2 * i + four + 1)
                            mm = pe.matmul(ps[:, 0, 0:N], small[f"wo{i}"][:, four * D:(four + 1) * D], oe[:, four, :],
                                           start=(four == 0), stop=(four == 1))
                        mm.then_inc(proj_mm, 1)

                    def ff(i, t):
                        if t < 3:
                            a, m = FF_TILES[t]
                            if t == 0:
                                pe.wait_ge(final_a, 2 * i + 1)
                            if t == 2:
                                pe.wait_ge(ff_act, 3 * i + 1)
                            bank = 2 * (t % 2)
                            pe.matmul(ps[0:m, bank, 0:N], small[f"wg{i}"][:, a:a + m], ha[:, :], start=True, stop=True)
                            pe.matmul(ps[0:m, bank + 1, 0:N], small[f"wu{i}"][:, a:a + m], ha[:, :], start=True, stop=True)\
                                .then_inc(ff_mm, 1)
                            return
                        for t, (a, m) in enumerate(FF_TILES):
                            pe.wait_ge(ff_act, 3 * i + (2, 2, 3)[t])
                            mm = pe.matmul(ps[:, 2, 0:N], small[f"wd{i}"][0:m, t * D:(t + 1) * D], gu[0:m, t, :],
                                           start=(t == 0), stop=(t == 2))
                        mm.then_inc(down_mm, 1)

                    def ret_in(j):
                        if j < 2:
                            pe.wait_ge(final_a, 5)
                            for r in range(2):
                                if j:
                                    pe.wait_ge(rot_part, 1 + r)
                                pe.matmul(ps[:, r, 0:N], small["rqk"][:, (2 * j + r) * D:(2 * j + r + 1) * D], xra[:, :],
                                          start=True, stop=True).then_inc(rot_mm, 1)
                            return
                        if pair_e is not None:
                            pe.wait_ge(embed_x, 1)
                        for c in range(4):
                            mm = pe.matmul(ps[0:C, 3, c * D:(c + 1) * D], xra[:, chunk(c)], small["rv"][:, :],
                                           start=True, stop=True)
                        mm.then_inc(rv_mm, 1)

                    def ret(r):
                        if r == 0:
                            pe.wait_ge(final_a, 6)
                            pe.wait_ge(rq_done, 2)
                            pe.wait_ge(rv_kept, 2)
                            if pair_e is not None:
                                pe.wait_ge(embed_x, 2)
                        for k in (2 * r, 2 * r + 1):
                            if k < BATCH_PIECES:
                                b, m, kk = k // 8, k // 2 % 4, k % 2
                                if k >= 3:
                                    pe.wait_ge(decayed, k - 2)
                                rows = slice(32 * m, 32 * m + 32)
                                first, width = RQ[kk]
                                for h in range(2):
                                    mm = pe.matmul(ps[0:C, k % 3, h * TP:h * TP + width], t1[rows, chunk(2 * b + kk)],
                                                   qeo[rows, h, b * TP + first:(b + 1) * TP], start=True, stop=True)
                                mm.then_inc(rs_mm, 1)
                            k -= 2
                            if k >= 0:
                                b, m, kk = k // 8, k // 2 % 4, k % 2
                                first, width = RQ[kk]
                                pe.wait_ge(decayed, k + 1)
                                for h in range(2):
                                    mm = pe.matmul(ps[32 * m:32 * m + 32, 3, b * TP + first:(b + 1) * TP],
                                                   rv2[0:KROWS[kk], h, 2 * b + kk, 32 * m:32 * m + 32],
                                                   rt[0:KROWS[kk], k % 3, h, 0:width],
                                                   start=(kk == 0 and h == 0), stop=(kk == 1 and h == 1),
                                                   tile_position=(0, 32 * m))
                                if k == BATCH_PIECES - 1:
                                    mm.then_inc(ro_mm, 1)

                    def route(m, part):
                        if part == 1:
                            pe.wait_ge(w_done, m + 1)
                            for c in range(4):
                                mm = pe.transpose(ps[0:2 * EXPERTS, 7, chunk(c)], wtok[:, c, :, :].rearrange("p r e -> p (r e)"),
                                                  ident[0:C, 0:C])
                            mm.then_inc(w_turned, 1)
                            return
                        if part == 2:
                            weights(m, 0)
                            return
                        pe.wait_ge(final_b, (2, 5)[m])
                        for c in range(4):
                            mm = pe.matmul(ps[0:C, 6, c * EXPERTS:(c + 1) * EXPERTS], x2[:, chunk(c)],
                                           small[f"route{m}"][:, :], start=True, stop=True)
                        mm.then_inc(lg_mm, 1)

                    def weights(m, e):
                        pe.wait_ge(w_split, m + 1)
                        if e >= 2:
                            pe.wait_ge(exp_scaled, EXPERTS * m + e - 1)
                        mm = pe.matmul(ps[:, 6 + e % 2, 0:N], onehot[:, e:e + 1].to_broadcast([2 * EXPERTS, D]), wst[:, :],
                                       start=True, stop=True)
                        mm.then_inc(wb_mm, 1)

                    def hidden(name, tile, bank):
                        hi, lo = split[name]
                        s = slice(tile * D, (tile + 1) * D)
                        pe.matmul(ps[:, bank, 0:N], hi[:, s], x2h[:, :], start=True, stop=False)
                        pe.matmul(ps[:, bank, 0:N], lo[:, s], x2h[:, :], start=False, stop=False)
                        return pe.matmul(ps[:, bank, 0:N], hi[:, s], x2l[:, :], start=False, stop=True)

                    def up0(n):
                        if n >= 2:
                            pe.wait_ge(hid_act, n - 1)
                        hidden("W1", n, 4 + n % 2).then_inc(hid_mm, 1)

                    def down(m, n, tiles, base):
                        e, t = divmod(n, tiles)
                        if t == 0:
                            pe.wait_ge(wb_kept, EXPERTS * m + e + 1)
                        pe.wait_ge(*((hid_act, n + 1) if m == 0 else (hid_up, n + 1)))
                        pe.matmul(ps[:, 6 + e % 2, 0:N], small[("W2", "Wd")[m]][:, n * D:(n + 1) * D],
                                  g[:, (base + n) % 3, :], start=(t == 0), stop=(t == tiles - 1)).then_inc(exp_mm, 1)

                    def moe0(n):
                        e, t = divmod(n, H0T)
                        if n == -1:
                            pe.wait_ge(split_x, 1)
                            up0(0)
                            up0(1)
                            return
                        if n + 2 < H0T * EXPERTS:
                            up0(n + 2)
                        if n < H0T * EXPERTS:
                            if t == 2 and e + 1 < EXPERTS:
                                weights(0, e + 1)
                            down(0, n, H0T, 0)

                    def up1(n):
                        e, t = divmod(n, H1T)
                        if n >= 1:
                            pe.wait_ge(hid_act, H0T * EXPERTS + n)
                        hidden("Wgu", 4 * e + t, 4).then_inc(hid_mm, 1)
                        if n >= 1:
                            pe.wait_ge(hid_up, n)
                        hidden("Wgu", 4 * e + 2 + t, 5).then_inc(up_mm, 1)

                    def moe1(n):
                        e, t = divmod(n - 1, H1T)
                        if n == -1:
                            pe.wait_ge(split_x, 2)
                        if 0 <= n - 1 < H1T * EXPERTS:
                            if t == 1 and e + 1 < EXPERTS:
                                weights(1, e + 1)
                            down(1, n - 1, H1T, H0T * EXPERTS)
                        if n + 1 < H1T * EXPERTS:
                            up1(n + 1)

                    def att_in(part):
                        if part < 2:
                            pe.wait_ge(final_b, 4)
                            for j in (2 * part, 2 * part + 1):
                                if part:
                                    pe.wait_ge(ai_relu, j - 1)
                                pe.matmul(ps[:, 4 + j % 2, 0:N], small["we1k1"][:, j * D:(j + 1) * D], x2[:, :],
                                          start=True, stop=True).then_inc(ai_mm, 1)
                            return
                        pe.wait_ge(ai_relu, 4)
                        for j in range(2):
                            for t in range(2):
                                mm = pe.matmul(ps[:, 6 + j, 0:N], small["wk2"][:, (2 * t + j) * D:(2 * t + j + 1) * D],
                                               k1[:, t, :], start=(t == 0), stop=(t == 1))
                            mm.then_inc(akq_mm, 1)
                        for c in range(4):
                            for t in range(2):
                                mm = pe.matmul(ps[0:C, 4, c * D:(c + 1) * D], e1[:, t, chunk(c)],
                                               small["we2"][:, t * D:(t + 1) * D], start=(t == 0), stop=(t == 1))
                        mm.then_inc(av_mm, 1)

                    def att_max(part):
                        if part == 0:
                            pe.wait_ge(akq_round, 2)
                            for c in range(4):
                                mm = pe.matmul(ps[0:C, 6 + c // 2, (c % 2) * TP:(c % 2 + 1) * TP], qr2[:, chunk(c)],
                                               kr2[:, (c // 2) * TP:(c // 2 + 1) * TP], start=True, stop=True)
                            mm.then_inc(am_mm, 1)
                            return
                        pe.wait_ge(am_max, 1)
                        for c in range(4):
                            mm = pe.matmul(ps[64:96, 5, chunk(c)], mp2[:, c, :], ident[0:C, 0:C], start=True, stop=True,
                                           tile_position=(0, 64))
                        mm.then_inc(am_t, 1)

                    def att_pv(part):
                        if part == 0:
                            pe.wait_ge(am_aug, 1)
                            pe.wait_ge(av_kept, 1)
                            for b in range(2):
                                for kk in range(2):
                                    mm = pe.matmul(ps[0:C, 6 + b, kk * TP:(kk + 1) * TP], ks2[:, chunk(2 * b + kk)],
                                                   qs2[:, b * TP:(b + 1) * TP], start=True, stop=True)
                            mm.then_inc(as_mm, 1)
                            return
                        pe.wait_ge(as_exp, 1)
                        for b in range(2):
                            for qc in range(2):
                                for kk in range(2):
                                    rows = KROWS[kk]
                                    mm = pe.matmul(ps[0:C, 4 + b, qc * 130:(qc + 1) * 130], ptb[0:rows, 2 * b + kk, chunk(qc)],
                                                   vt[0:rows, 2 * b + kk, :], start=(kk == 0), stop=(kk == 1))
                        mm.then_inc(ao_mm, 1)

                    def att_out():
                        pe.wait_ge(ao_norm, 1)
                        for c in range(4):
                            mm = pe.transpose(ps[:, 6, chunk(c)], outs[:, c, :], ident[0:C, 0:C])
                        mm.then_inc(at_mm, 1)

                    def store():
                        pe.wait_ge(acc_done, 2 * EXPERTS)
                        for c in range(4):
                            mm = pe.transpose(ps[0:C, 4, c * D:(c + 1) * D], hb[:, chunk(c)], ident[:, :])
                        mm.then_inc(y_mm, 1)

                    walk(order, {"norm": lambda *a: norm_pe(pe, pair_a is None, *a), "embed": embed, "qkv": qkv, "maxima": maxima,
                                 "heads": heads, "proj": proj, "ff": ff, "ret_in": ret_in, "ret": ret,
                                 "route": route, "moe0": moe0, "moe1": moe1, "att_in": att_in, "att_max": att_max,
                                 "att_pv": att_pv, "att_out": att_out, "store": store})

                @block.scalar
                def _(act):
                    def keep(dst, src, done, bias=0.0, func=ACT.Identity, scale=1.0):
                        act.activation(dst, src, func, bias=bias, scale=scale).then_inc(done, 1)

                    def qkv(i, part):
                        if part < 4:
                            for j in (2 * part, 2 * part + 1):
                                act.wait_ge(qk_mm, 8 * i + j + 1)
                                if j >= 2:
                                    act.wait_ge(stacked, 8 * i + j - 1)
                                keep(high[:, j % 2, :], ps[:, j % 4, 0:N], qk_high,
                                     bias=0.0 if j < 4 else col("ones_row", j % 2))
                            return
                        act.wait_ge(v_mm, i + 1)
                        v = ps[0:C, 0, :].rearrange("p (c h d) -> p c h d", c=4, h=HEADS)
                        for half in range(2):
                            keep(vph[:, 2 * half:2 * half + 2, :, 0:HD], v[:, 2 * half:2 * half + 2], v_kept)

                    def heads(i, u):
                        if u < UNITS:
                            for j in range(2):
                                act.wait_ge(st_mm, 2 * (8 * i + u) + 1 + j)
                                keep(pt[:, u % 2, j::2, :], ps[0:C, j, 0:2 * TP].rearrange("p (t n) -> p t n", t=2), exp_done,
                                     func=ACT.Exp, scale=HD ** -0.5)
                        if u in (4, UNITS):
                            four = u // 4 - 1
                            act.wait_ge(pv_mm, 2 * i + four + 1)
                            keep(oe[:, four, :], ps[:, 2 + four, 0:N], o_kept)

                    def ff(i, t):
                        if t < 3:
                            m = FF_TILES[t][1]
                            act.wait_ge(ff_mm, 3 * i + t + 1)
                            if t >= 2:
                                act.wait_ge(ff_gate, 3 * i + t - 1)
                            keep(th[0:m, t % 2, :], ps[0:m, 2 * (t % 2), 0:N], ff_tanh, func=ACT.Tanh, scale=0.5)

                    def ret_in(part):
                        if part == 2:
                            act.wait_ge(rv_mm, 1)
                            for h in range(2):
                                v = (t.rearrange("p (m h d) -> p m h d", h=2, d=HD)[:, :, h, :]
                                     for t in (rv2[:, h, :, :].rearrange("p c d -> p (c d)"), ps[0:C, 3, :]))
                                keep(*v, rv_kept)

                    def ret_qk():
                        act.wait_ge(rot_sum, 1)
                        keep(th[:, 0, :], t2[:, :], rq_tanh, func=ACT.Tanh, scale=0.5)

                    def take():
                        keep(hb[:, :], hout[:, :], taken)

                    def splitx(m):
                        act.wait_ge(final_b, (2, 5)[m])
                        keep(x2h[:, :], x2[:, :], high_x)

                    def route(m, part):
                        if part == 0:
                            act.wait_ge(gap_done, m + 1)
                            keep(dth[:, :], dl[:, :], gap_tanh, func=ACT.Tanh, scale=0.5)
                        elif part == 1:
                            act.wait_ge(w_turned, m + 1)
                            keep(wst_high, ps[0:2 * EXPERTS, 7, 0:N], w_high)
                        else:
                            weights(m, 0)

                    def weights(m, e):
                        act.wait_ge(wb_mm, EXPERTS * m + e + 1)
                        if e >= 2:
                            act.wait_ge(exp_scaled, EXPERTS * m + e - 1)
                        keep(wb[:, e % 2, :], ps[:, 6 + e % 2, 0:N], wb_kept)

                    def moe0(n):
                        e, t = divmod(n, H0T)
                        n += 1
                        if n < H0T * EXPERTS:
                            act.wait_ge(hid_mm, n + 1)
                            if n >= 3:
                                act.wait_ge(exp_mm, n - 2)
                            keep(g[:, n % 3, :], ps[:, 4 + n % 2, 0:N], hid_act, func=ACT.Gelu_apprx_tanh,
                                 bias=small["b1"][:, n:n + 1])
                        if t == 2 and e + 1 < EXPERTS:
                            weights(0, e + 1)

                    def moe1(n):
                        e, t = divmod(n - 1, H1T)
                        if n >= 1 and t == 1 and e + 1 < EXPERTS:
                            weights(1, e + 1)
                        n += 1
                        if n < H1T * EXPERTS:
                            act.wait_ge(hid_mm, H0T * EXPERTS + n + 1)
                            if n >= 2:
                                act.wait_ge(hid_up, n - 1)
                            keep(gs[:, n % 2, :], ps[:, 4, 0:N], hid_act, func=ACT.Gelu_apprx_sigmoid,
                                 bias=small["bg"][:, n:n + 1])

                    def att_in(part):
                        if part < 2:
                            for j in (2 * part, 2 * part + 1):
                                act.wait_ge(ai_mm, j + 1)
                                keep((e1 if j < 2 else k1)[:, j % 2, :], ps[:, 4 + j % 2, 0:N], ai_relu, func=ACT.Relu,
                                     bias=col("be1k1", j))
                            return
                        for j in range(2):
                            act.wait_ge(akq_mm, j + 1)
                            keep((ks2, qs2)[j][:, :], ps[:, 6 + j, 0:N], akq_kept, bias=col("bkq", j))
                        act.wait_ge(av_mm, 1)
                        keep(vt[:, :, 0:D], ps[0:C, 4, :].rearrange("p (c d) -> p c d", c=4), av_kept)

                    def att_pv(part):
                        if part == 0:
                            act.wait_ge(as_mm, 1)
                            keep(ptb[:, :, :].rearrange("p (b k) t -> p b k t", k=2), heads_of(6), as_exp, func=ACT.Exp)

                    def store():
                        act.wait_ge(y_mm, 1)
                        keep(outs[:, :, :].rearrange("p c d -> p (c d)"), ps[0:C, 4, :], y_kept)

                    walk(order, {"norm": lambda *a: norm_act(act, pair_a is None, *a), "qkv": qkv, "heads": heads, "ff": ff,
                                 "ret_in": ret_in, "ret_qk": ret_qk, "take": take, "split": splitx,
                                 "route": route, "moe0": moe0, "moe1": moe1, "att_in": att_in, "att_pv": att_pv,
                                 "store": store})

                @block.vector
                def _(dve):
                    def embed(half):
                        both = xa[:, :].rearrange("p (b t) -> p b t", b=2)
                        pos = small["pos"]
                        if pair_a is not None:
                            dve.wait_ge(final_a, 4)
                        if half == 0:
                            dve.tensor_copy(both[:, :, 0:TP:T], pos[:, 0:TP:T].unsqueeze(1).to_broadcast([D, 2, 2]))
                        dve.wait_ge(embed_mm, half + 1)
                        n = HALF * SIDE
                        dve.tensor_tensor(both[:, :, 1 + half * n:1 + (half + 1) * n],
                                          ps[:, 3, 0:2 * n].rearrange("p (b t) -> p b t", b=2),
                                          pos[:, 1 + half * n:1 + (half + 1) * n].unsqueeze(1).to_broadcast([D, 2, n]),
                                          ALU.add).then_inc(embed_x, 1)

                    def qkv(i, part):
                        if part == 4:
                            return
                        for j in (2 * part, 2 * part + 1):
                            dve.wait_ge(qk_high, 8 * i + j + 1)
                            dve.scalar_tensor_tensor(out=(qst, kst)[j // 4][:, j % 4, :], in0=high[:, j % 2, :].bitcast(F32),
                                                     scalar=col("parts", j // 4), in1=ps[:, j % 4, 0:N],
                                                     op0=ALU.mult, op1=ALU.add).then_inc(stacked, 1)

                    def maxima(i, part):
                        if part == 4:
                            for t in range(TILES):
                                dve.wait_ge(max_t, 2 * i + t // 2 + 1)
                                dve.tensor_tensor(qst[:, t, :], qst[:, t, :].bitcast(F32), ps[:, t // 2, 0:N], ALU.add)\
                                    .then_inc(q_aug, 1)
                            return
                        for u in (2 * part, 2 * part + 1):
                            four, c = divmod(u, 4)
                            dve.wait_ge(sq_mm, 8 * i + u + 1)
                            m = mp[:, c, four, :].rearrange("p (j r) -> p j r", j=2)[:, :, STACK:STACK + 2]
                            dve.tensor_reduce(m, heads_of(2 * (u % 2))[:, :, :, 0:T], AX.X, ALU.max, negate=True)\
                                .then_inc(max_done, 1)

                    def heads(i, u):
                        if u in (5, UNITS + 1):
                            n = 2 * i + u // UNITS + 1
                            dve.wait_ge(sum_mm, n)
                            dve.reciprocal(rec[:, :, :], ps[0:C, 2 + u // UNITS, 0:16].rearrange("p (c h) -> p c h", c=4))\
                                .then_inc(rec_done, 1)
                            dve.wait_ge(rec_done, n)
                            dve.tensor_copy(rec_wide[:, :, :, :], rec[:, :, :].unsqueeze(3).to_broadcast([C, 4, 4, 32]))\
                                .then_inc(rec_spread, 1)
                        if u in (6, UNITS + 2):
                            four = u // UNITS
                            dve.wait_ge(rec_mm, 2 * i + four + 1)
                            dve.tensor_tensor(oe[:, four, :], oe[:, four, :], ps[:, 2 + four, 0:N], ALU.mult).then_inc(on_done, 1)

                    def proj(i):
                        dve.wait_ge(proj_mm, i + 1)
                        dve.tensor_tensor(xa[:, :], xa[:, :], ps[:, 0, 0:N], ALU.add).then_inc(x_proj, 1)

                    def ff(i, t):
                        if t < 3:
                            m = FF_TILES[t][1]
                            n = 3 * i + t + 1
                            dve.wait_ge(ff_tanh, n)
                            dve.scalar_tensor_tensor(out=gu[0:m, t, :], in0=th[0:m, t % 2, :], scalar=1.0,
                                                     in1=ps[0:m, 2 * (t % 2), 0:N], op0=ALU.add, op1=ALU.mult)\
                                .then_inc(ff_gate, 1)
                            dve.wait_ge(ff_gate, n)
                            dve.tensor_tensor(gu[0:m, t, :], gu[0:m, t, :], ps[0:m, 2 * (t % 2) + 1, 0:N], ALU.mult)\
                                .then_inc(ff_act, 1)
                            return
                        dve.wait_ge(down_mm, i + 1)
                        dve.scalar_tensor_tensor(out=xa[:, :], in0=ps[:, 2, 0:N], scalar=0.5, in1=xa[:, :],
                                                 op0=ALU.mult, op1=ALU.add).then_inc(x_ff, 1)

                    def table(name):
                        return small[name][:, :].unsqueeze(1).to_broadcast([D, 2, TP])

                    def pair3(t):
                        return t.rearrange("p (b t) -> p b t", b=2)

                    def ret_in(j):
                        if j == 2:
                            return
                        dst = (t2, t1)[j]
                        dve.wait_ge(rot_mm, 2 * j + 1)
                        dve.tensor_tensor(pair3(dst[:, :]), pair3(ps[:, 0, 0:N]), table("cos"), ALU.mult)\
                            .then_inc(rot_part, 1)
                        dve.wait_ge(rot_mm, 2 * j + 2)
                        if j:
                            dve.wait_ge(rot_sum, 1)
                        dve.tensor_tensor(pair3(sqa[:, :]), pair3(ps[:, 1, 0:N]), table("sin"), ALU.mult)\
                            .then_inc(rot_part, 1)
                        dve.wait_ge(rot_part, 2 * j + 2)
                        dve.tensor_tensor(dst[:, :], dst[:, :], sqa[:, :], ALU.add).then_inc(rot_sum, 1)

                    def ret_qk():
                        dve.wait_ge(rq_tanh, 1)
                        dve.scalar_tensor_tensor(out=t2[:, :], in0=th[:, 0, :], scalar=1.0, in1=t2[:, :],
                                                 op0=ALU.add, op1=ALU.mult).then_inc(rq_gate, 1)
                        dve.wait_ge(rq_gate, 1)
                        for e in range(2):
                            dve.tensor_scalar(qeo[:, e, :], t2[:, :], col("evenodd", e), None, ALU.mult).then_inc(rq_done, 1)

                    def ret(r):
                        decay = small["decay"]
                        for k in (2 * r, 2 * r + 1):
                            if k < BATCH_PIECES:
                                width = RQ[k % 2][1]
                                start = (1, 0)[k % 2]
                                dve.wait_ge(rs_mm, k + 1)
                                dve.tensor_tensor(rt[:, k % 3, :, 0:width],
                                                  ps[0:C, k % 3, 0:2 * TP].rearrange("p (h t) -> p h t", h=2)[:, :, 0:width],
                                                  decay[:, start:start + width].unsqueeze(1).to_broadcast([C, 2, width]),
                                                  ALU.mult).then_inc(decayed, 1)

                    def ret_out():
                        dve.wait_ge(ro_mm, 1)
                        dve.tensor_tensor(xra[:, :], xra[:, :], ps[:, 3, 0:N], ALU.add).then_inc(ret_sum, 1)
                        dve.wait_ge(ret_sum, 1)
                        if pair_b is not None:
                            dve.wait_ge(taken, 1)
                        dve.scalar_tensor_tensor(out=hout[:, :], in0=xra[:, :], scalar=0.0, in1=hout[:, :],
                                                 op0=ALU.max, op1=ALU.add).then_inc(a_done, 1)

                    def splitx(m):
                        dve.wait_ge(high_x, m + 1)
                        dve.tensor_tensor(x2l[:, :], x2[:, :], x2h[:, :].bitcast(F32), ALU.subtract).then_inc(split_x, 1)

                    def route(m, part):
                        if part == 1:
                            dve.wait_ge(w_high, m + 1)
                            dve.scalar_tensor_tensor(out=wst[:, :], in0=wst_high.bitcast(F32),
                                                     scalar=col("low_half")[0:2 * EXPERTS], in1=ps[0:2 * EXPERTS, 7, 0:N],
                                                     op0=ALU.mult, op1=ALU.add).then_inc(w_split, 1)
                        if part:
                            return
                        dve.wait_ge(lg_mm, m + 1)
                        dve.tensor_tensor(lg[:, :, :], ps[0:C, 6, 0:4 * EXPERTS].rearrange("p (c e) -> p c e", c=4),
                                          small["rb"][:, m * EXPERTS:(m + 1) * EXPERTS].unsqueeze(1).to_broadcast([C, 4, EXPERTS]),
                                          ALU.add).then_inc(lg_kept, 1)
                        dve.wait_ge(lg_kept, m + 1)
                        for c in range(4):
                            dve.max(m8[:, c, :], lg[:, c, :]).then_inc(top_done, 1)
                        dve.wait_ge(top_done, 4 * m + 4)
                        dve.tensor_tensor(dl[:, :], m8[:, :, 1], m8[:, :, 0], ALU.subtract).then_inc(gap_done, 1)
                        for c in range(4):
                            dve.max_index(i8[:, c, :], m8[:, c, :], lg[:, c, :]).then_inc(idx_done, 1)
                        dve.wait_ge(idx_done, 4 * m + 4)
                        dve.tensor_copy(i8f[:, :, :], i8[:, :, 0:2]).then_inc(idx_f, 1)
                        dve.wait_ge(gap_tanh, m + 1)
                        dve.tensor_scalar(cw[:, 0, :], dth[:, :], -0.5, 0.5, ALU.mult, ALU.add)
                        dve.tensor_scalar(cw[:, 1, :], dth[:, :], 0.5, 0.5, ALU.mult, ALU.add).then_inc(conf_done, 1)
                        dve.wait_ge(conf_done, m + 1)
                        dve.wait_ge(idx_f, m + 1)
                        both = [C, 4, 2, EXPERTS]
                        dve.tensor_tensor(picks[:, :, :, :], small["iota"][:, :].unsqueeze(1).unsqueeze(1).to_broadcast(both),
                                          i8f[:, :, :].unsqueeze(3).to_broadcast(both), ALU.is_equal).then_inc(pick_done, 1)
                        dve.wait_ge(pick_done, 2 * m + 1)
                        dve.tensor_tensor(picks[:, :, :, :], picks[:, :, :, :],
                                          cw[:, :, :].rearrange("p k c -> p c k").unsqueeze(3).to_broadcast(both),
                                          ALU.mult).then_inc(pick_done, 1)
                        dve.wait_ge(pick_done, 2 * m + 2)
                        dve.tensor_tensor(wtok[:, :, :, :], picks[:, :, 0, :].unsqueeze(2).to_broadcast([C, 4, 2, EXPERTS]),
                                          picks[:, :, 1, :].unsqueeze(2).to_broadcast([C, 4, 2, EXPERTS]), ALU.add).then_inc(w_done, 1)

                    def scaled(m, e, tiles, base):
                        dve.wait_ge(exp_mm, base + tiles * (e + 1))
                        n = EXPERTS * m + e
                        if n >= 2:
                            dve.wait_ge(acc_done, n - 1)
                        dve.scalar_tensor_tensor(out=to[:, e % 2, :], in0=ps[:, 6 + e % 2, 0:N],
                                                 scalar=small["b2bd"][:, n:n + 1], in1=wb[:, e % 2, :],
                                                 op0=ALU.add, op1=ALU.mult).then_inc(exp_scaled, 1)

                    def moe0(n):
                        e, t = divmod(n, H0T)
                        if n >= 1 and t == 0:
                            scaled(0, e - 1, H0T, 0)

                    def moe1(n):
                        base = H0T * EXPERTS
                        e, t = divmod(n, H1T)
                        if n >= 2 and t == 1:
                            scaled(1, e - 1, H1T, base)
                        n += 1
                        if n < H1T * EXPERTS:
                            dve.wait_ge(hid_act, base + n + 1)
                            dve.wait_ge(up_mm, n + 1)
                            k = (base + n) % 3
                            dve.wait_ge(exp_mm, base + n - 2)
                            dve.scalar_tensor_tensor(out=g[:, k, :], in0=ps[:, 5, 0:N], scalar=bu1[:, n:n + 1],
                                                     in1=gs[:, n % 2, :], op0=ALU.add, op1=ALU.mult).then_inc(hid_up, 1)

                    def sum0():
                        last_add(0, x1)

                    def last_add(m, dst):
                        dve.wait_ge(exp_scaled, EXPERTS * (m + 1))
                        dve.wait_ge(acc_done, EXPERTS * (m + 1) - 1)
                        dve.tensor_tensor(dst[:, :], acc[:, :], to[:, (EXPERTS - 1) % 2, :], ALU.add).then_inc(acc_done, 1)

                    def add0():
                        dve.wait_ge(final_b, 3)
                        dve.tensor_tensor(hb[:, :], hb[:, :], x1[:, :], ALU.add).then_inc(hb_add, 1)

                    def att_in(part):
                        if part == 2:
                            for j in range(2):
                                dve.wait_ge(akq_kept, j + 1)
                                dve.tensor_copy((kr2, qr2)[j][:, :], (ks2, qs2)[j][:, :]).then_inc(akq_round, 1)

                    def att_max(part):
                        if part == 0:
                            dve.wait_ge(am_mm, 1)
                            dve.tensor_reduce(mp2[:, :, 0].rearrange("p (b k) -> p b k", k=2), heads_of(6)[:, :, :, 0:T],
                                              AX.X, ALU.max, negate=True).then_inc(am_max, 1)
                            return
                        dve.wait_ge(am_t, 1)
                        dve.tensor_tensor(qs2[64:96, :], qs2[64:96, :], ps[64:96, 5, 0:N], ALU.add).then_inc(am_aug, 1)

                    def att_pv(part):
                        if part == 0:
                            return
                        dve.wait_ge(ao_mm, 1)
                        o = ps[0:C, 4:6, 0:260].rearrange("p b (q d) -> p b q d", q=2)
                        dve.reciprocal(recb[:, :].rearrange("p (b q) -> p b q", b=2), o[:, :, :, D]).then_inc(ao_rec, 1)
                        dve.wait_ge(ao_rec, 1)
                        dve.tensor_tensor(outs[:, :, :].rearrange("p (b q) d -> p b q d", b=2), o[:, :, :, 0:D],
                                          recb[:, :].rearrange("p (b q) -> p b q", b=2).unsqueeze(3).to_broadcast([C, 2, 2, D]),
                                          ALU.mult).then_inc(ao_norm, 1)

                    def att_out():
                        dve.wait_ge(at_mm, 1)
                        dve.scalar_tensor_tensor(out=hb[:, :], in0=ps[:, 6, 0:N], scalar=col("be2"), in1=hb[:, :],
                                                 op0=ALU.add, op1=ALU.add).then_inc(hb_add, 1)

                    def store():
                        last_add(1, hb)

                    walk(order, {"norm": lambda *a: norm_dve(dve, pair_a is None, *a), "embed": embed, "qkv": qkv, "maxima": maxima,
                                 "heads": heads, "proj": proj, "ff": ff, "ret_in": ret_in, "ret_qk": ret_qk, "ret": ret,
                                 "ret_out": ret_out, "split": splitx, "route": route, "moe0": moe0, "moe1": moe1,
                                 "sum0": sum0, "add0": add0, "att_in": att_in, "att_max": att_max, "att_pv": att_pv,
                                 "att_out": att_out, "store": store})

                @block.gpsimd
                def _(pool):
                    def add(m, e):
                        if e == EXPERTS - 1:
                            return
                        n = EXPERTS * m + e
                        pool.wait_ge(exp_scaled, n + 1)
                        if e == 0:
                            pool.tensor_tensor(acc[:, :], (x1, hb)[m][:, :], to[:, 0, :], ALU.add).then_inc(acc_done, 1)
                        else:
                            pool.wait_ge(acc_done, n)
                            pool.tensor_tensor(acc[:, :], acc[:, :], to[:, e % 2, :], ALU.add).then_inc(acc_done, 1)

                    def moe0(n):
                        if n >= 1 and n % H0T == 0:
                            add(0, n // H0T - 1)

                    def moe1(n):
                        if n >= 2 and n % H1T == 1:
                            add(1, n // H1T - 1)

                    walk(order, {"norm": lambda *a: norm_pool(pool, pair_a is None, *a), "moe0": moe0, "moe1": moe1})

            nc.sync.sem_clear(range(sems[0].num, sems[-1].num + 1))
            nc.all_engine_barrier()

        assert [s.num for s in sems] == list(range(sems[0].num, sems[0].num + len(sems)))
        body([("embed", 0), ("embed", 1)] + NEXT, None, None, 0)
        body(only(0), 0, None, 1)
        with nc.Fori(0, PAIRS - 2) as i:
            body(merged(), i + 1, i, i + 2)
        body(merged(last=True), PAIRS - 1, PAIRS - 2, None)
        body(only(1), None, PAIRS - 1, None)


def walk(order, steps):
    for name, *arguments in order:
        if name in steps:
            steps[name](*arguments)


SPLIT = ("W1", "Wgu")
COLUMNS = (("conv_b", 1), ("cls", 1), ("ln1", 2), ("ln2", 2), ("ln_f", 1), ("gn_w", 1), ("gn_b", 1), ("ln_g", 1),
           ("ln_b", 1), ("out_g", 1), ("out_b", 1), ("be2", 1), ("be1k1", 4), ("bkq", 2), ("ones_row", 2), ("low_half", 1), ("parts", 2), ("evenodd", 2))
COL = {name: sum(n for _, n in COLUMNS[:k]) for k, (name, _) in enumerate(COLUMNS)}
COL_TOTAL = sum(n for _, n in COLUMNS)


def constants():
    c = {"ident": np.eye(D, dtype=np.float32)}
    c["cen_all"] = (np.eye(D) - 1.0 / D).astype(np.float32)
    same = np.arange(D)[:, None] // HD == np.arange(D)[None, :] // HD
    c["cen_group"] = (np.eye(D) - same / HD).astype(np.float32)
    c["stat_all"] = np.full((D, 2), 1.0 / D, np.float32)
    c["stat_group"] = ((np.arange(D)[:, None] // HD == np.arange(HEADS)[None, :]) / HD).astype(np.float32)
    s, d = np.arange(T, dtype=np.float64), np.arange(D)
    scale = ((d // 2 * 2 + 0.4 * D) / (1.4 * D))[:, None] ** (s / 512.0)[None, :]
    angle = (1.0 / 10000.0 ** ((d // 2) / (D // 2)))[:, None] * s[None, :]
    sign = np.where(d % 2 == 0, -1.0, 1.0)[:, None]
    c["cos"], c["sin"] = np.zeros((D, TP), np.float32), np.zeros((D, TP), np.float32)
    c["cos"][:, :T] = np.cos(angle) * scale
    c["sin"][:, :T] = np.sin(angle) * scale * sign
    gap = np.arange(TP + 1)[None, :] - 1 - np.arange(C)[:, None]
    c["decay"] = np.where(gap >= 0, 0.5 * 0.9 ** np.maximum(gap, 0), 0.0).astype(np.float32)
    row = np.arange(D)
    c["sums"] = (row[:, None] == 32 * np.arange(4)[None, :] + HD).astype(np.float32)
    c["two_eyes"] = np.tile(np.eye(EXPERTS, dtype=np.float32), (2, 1))
    c["iota"] = np.tile(np.arange(EXPERTS, dtype=np.float32), (C, 1))
    return c


def layout(a):
    f = {k: np.asarray(v) for k, v in a.items()}
    out = constants()

    def rows(m):
        return m.reshape(-1, D, m.shape[-1]).transpose(1, 0, 2).reshape(D, -1)

    wp = f["L0_tok_conv_w"].transpose(1, 2, 3, 0).reshape(3 * PATCH, PATCH * D)
    out["wp"] = np.zeros((128, PATCH // 2 * D), np.float32)
    out["wp"][0:48], out["wp"][64:112] = wp[:, :PATCH // 2 * D], wp[:, PATCH // 2 * D:]
    out["pos"] = np.zeros((D, TP), np.float32)
    out["pos"][:, :T] = f["L0_tok_pos_emb"][0].T
    for i in range(2):
        qkv = f[f"L0_tok_qkv_{i}"].T
        padded = np.zeros((D, 2 * HEADS, 64), np.float32)
        for part in range(3):
            padded[:, :, part * HD:(part + 1) * HD] = qkv[:, :2 * D].reshape(D, 2 * HEADS, HD)
        out[f"wqk{i}"] = padded.reshape(D, 8 * D)
        out[f"wv{i}"] = qkv[:, 2 * D:]
        wo = np.zeros((2, 4, 32, D), np.float32)
        wo[:, :, :HD] = f[f"L0_tok_wo_{i}"].T.reshape(2, 4, HD, D)
        out[f"wo{i}"] = rows(wo.reshape(2 * D, D))
        out[f"wg{i}"], out[f"wu{i}"] = f[f"L0_tok_gate_{i}"].T, f[f"L0_tok_up_{i}"].T
        down = np.zeros((3 * D, D), np.float32)
        down[:FF] = f[f"L0_tok_down_{i}"].T
        out[f"wd{i}"] = rows(down)
    swap = np.arange(D) ^ 1
    out["rqk"] = np.concatenate([m for n in ("Wq", "Wk") for m in (f["L0_attn_" + n], f["L0_attn_" + n][:, swap])], 1)
    out["rv"] = f["L0_attn_Wv"]
    out["route0"], out["route1"] = f["L0_ffn_Wg"], f["L1_ffn_router_w"]
    rb = np.zeros((C, 2 * EXPERTS), np.float32)
    rb[:, EXPERTS:] = f["L1_ffn_router_b"][None, :]
    out["rb"] = rb
    out["W1"] = f["L0_ffn_W1"].transpose(1, 0, 2).reshape(D, -1)
    out["W2"] = rows(f["L0_ffn_W2"].reshape(-1, D))
    out["Wgu"] = f["L1_ffn_gate_up_proj"].transpose(1, 0, 2).reshape(D, -1)
    out["Wd"] = rows(f["L1_ffn_down_proj"].reshape(-1, D))
    out["b1"] = f["L0_ffn_b1"].reshape(-1, D).T
    bgu = f["L1_ffn_gate_up_proj_bias"].reshape(EXPERTS, 2, H1T, D)
    out["bg"], out["bu"] = bgu[:, 0].reshape(-1, D).T, bgu[:, 1].reshape(-1, D).T
    out["b2bd"] = np.concatenate([f["L0_ffn_b2"].T, f["L1_ffn_down_proj_bias"].T], 1)
    out["we1k1"] = np.concatenate([f["L1_attn_We1"], f["L1_attn_Wk1"]], 1)
    out["we2"] = rows(f["L1_attn_We2"])
    wk2 = np.zeros((2 * D, 2, D), np.float32)
    wk2[:, 0, :64], wk2[:, 1, :64] = f["L1_attn_Wk2"][:, :64], f["L1_attn_Wk2"][:, 64:]
    out["wk2"] = rows(wk2.reshape(2 * D, 2 * D))
    cols = np.zeros((D, COL_TOTAL), np.float32)

    def put(name, *vectors):
        for k, v in enumerate(vectors):
            cols[:, COL[name] + k] = v

    put("conv_b", f["L0_tok_conv_b"])
    put("cls", f["L0_tok_cls_token"].reshape(D))
    put("ln1", f["L0_tok_ln1_0"], f["L0_tok_ln1_1"])
    put("ln2", f["L0_tok_ln2_0"], f["L0_tok_ln2_1"])
    put("ln_f", f["L0_tok_ln_f"])
    put("gn_w", f["L0_attn_gn_weight"])
    put("gn_b", f["L0_attn_gn_bias"])
    put("ln_g", f["L0_ffn_ln_g"])
    put("ln_b", f["L0_ffn_ln_b"])
    put("out_g", f["L0_ffn_out_g"])
    put("out_b", f["L0_ffn_out_b"])
    put("low_half", -1.0 * (np.arange(D) // EXPERTS == 1))
    put("be2", f["L1_attn_be2"])
    put("be1k1", *f["L1_attn_be1"].reshape(2, D), *f["L1_attn_bk1"].reshape(2, D))
    bk, bq = np.zeros(D, np.float32), np.zeros(D, np.float32)
    bk[:64], bq[:64] = f["L1_attn_bk2"][:64], f["L1_attn_bk2"][64:]
    bk[64] = 1.0
    put("bkq", bk, bq)
    row = np.arange(D) % 64
    put("ones_row", *(row == STACK + t for t in range(2)))
    put("parts", -1.0 * (row // HD == 1), -1.0 * (row // HD == 2) + 1.0 * (row // 2 * 2 == STACK))
    even = (np.arange(D) // HD % 2 == 0).astype(np.float32)
    put("evenodd", even, 1.0 - even)
    out["cols"] = cols
    return {k: np.ascontiguousarray(v) for k, v in out.items()}


def kernel(**inputs):
    import concourse.bacc as bacc
    from concourse.bass_utils import run_bass_kernel_spmd
    arrays = {"x": np.ascontiguousarray(inputs.pop("x")), **layout(inputs)}
    nc = bacc.Bacc("TRN2", target_bir_lowering=False, num_devices=1)
    aps = {k: nc.dram_tensor(k + "_dram", v.shape, F32, kind="ExternalInput").ap() for k, v in arrays.items()}
    out = nc.dram_tensor("out_dram", (BATCH, T, D), F32, kind="ExternalOutput").ap()
    tower(nc, aps.pop("x"), aps, out)
    r = run_bass_kernel_spmd(nc, [{k + "_dram": v for k, v in arrays.items()}], core_ids=[0])
    return r.results[0]["out_dram"]
```
